# Optimizing a Trainium2 kernel written in Bass

```python
import numpy as np
import jax
import jax.numpy as jnp

def _softmax(x, axis=-1):
    return jax.nn.softmax(x, axis=axis)

def _gelu(x):
    return jax.nn.gelu(x, approximate=True)

def _silu(x):
    return jax.nn.silu(x)

def _sigmoid(x):
    return jax.nn.sigmoid(x)

def _layernorm(x, axis=-1, eps=1e-05):
    m = jnp.mean(x, axis=axis, keepdims=True)
    v = jnp.var(x, axis=axis, keepdims=True)
    return (x - m) / jnp.sqrt(v + eps)

def _scatter_add(tgt, idx, src, axis=0):
    return tgt.at[idx].add(src)

def _segment_sum(src, seg, n):
    return jax.ops.segment_sum(src, seg, n)
kernel_name = 'mk_adj_ffn_d4_adj_r2_27be6b'

def setup_inputs(seed: int=0):
    np.random.seed(seed)
    _w = jnp.asarray

    def _rec_inputs():
        import jax
        import jax.numpy as jnp
        _gk = jax.random.key(seed)
        x = -0.000929 + 1 * jax.random.normal(jax.random.fold_in(_gk, 1), (2048, 128), jnp.float32)
        _w = (1.0 + jnp.arange(2048, dtype=jnp.float32)) ** (-0.5)
        _w = _w / _w.mean()
        _pij = jnp.clip(0.00195312 * _w[:, None] * _w[None, :], 0.0, 1.0)
        _a = jax.random.uniform(jax.random.fold_in(_gk, 2), (2048, 2048)) < _pij
        _a = jnp.logical_or(_a, jnp.eye(2048, dtype=bool))
        _af = _a.astype(jnp.float32)
        _af = _af * jax.random.uniform(jax.random.fold_in(_gk, 3), (2048, 2048), jnp.float32, 0.05, 1)
        adj = _af
        return (x, adj)
    x, adj = _rec_inputs()

    def _L0_gnn_setup():
        import jax, jax.numpy as jnp
        import numpy as np
        N, H, HEADS = (2048, 128, 3)
        ALPHA = 0.2
        NEG_INF = -9000000000000000.0

        def _sign_adj(key, n, density):
            k1, k2 = jax.random.split(key)
            mask = jax.random.uniform(k1, (n, n)) < density
            sign = jnp.where(jax.random.uniform(k2, (n, n)) < 0.5, -1.0, 1.0)
            adj = jnp.where(mask, sign, 0.0).astype(jnp.float32)
            idx = jnp.arange(n)
            return adj.at[idx, idx].set(1.0)

        def _gru_cell(x, hstate, Wih, Whh, bih, bhh):
            gi = x @ Wih.T + bih
            gh = hstate @ Whh.T + bhh
            ir, iz, inn = jnp.split(gi, 3, axis=1)
            hr, hz, hn = jnp.split(gh, 3, axis=1)
            r = jax.nn.sigmoid(ir + hr)
            z = jax.nn.sigmoid(iz + hz)
            n = jnp.tanh(inn + r * hn)
            return (1.0 - z) * n + z * hstate

        def _gat_head(h, node_adj, edge_adj, W, a):
            hW = h @ W
            hp = (node_adj > 0).astype(hW.dtype) @ hW
            hm = (node_adj < 0).astype(hW.dtype) @ hW
            e_plus = jax.nn.leaky_relu(jnp.concatenate([hp, hm], axis=1) @ a, ALPHA)[:, 0]
            e_minus = jax.nn.leaky_relu(jnp.concatenate([hm, hp], axis=1) @ a, ALPHA)[:, 0]
            att = jnp.where(edge_adj > 0, e_plus[None, :], NEG_INF)
            att = jnp.where(edge_adj < 0, e_minus[None, :], att)
            att = jax.nn.softmax(att, axis=1)
            return att * edge_adj @ hW
        key = jax.random.key(seed)
        ks = jax.random.split(key, 16)
        std = 0.01
        gain = 1.414
        return {'h': jax.random.normal(ks[0], (N, H), jnp.float32), 'node_adj': _sign_adj(ks[1], N, 0.005), 'edge_adj': _sign_adj(ks[2], N, 0.005), 'gat_W': jax.random.normal(ks[3], (HEADS, H, H), jnp.float32) * (gain / np.sqrt(H, dtype=np.float32)), 'gat_a': jax.random.normal(ks[4], (HEADS, 2 * H, 1), jnp.float32) * 0.1, 'edge_Wih': jax.random.normal(ks[5], (3 * H, H), jnp.float32) * std, 'edge_Whh': jax.random.normal(ks[6], (3 * H, H), jnp.float32) * std, 'edge_bih': jnp.zeros((3 * H,), jnp.float32), 'edge_bhh': jnp.zeros((3 * H,), jnp.float32), 'node_Wih': jax.random.normal(ks[7], (3 * H, H), jnp.float32) * std, 'node_Whh': jax.random.normal(ks[8], (3 * H, H), jnp.float32) * std, 'node_bih': jnp.zeros((3 * H,), jnp.float32), 'node_bhh': jnp.zeros((3 * H,), jnp.float32)}
    _L0_gnn_all = _L0_gnn_setup()
    _L0_gnn_in = {k: v for k, v in _L0_gnn_all.items() if k in ('gat_W', 'gat_a', 'edge_Wih', 'edge_Whh', 'edge_bih', 'edge_bhh', 'node_Wih', 'node_Whh', 'node_bih', 'node_bhh')}
    del _L0_gnn_all

    def _L0_ffn_setup():
        import math
        import jax, jax.numpy as jnp
        import numpy as np
        CAPACITY_FACTOR = 1.25
        key = jax.random.key(seed)
        ks = jax.random.split(key, 5)
        B, L, D, F, E = (8, 4096, 128, 512, 8)
        h = jax.random.normal(ks[0], (B, L, D), dtype=jnp.float32)
        gate_w = jax.random.normal(ks[1], (D, E), dtype=jnp.float32) * 0.02
        gate_b = jnp.zeros((E,), dtype=jnp.float32)
        w1 = jax.random.normal(ks[2], (E, D, F), dtype=jnp.float32) * (1.0 / math.sqrt(D))
        b1 = jnp.zeros((E, F), dtype=jnp.float32)
        w2 = jax.random.normal(ks[3], (E, F, D), dtype=jnp.float32) * (1.0 / math.sqrt(F))
        b2 = jnp.zeros((E, D), dtype=jnp.float32)
        return {'h': h, 'gate_w': gate_w, 'gate_b': gate_b, 'w1': w1, 'b1': b1, 'w2': w2, 'b2': b2}
    _L0_ffn_all = _L0_ffn_setup()
    _L0_ffn_in = {k: v for k, v in _L0_ffn_all.items() if k in ('gate_w', 'gate_b', 'w1', 'b1', 'w2', 'b2')}
    del _L0_ffn_all

    def _L1_gnn_setup():
        import jax, jax.numpy as jnp
        import numpy as np
        N = 4096
        F_IN = 128
        F_OUT = 128
        key = jax.random.key(seed)
        k1, k2, k3 = jax.random.split(key, 3)
        H = jax.random.normal(k1, (N, F_IN), dtype=jnp.float32)
        A_tilde = jax.random.uniform(k2, (N, N), dtype=jnp.float32)
        limit = np.sqrt(6.0 / (F_IN + F_OUT)).astype(np.float32)
        W = jax.random.uniform(k3, (F_IN, F_OUT), dtype=jnp.float32, minval=-limit, maxval=limit)
        return {'H': H, 'A_tilde': A_tilde, 'W': W}
    _L1_gnn_all = _L1_gnn_setup()
    _L1_gnn_in = {k: v for k, v in _L1_gnn_all.items() if k in ('W',)}
    del _L1_gnn_all

    def _L1_ffn_setup():
        import jax, jax.numpy as jnp
        import numpy as np
        INPUT_WIDTH = 128
        DEPTH = 7
        OUTPUT_WIDTH = 128
        N_NODES = 2 ** (DEPTH + 1) - 1
        key = jax.random.key(seed)
        k_x, k_w1, k_w2 = jax.random.split(key, 3)
        init1 = 1.0 / np.sqrt(INPUT_WIDTH)
        x = jax.random.normal(k_x, (2, 512, INPUT_WIDTH), dtype=jnp.float32)
        w1s = jax.random.uniform(k_w1, (N_NODES, INPUT_WIDTH), jnp.float32, -init1, init1)
        b1s = jnp.zeros((N_NODES,), jnp.float32)
        w2s = jax.random.uniform(k_w2, (N_NODES, INPUT_WIDTH, OUTPUT_WIDTH), jnp.float32, -init1, init1)
        b2s = jnp.zeros((N_NODES, OUTPUT_WIDTH), jnp.float32)
        return {'x': x, 'w1s': w1s, 'b1s': b1s, 'w2s': w2s, 'b2s': b2s}
    _L1_ffn_all = _L1_ffn_setup()
    _L1_ffn_in = {k: v for k, v in _L1_ffn_all.items() if k in ('w1s', 'b1s', 'w2s', 'b2s')}
    del _L1_ffn_all

    def _L2_gnn_setup():
        import jax, jax.numpy as jnp
        import numpy as np
        N, D_IN, D_OUT = (8192, 128, 128)
        key = jax.random.key(seed)
        k1, k2, k3, k4 = jax.random.split(key, 4)
        x = jax.random.normal(k1, (N, D_IN), dtype=jnp.float32)
        adj = jax.random.uniform(k2, (N, N), dtype=jnp.float32)
        W = jax.random.normal(k3, (D_IN, D_OUT), dtype=jnp.float32) / np.sqrt(D_IN)
        b = jax.random.normal(k4, (D_OUT,), dtype=jnp.float32) * 0.01
        return {'x': x, 'adj': adj, 'W': W, 'b': b}
    _L2_gnn_all = _L2_gnn_setup()
    _L2_gnn_in = {k: v for k, v in _L2_gnn_all.items() if k in ('W', 'b')}
    del _L2_gnn_all

    def _L2_ffn_setup():
        import jax, jax.numpy as jnp
        import numpy as np
        BN_EPS = 0.001

        def _bn(h, g, b, m, v):
            return g * (h - m) * jax.lax.rsqrt(v + BN_EPS) + b
        key = jax.random.key(seed)
        ks = jax.random.split(key, 8)
        B, F, Df = (128, 64, 128)
        E, H, D = (8, 128, 128)
        s1 = 1.0 / np.sqrt(Df)
        s2 = 1.0 / np.sqrt(H)
        return {'x': jax.random.normal(ks[0], (B, F, Df), jnp.float32), 'Wr': jax.random.normal(ks[1], (Df, E), jnp.float32) * s1, 'br': jnp.zeros((E,), jnp.float32), 'W1': jax.random.normal(ks[2], (E, Df, H), jnp.float32) * s1, 'b1': jnp.zeros((E, H), jnp.float32), 'g1': jnp.ones((E, H), jnp.float32), 'be1': jnp.zeros((E, H), jnp.float32), 'm1': jnp.zeros((E, H), jnp.float32), 'v1': jnp.ones((E, H), jnp.float32), 'W2': jax.random.normal(ks[3], (E, H, H), jnp.float32) * s2, 'b2': jnp.zeros((E, H), jnp.float32), 'g2': jnp.ones((E, H), jnp.float32), 'be2': jnp.zeros((E, H), jnp.float32), 'm2': jnp.zeros((E, H), jnp.float32), 'v2': jnp.ones((E, H), jnp.float32), 'Wo': jax.random.normal(ks[4], (E, H, D), jnp.float32) * s2, 'bo': jnp.zeros((E, D), jnp.float32)}
    _L2_ffn_all = _L2_ffn_setup()
    _L2_ffn_in = {k: v for k, v in _L2_ffn_all.items() if k in ('Wr', 'br', 'W1', 'b1', 'g1', 'be1', 'm1', 'v1', 'W2', 'b2', 'g2', 'be2', 'm2', 'v2', 'Wo', 'bo')}
    del _L2_ffn_all

    def _L3_gnn_setup():
        import jax, jax.numpy as jnp
        import numpy as np
        N = 4096
        IN_DIM = 128
        OUT_DIM = 128
        key = jax.random.key(seed)
        k1, k2, k3, k4 = jax.random.split(key, 4)
        x = jax.random.normal(k1, (N, IN_DIM), dtype=jnp.float32)
        adj = jax.random.uniform(k2, (N, N), dtype=jnp.float32)
        bound = 1.0 / np.sqrt(IN_DIM)
        W = jax.random.uniform(k3, (IN_DIM, OUT_DIM), dtype=jnp.float32, minval=-bound, maxval=bound)
        b = jax.random.uniform(k4, (OUT_DIM,), dtype=jnp.float32, minval=-bound, maxval=bound)
        return {'x': x, 'adj': adj, 'W': W, 'b': b}
    _L3_gnn_all = _L3_gnn_setup()
    _L3_gnn_in = {k: v for k, v in _L3_gnn_all.items() if k in ('W', 'b')}
    del _L3_gnn_all

    def _L3_ffn_setup():
        import jax, jax.numpy as jnp
        import numpy as np
        DIM = 128
        HEADS = 8
        NUM_KEYS = 128
        NUM_KV = NUM_KEYS ** 2
        PK_TOPK = 16
        FINAL_TOPK = 16
        DIM_KEY = DIM // 2
        P = 2

        def _pk(x, Wq_pk, pk_keys):
            b, n, _ = x.shape
            q = (x @ Wq_pk).reshape(b, n, P, HEADS, DIM_KEY).transpose(2, 0, 1, 3, 4)
            sim = jnp.einsum('pbnhd,pkhd->pbnhk', q, pk_keys)
            scores, idx = jax.lax.top_k(sim, PK_TOPK)
            idx0 = idx[0]
            idx1 = idx[1] * NUM_KEYS
            index = (idx0[..., :, None] + idx1[..., None, :]).reshape(b, n, HEADS, PK_TOPK * PK_TOPK)
            score = (scores[0][..., :, None] + scores[1][..., None, :]).reshape(b, n, HEADS, PK_TOPK * PK_TOPK)
            final_scores, pk_idx = jax.lax.top_k(score, FINAL_TOPK)
            final_indices = jnp.take_along_axis(index, pk_idx, axis=-1)
            final_scores = jax.nn.softmax(final_scores, axis=-1)
            return (final_scores, final_indices)
        key = jax.random.key(seed)
        ks = jax.random.split(key, 7)
        b, n = (2, 512)
        std = 0.02
        x = jax.random.normal(ks[0], (b, n, DIM), dtype=jnp.float32)
        Wq_pk = jax.random.normal(ks[1], (DIM, P * HEADS * DIM_KEY), dtype=jnp.float32) * std
        pk_keys = jax.random.normal(ks[2], (P, NUM_KEYS, HEADS, DIM_KEY), dtype=jnp.float32) * std
        Wq = jax.random.normal(ks[3], (DIM, HEADS * DIM), dtype=jnp.float32) * std
        keys_table = jax.random.normal(ks[4], (NUM_KV * HEADS, DIM), dtype=jnp.float32) * std
        values_table = jax.random.normal(ks[5], (NUM_KV * HEADS, DIM), dtype=jnp.float32) * std
        Wo = jax.random.normal(ks[6], (DIM * HEADS, DIM), dtype=jnp.float32) * std
        return {'x': x, 'Wq_pk': Wq_pk, 'pk_keys': pk_keys, 'Wq': Wq, 'keys_table': keys_table, 'values_table': values_table, 'Wo': Wo}
    _L3_ffn_all = _L3_ffn_setup()
    _L3_ffn_in = {k: v for k, v in _L3_ffn_all.items() if k in ('Wq_pk', 'pk_keys', 'Wq', 'keys_table', 'values_table', 'Wo')}
    del _L3_ffn_all
    return {'x': x, 'adj': adj, 'L0_gnn_gat_W': _L0_gnn_in['gat_W'], 'L0_gnn_gat_a': _L0_gnn_in['gat_a'], 'L0_gnn_edge_Wih': _L0_gnn_in['edge_Wih'], 'L0_gnn_edge_Whh': _L0_gnn_in['edge_Whh'], 'L0_gnn_edge_bih': _L0_gnn_in['edge_bih'], 'L0_gnn_edge_bhh': _L0_gnn_in['edge_bhh'], 'L0_gnn_node_Wih': _L0_gnn_in['node_Wih'], 'L0_gnn_node_Whh': _L0_gnn_in['node_Whh'], 'L0_gnn_node_bih': _L0_gnn_in['node_bih'], 'L0_gnn_node_bhh': _L0_gnn_in['node_bhh'], 'L0_ffn_gate_w': _L0_ffn_in['gate_w'], 'L0_ffn_gate_b': _L0_ffn_in['gate_b'], 'L0_ffn_w1': _L0_ffn_in['w1'], 'L0_ffn_b1': _L0_ffn_in['b1'], 'L0_ffn_w2': _L0_ffn_in['w2'], 'L0_ffn_b2': _L0_ffn_in['b2'], 'L1_gnn_W': _L1_gnn_in['W'], 'L1_ffn_w1s': _L1_ffn_in['w1s'], 'L1_ffn_b1s': _L1_ffn_in['b1s'], 'L1_ffn_w2s': _L1_ffn_in['w2s'], 'L1_ffn_b2s': _L1_ffn_in['b2s'], 'L2_gnn_W': _L2_gnn_in['W'], 'L2_gnn_b': _L2_gnn_in['b'], 'L2_ffn_Wr': _L2_ffn_in['Wr'], 'L2_ffn_br': _L2_ffn_in['br'], 'L2_ffn_W1': _L2_ffn_in['W1'], 'L2_ffn_b1': _L2_ffn_in['b1'], 'L2_ffn_g1': _L2_ffn_in['g1'], 'L2_ffn_be1': _L2_ffn_in['be1'], 'L2_ffn_m1': _L2_ffn_in['m1'], 'L2_ffn_v1': _L2_ffn_in['v1'], 'L2_ffn_W2': _L2_ffn_in['W2'], 'L2_ffn_b2': _L2_ffn_in['b2'], 'L2_ffn_g2': _L2_ffn_in['g2'], 'L2_ffn_be2': _L2_ffn_in['be2'], 'L2_ffn_m2': _L2_ffn_in['m2'], 'L2_ffn_v2': _L2_ffn_in['v2'], 'L2_ffn_Wo': _L2_ffn_in['Wo'], 'L2_ffn_bo': _L2_ffn_in['bo'], 'L3_gnn_W': _L3_gnn_in['W'], 'L3_gnn_b': _L3_gnn_in['b'], 'L3_ffn_Wq_pk': _L3_ffn_in['Wq_pk'], 'L3_ffn_pk_keys': _L3_ffn_in['pk_keys'], 'L3_ffn_Wq': _L3_ffn_in['Wq'], 'L3_ffn_keys_table': _L3_ffn_in['keys_table'], 'L3_ffn_values_table': _L3_ffn_in['values_table'], 'L3_ffn_Wo': _L3_ffn_in['Wo']}

def reference(x, adj, L0_gnn_gat_W, L0_gnn_gat_a, L0_gnn_edge_Wih, L0_gnn_edge_Whh, L0_gnn_edge_bih, L0_gnn_edge_bhh, L0_gnn_node_Wih, L0_gnn_node_Whh, L0_gnn_node_bih, L0_gnn_node_bhh, L0_ffn_gate_w, L0_ffn_gate_b, L0_ffn_w1, L0_ffn_b1, L0_ffn_w2, L0_ffn_b2, L1_gnn_W, L1_ffn_w1s, L1_ffn_b1s, L1_ffn_w2s, L1_ffn_b2s, L2_gnn_W, L2_gnn_b, L2_ffn_Wr, L2_ffn_br, L2_ffn_W1, L2_ffn_b1, L2_ffn_g1, L2_ffn_be1, L2_ffn_m1, L2_ffn_v1, L2_ffn_W2, L2_ffn_b2, L2_ffn_g2, L2_ffn_be2, L2_ffn_m2, L2_ffn_v2, L2_ffn_Wo, L2_ffn_bo, L3_gnn_W, L3_gnn_b, L3_ffn_Wq_pk, L3_ffn_pk_keys, L3_ffn_Wq, L3_ffn_keys_table, L3_ffn_values_table, L3_ffn_Wo):
    import jax
    import jax.numpy as jnp

    def _L0_gnn_ref(h, node_adj, edge_adj, gat_W, gat_a, edge_Wih, edge_Whh, edge_bih, edge_bhh, node_Wih, node_Whh, node_bih, node_bhh):
        import jax, jax.numpy as jnp
        import numpy as np
        N, H, HEADS = (2048, 128, 3)
        ALPHA = 0.2
        NEG_INF = -9000000000000000.0

        def _sign_adj(key, n, density):
            k1, k2 = jax.random.split(key)
            mask = jax.random.uniform(k1, (n, n)) < density
            sign = jnp.where(jax.random.uniform(k2, (n, n)) < 0.5, -1.0, 1.0)
            adj = jnp.where(mask, sign, 0.0).astype(jnp.float32)
            idx = jnp.arange(n)
            return adj.at[idx, idx].set(1.0)

        def _gru_cell(x, hstate, Wih, Whh, bih, bhh):
            gi = x @ Wih.T + bih
            gh = hstate @ Whh.T + bhh
            ir, iz, inn = jnp.split(gi, 3, axis=1)
            hr, hz, hn = jnp.split(gh, 3, axis=1)
            r = jax.nn.sigmoid(ir + hr)
            z = jax.nn.sigmoid(iz + hz)
            n = jnp.tanh(inn + r * hn)
            return (1.0 - z) * n + z * hstate

        def _gat_head(h, node_adj, edge_adj, W, a):
            hW = h @ W
            hp = (node_adj > 0).astype(hW.dtype) @ hW
            hm = (node_adj < 0).astype(hW.dtype) @ hW
            e_plus = jax.nn.leaky_relu(jnp.concatenate([hp, hm], axis=1) @ a, ALPHA)[:, 0]
            e_minus = jax.nn.leaky_relu(jnp.concatenate([hm, hp], axis=1) @ a, ALPHA)[:, 0]
            att = jnp.where(edge_adj > 0, e_plus[None, :], NEG_INF)
            att = jnp.where(edge_adj < 0, e_minus[None, :], att)
            att = jax.nn.softmax(att, axis=1)
            return att * edge_adj @ hW
        dn = jnp.diag(node_adj)
        de = jnp.diag(edge_adj)
        idx = jnp.arange(node_adj.shape[0])
        node_adj_norm = node_adj.at[idx, idx].add(-dn)
        edge_adj_norm = edge_adj.at[idx, idx].add(-de)
        node_support = node_adj_norm @ h
        edge_output = _gru_cell(node_support, h, edge_Wih, edge_Whh, edge_bih, edge_bhh)
        edge_support = _gat_head(h, node_adj_norm, edge_adj_norm, gat_W[0], gat_a[0])
        for i in range(1, HEADS):
            edge_support = edge_support + _gat_head(h, node_adj_norm, edge_adj_norm, gat_W[i], gat_a[i])
        edge_support = edge_support / HEADS
        node_output = _gru_cell(edge_support, h, node_Wih, node_Whh, node_bih, node_bhh)
        return de[:, None] * edge_output + dn[:, None] * node_output

    def _L0_ffn_ref(h, gate_w, gate_b, w1, b1, w2, b2):
        import math
        import jax, jax.numpy as jnp
        import numpy as np
        CAPACITY_FACTOR = 1.25
        B, L, D = h.shape
        E = gate_w.shape[1]
        T = B * L
        C = max(1, math.ceil(CAPACITY_FACTOR * T / E))
        x = h.reshape(T, D)
        logits = x @ gate_w + gate_b
        probs = jax.nn.softmax(logits, axis=-1)
        idx = jnp.argmax(probs, axis=-1)
        prb = jnp.take_along_axis(probs, idx[:, None], axis=1)[:, 0]
        one_hot = jax.nn.one_hot(idx, E, dtype=jnp.float32)
        pos = (jnp.cumsum(one_hot, axis=0) * one_hot).sum(-1).astype(jnp.int32) - 1
        kept = pos < C
        pos_safe = jnp.where(kept, pos, C)
        buf = jnp.zeros((E, C, D), dtype=h.dtype).at[idx, pos_safe].set(x, mode='drop')
        hmid = jax.nn.relu(jnp.einsum('ecd,edf->ecf', buf, w1) + b1[:, None, :])
        ybuf = jnp.einsum('ecf,efd->ecd', hmid, w2) + b2[:, None, :]
        pos_g = jnp.minimum(pos, C - 1)
        y_tok = ybuf[idx, pos_g] * (prb * kept)[:, None]
        y = y_tok.reshape(B, L, D)
        y = jnp.nan_to_num(y, nan=0.0, posinf=10000.0, neginf=-10000.0)
        return y

    def _L1_gnn_ref(H, A_tilde, W):
        import jax, jax.numpy as jnp
        import numpy as np
        N = 4096
        F_IN = 128
        F_OUT = 128
        d_inv_sqrt = jnp.sum(A_tilde, axis=1) ** (-0.5)
        A_norm = d_inv_sqrt[:, None] * A_tilde * d_inv_sqrt[None, :]
        H_next = A_norm @ H @ W
        return jax.nn.relu(H_next)

    def _L1_ffn_ref(x, w1s, b1s, w2s, b2s):
        import jax, jax.numpy as jnp
        import numpy as np
        INPUT_WIDTH = 128
        DEPTH = 7
        OUTPUT_WIDTH = 128
        N_NODES = 2 ** (DEPTH + 1) - 1
        B, S, D = x.shape
        flat_x = x.reshape(B * S, D)
        T = flat_x.shape[0]
        current = jnp.zeros((T,), dtype=jnp.int32)
        all_nodes = []
        all_logits = []
        for _ in range(DEPTH + 1):
            all_nodes.append(current)
            score = jnp.einsum('td,td->t', flat_x, w1s[current]) + b1s[current]
            all_logits.append(score)
            choice = ((jnp.sign(score) + 1.0) / 2.0).astype(jnp.int32)
            current = current * 2 + choice + 1
        logits = jnp.stack(all_logits, axis=1)
        path_weights = jax.nn.gelu(jnp.abs(logits), approximate=False)
        out = jnp.zeros((T, OUTPUT_WIDTH), dtype=x.dtype)
        for i in range(DEPTH + 1):
            nodes_i = all_nodes[i]
            t_i = jnp.einsum('td,tdo->to', flat_x, w2s[nodes_i]) + b2s[nodes_i]
            out = out + t_i * path_weights[:, i][:, None]
        return out.reshape(B, S, OUTPUT_WIDTH)

    def _L2_gnn_ref(x, adj, W, b):
        import jax, jax.numpy as jnp
        import numpy as np
        N, D_IN, D_OUT = (8192, 128, 128)
        support = jnp.matmul(x, W)
        out = jnp.matmul(adj, support) + b
        return jax.nn.relu(out)

    def _L2_ffn_ref(x, Wr, br, W1, b1, g1, be1, m1, v1, W2, b2, g2, be2, m2, v2, Wo, bo):
        import jax, jax.numpy as jnp
        import numpy as np
        BN_EPS = 0.001

        def _bn(h, g, b, m, v):
            return g * (h - m) * jax.lax.rsqrt(v + BN_EPS) + b
        feat = jnp.mean(x, axis=0)
        w = jax.nn.softmax(feat @ Wr + br, axis=-1)
        h = jnp.einsum('bfd,edh->bfeh', x, W1) + b1
        h = jax.nn.relu(_bn(h, g1, be1, m1, v1))
        h = jnp.einsum('bfeh,ehk->bfek', h, W2) + b2
        h = jax.nn.relu(_bn(h, g2, be2, m2, v2))
        y = jnp.einsum('bfeh,ehd->bfed', h, Wo) + bo
        return jnp.einsum('bfed,fe->bfd', y, w)

    def _L3_gnn_ref(x, adj, W, b):
        import jax, jax.numpy as jnp
        import numpy as np
        N = 4096
        IN_DIM = 128
        OUT_DIM = 128
        n = adj.shape[0]
        A_hat = adj + jnp.eye(n, dtype=adj.dtype)
        degree = A_hat.sum(axis=1)
        d_inv_sqrt = degree ** (-0.5)
        A_norm = A_hat * d_inv_sqrt[:, None] * d_inv_sqrt[None, :]
        out = A_norm @ x
        out = out @ W + b
        return jax.nn.relu(out)

    def _L3_ffn_ref(x, Wq_pk, pk_keys, Wq, keys_table, values_table, Wo):
        import jax, jax.numpy as jnp
        import numpy as np
        DIM = 128
        HEADS = 8
        NUM_KEYS = 128
        NUM_KV = NUM_KEYS ** 2
        PK_TOPK = 16
        FINAL_TOPK = 16
        DIM_KEY = DIM // 2
        P = 2

        def _pk(x, Wq_pk, pk_keys):
            b, n, _ = x.shape
            q = (x @ Wq_pk).reshape(b, n, P, HEADS, DIM_KEY).transpose(2, 0, 1, 3, 4)
            sim = jnp.einsum('pbnhd,pkhd->pbnhk', q, pk_keys)
            scores, idx = jax.lax.top_k(sim, PK_TOPK)
            idx0 = idx[0]
            idx1 = idx[1] * NUM_KEYS
            index = (idx0[..., :, None] + idx1[..., None, :]).reshape(b, n, HEADS, PK_TOPK * PK_TOPK)
            score = (scores[0][..., :, None] + scores[1][..., None, :]).reshape(b, n, HEADS, PK_TOPK * PK_TOPK)
            final_scores, pk_idx = jax.lax.top_k(score, FINAL_TOPK)
            final_indices = jnp.take_along_axis(index, pk_idx, axis=-1)
            final_scores = jax.nn.softmax(final_scores, axis=-1)
            return (final_scores, final_indices)
        b, n, d = x.shape
        q = (x @ Wq).reshape(b, n, HEADS, DIM) * DIM ** (-0.5)
        kv_scores, indices = _pk(x, Wq_pk, pk_keys)
        offsets = jnp.arange(HEADS, dtype=indices.dtype) * NUM_KV
        ind = indices + offsets[None, None, :, None]
        k = jnp.einsum('bnhk,bnhkd->bnhd', kv_scores, keys_table[ind])
        v = jnp.einsum('bnhk,bnhkd->bnhd', kv_scores, values_table[ind])
        sim = jnp.einsum('bihd,bjhd->bhij', q, k)
        neg = -jnp.finfo(sim.dtype).max
        causal = jnp.tril(jnp.ones((n, n), dtype=bool))
        sim = jnp.where(causal, sim, neg)
        attn = jax.nn.softmax(sim, axis=-1)
        out = jnp.einsum('bhij,bjhd->bhid', attn, v)
        out = out.transpose(0, 2, 1, 3).reshape(b, n, HEADS * DIM)
        return out @ Wo
    x = x + _L0_gnn_ref(_layernorm(x, axis=-1), adj, adj, L0_gnn_gat_W, L0_gnn_gat_a, L0_gnn_edge_Wih, L0_gnn_edge_Whh, L0_gnn_edge_bih, L0_gnn_edge_bhh, L0_gnn_node_Wih, L0_gnn_node_Whh, L0_gnn_node_bih, L0_gnn_node_bhh)
    x = x + _L0_ffn_ref(_layernorm(x, axis=-1)[None], L0_ffn_gate_w, L0_ffn_gate_b, L0_ffn_w1, L0_ffn_b1, L0_ffn_w2, L0_ffn_b2)[0]
    x = x + _L1_gnn_ref(_layernorm(x, axis=-1), adj, L1_gnn_W)
    x = x + _L1_ffn_ref(_layernorm(x, axis=-1)[None], L1_ffn_w1s, L1_ffn_b1s, L1_ffn_w2s, L1_ffn_b2s)[0]
    x = x + _L2_gnn_ref(_layernorm(x, axis=-1), adj, L2_gnn_W, L2_gnn_b)
    x = x + _L2_ffn_ref(_layernorm(x, axis=-1)[None], L2_ffn_Wr, L2_ffn_br, L2_ffn_W1, L2_ffn_b1, L2_ffn_g1, L2_ffn_be1, L2_ffn_m1, L2_ffn_v1, L2_ffn_W2, L2_ffn_b2, L2_ffn_g2, L2_ffn_be2, L2_ffn_m2, L2_ffn_v2, L2_ffn_Wo, L2_ffn_bo)[0]
    x = x + _L3_gnn_ref(_layernorm(x, axis=-1), adj, L3_gnn_W, L3_gnn_b)
    x = x + _L3_ffn_ref(_layernorm(x, axis=-1)[None], L3_ffn_Wq_pk, L3_ffn_pk_keys, L3_ffn_Wq, L3_ffn_keys_table, L3_ffn_values_table, L3_ffn_Wo)[0]
    return x

_drawn_inputs = setup_inputs


def setup_inputs(seed=0):
    import zlib

    import numpy as np

    out = dict(_drawn_inputs(seed))
    spreads = {'L0_gnn_edge_bih': (0.0, 0.1),
     'L0_gnn_edge_bhh': (0.0, 0.1),
     'L0_gnn_node_bih': (0.0, 0.1),
     'L0_gnn_node_bhh': (0.0, 0.1),
     'L0_ffn_gate_b': (0.0, 0.1),
     'L0_ffn_b1': (0.0, 0.1),
     'L0_ffn_b2': (0.0, 0.1),
     'L1_ffn_b1s': (0.0, 0.1),
     'L1_ffn_b2s': (0.0, 0.1),
     'L2_ffn_br': (0.0, 0.8),
     'L2_ffn_b1': (0.0, 0.708),
     'L2_ffn_g1': (1.0, 0.6),
     'L2_ffn_be1': (0.0, 0.743),
     'L2_ffn_m1': (0.0, 0.709),
     'L2_ffn_v1': (1.0, 0.6),
     'L2_ffn_b2': (0.0, 0.537),
     'L2_ffn_g2': (1.0, 0.6),
     'L2_ffn_be2': (0.0, 0.563),
     'L2_ffn_m2': (0.0, 0.55),
     'L2_ffn_v2': (1.0, 0.6),
     'L2_ffn_bo': (0.0, 0.38)}
    factors = {'L2_gnn_b': 8.0,
     'L3_gnn_b': 3.937,
     'L3_ffn_Wq_pk': 55.711,
     'L3_ffn_pk_keys': 55.429,
     'L3_ffn_Wq': 64.0,
     'L3_ffn_keys_table': 64.0,
     'L3_ffn_values_table': 51.652,
     'L3_ffn_Wo': 49.488}
    for name, (base, spread) in spreads.items():
        noise = np.random.default_rng([zlib.crc32(name.encode()), seed]).standard_normal(out[name].shape)
        drawn = base * np.exp(spread * noise) if base else spread * noise
        out[name] = jnp.asarray(drawn.astype(out[name].dtype))
    for name, factor in factors.items():
        out[name] = (out[name] * factor).astype(out[name].dtype)
    return out
```

```python
from contextlib import ExitStack

import concourse.bass as bass
from concourse import mybir

F32 = mybir.dt.float32
BF16 = mybir.dt.bfloat16
I32 = mybir.dt.int32
ALU = mybir.AluOpType
ACT = mybir.ActivationFunctionType
AX = mybir.AxisListType.X

P = 128
N = 2048
NT = N // P
CW = 512
NC = N // CW
LN_EPS = 1e-5
RING = 4


def build(nc, io, upto=99):
    with ExitStack() as ctx:
        kept = {}

        def sb(name, shape, dt=F32, scope=ctx):
            return scope.enter_context(nc.sbuf_tensor(name, shape, dt))

        retired = []

        def sem(name, scope=ctx):
            s = scope.enter_context(nc.semaphore(name))
            if scope is not ctx:
                assert s.num not in retired
                scope.callback(retired.append, s.num)
            return s

        def clear_retired():
            nums = sorted(retired)
            retired.clear()
            with nc.Block() as block:
                @block.gpsimd
                def _(pool):
                    while nums:
                        first = last = nums.pop(0)
                        while nums and nums[0] == last + 1:
                            last = nums.pop(0)
                        pool.sem_clear(range(first, last + 1))

        psum = ctx.enter_context(nc.psum_tensor("psum", [P, 8 * CW], F32))
        bank = [psum[:, i * CW:(i + 1) * CW] for i in range(8)]
        xT = sb("xT", [P, N])
        hT = sb("hT", [P, N])
        ident = sb("ident", [P, P])
        mean_w = sb("mean_w", [P, P])
        ones = sb("ones", [P, P])
        tri = sb("tri", [P, P])
        eps = sb("eps", [P, 1])
        off_diag = sb("off_diag", [P, P])
        rowsum = sb("rowsum", [P, N])
        diag_col = sb("diag_col", [P, NT])
        ring = sb("ring", [P, RING, N])
        a_ready = [sem(f"a_ready{i}") for i in range(RING)]
        a_used = sem("a_used")

        class Stream:
            issued = 0
            taken = 0

        def a_source(layout, n):
            if layout == "tile":
                return lambda slot: (ring[:, slot, :], io["adjT"][n * P:(n + 1) * P, :])
            q, s = n // 4, n % 4
            return lambda slot: (ring[:, slot, :].rearrange("p (m c) -> p m c", m=4),
                                 io["adjT"][4 * s * P:(4 * s + 4) * P, q * CW:(q + 1) * CW]
                                 .rearrange("(m p) c -> p m c", p=P))

        plan = []
        plan += [a_source("tile", n) for n in range(NT)]
        plan += [a_source("chunk", n) for n in range(NT)]
        for _ in range(3):
            plan += [a_source("tile", n) for n in range(NT)]

        def issue_a(eng, upto_n):
            while Stream.issued < min(upto_n, len(plan)):
                n = Stream.issued
                if n >= RING:
                    eng.wait_ge(a_used, n - RING + 1)
                dst, src = plan[n](n % RING)
                eng.dma_start(dst, src).then_inc(a_ready[n % RING], 16)
                Stream.issued += 1

        def wait_a(eng, n):
            eng.wait_ge(a_ready[n % RING], 16 * (n // RING + 1))

        def chunk(t, c):
            return t[:, c * CW:(c + 1) * CW]

        def tile(t, i):
            return t[:, i * P:(i + 1) * P]

        class Chain:
            def __init__(self, eng, s):
                self.eng, self.s, self.n = eng, s, 0

            def __call__(self, ins):
                self.n += 1
                ins.then_inc(self.s, 1)
                self.eng.wait_ge(self.s, self.n)

        small = {}
        w_loaded = sem("w_loaded")
        n_w = [0]

        def weight(eng, name, shape, src=None, dt=F32, scope=ctx):
            t = sb("w_" + name, shape, dt, scope)
            eng.dma_start(t[tuple(slice(None) for _ in shape)], io[name] if src is None else src).then_inc(w_loaded, 16)
            n_w[0] += 1
            return t

        consts_set = sem("consts_set")
        x_loaded = sem("x_loaded")
        with nc.Block() as block:
            @block.sync
            def _(sp):
                sp.dma_start(xT[:, :], io["xT"]).then_inc(x_loaded, 16)
                issue_a(sp, RING)

            @block.gpsimd
            def _(pool):
                pool.memset(ident[:, :], 0.0).then_inc(consts_set, 1)
                pool.memset(off_diag[:, :], 1.0).then_inc(consts_set, 1)
                pool.memset(mean_w[:, :], 1.0 / P).then_inc(consts_set, 1)
                pool.memset(ones[:, :], 1.0).then_inc(consts_set, 1)
                pool.memset(eps[:, :], LN_EPS).then_inc(consts_set, 1)
                pool.memset(rowsum[:, :], 0.0).then_inc(consts_set, 1)
                pool.wait_ge(consts_set, 2)
                pool.affine_select(out=ident[:, :], in_=ident[:, :], compare_op=ALU.not_equal, fill=1.0,
                                   base=0, pattern=[[-1, P]], channel_multiplier=1).then_inc(consts_set, 1)
                pool.affine_select(out=off_diag[:, :], in_=off_diag[:, :], compare_op=ALU.not_equal, fill=0.0,
                                   base=0, pattern=[[-1, P]], channel_multiplier=1).then_inc(consts_set, 1)
                pool.wait_ge(x_loaded, 16)

        def layer_norm(tag, loads=None):
            with ExitStack() as st, nc.Block() as block:
                squares = sb(f"squares_{tag}", [P, N], scope=st)
                std = sb(f"std_{tag}", [P, NT], scope=st)
                rstd = sb(f"rstd_{tag}", [P, NT], scope=st)
                rstd_d = sb(f"rstd_d_{tag}", [P, NT, P], scope=st)
                mean_done, centred, squared, var_done, std_done, inverted, placed, rstd_spread = (
                    sem(f"{k}_{tag}", st) for k in ("mean_done", "centred", "squared", "var_done", "std_done",
                                                    "inverted", "placed", "rstd_spread"))

                @block.sync
                def _(sp):
                    if loads:
                        loads(sp)

                @block.tensor
                def _(pe):
                    for c in range(NC):
                        pe.matmul(bank[c][:, :], mean_w[:, :], chunk(xT, c), start=True, stop=True).then_inc(mean_done, 1)
                    for i in range(NT):
                        if i % 4 == 0:
                            pe.wait_ge(squared, i // 4 + 1)
                        ins = pe.matmul(bank[4][:, i:i + 1], tile(squares, i), mean_w[:, 0:1], start=True, stop=True)
                    ins.then_inc(var_done, 1)
                    for c in range(NC):
                        pe.wait_ge(placed, c + 1)
                        pe.matmul(bank[c][:, :], ones[:, :], rstd_d[:, 4 * c:4 * c + 4, :].rearrange("p t d -> p (t d)"),
                                  start=True, stop=True).then_inc(rstd_spread, 1)

                @block.scalar
                def _(act):
                    for c in range(NC):
                        act.wait_ge(centred, c + 1)
                        act.activation(chunk(squares, c), chunk(hT, c), ACT.Square).then_inc(squared, 1)
                    act.wait_ge(var_done, 1)
                    act.activation(std[:, :], bank[4][:, 0:NT], ACT.Sqrt, bias=eps[:, 0:1]).then_inc(std_done, 1)

                @block.vector
                def _(dve):
                    for c in range(NC):
                        dve.wait_ge(mean_done, c + 1)
                        dve.tensor_tensor(chunk(hT, c), chunk(xT, c), bank[c][:, :], ALU.subtract).then_inc(centred, 1)
                    dve.wait_ge(std_done, 1)
                    dve.reciprocal(rstd[:, :], std[:, :]).then_inc(inverted, 1)
                    dve.wait_ge(inverted, 1)
                    for i in range(NT):
                        ins = dve.tensor_scalar(rstd_d[:, i, :], ident[:, :], rstd[:, i:i + 1], None, ALU.mult)
                        if i % 4 == 3:
                            ins.then_inc(placed, 1)
                    for c in range(NC):
                        dve.wait_ge(rstd_spread, c + 1)
                        dve.tensor_tensor(chunk(hT, c), chunk(hT, c), bank[c][:, :], ALU.mult)

        HEADS = 3
        base = 0
        layer_norm("l0g")
        with ExitStack() as l0:
            hW = sb("hW", [P, NT, HEADS * P], scope=l0)
            uP = sb("uP", [P, NT, 19], BF16, l0)
            uM = sb("uM", [P, NT, 19], BF16, l0)
            g9 = [sb(f"g9{s}", [P, NT, 9], BF16, l0) for s in "pm"]
            g = sb("g", [P, NT, 6], scope=l0)
            support = sb("support", [P, N], scope=l0)
            diag_b = sb("diag_b", [P, N], scope=l0)
            w_hw = sb("w_hw", [P, HEADS * P + 6], scope=l0)
            gru_w, gru_b = {}, {}
            for kind in ("edge", "node"):
                gru_w[kind] = [sb(f"{kind}_{m}", [P, 3 * P], scope=l0) for m in ("ih", "hh")]
                gru_b[kind] = [sb(f"{kind}_b{m}", [P, 3], scope=l0) for m in ("ih", "hh", "sum")]

            with ExitStack() as st:
                h_rows = sb("h_rows", [P, NT, P], scope=st)
                with ExitStack() as s1, nc.Block() as block:
                    gat_wT = sb("gat_wT", [P, HEADS, P], scope=s1)
                    gat_a = sb("gat_a", [P, HEADS, 2], scope=s1)
                    u = sb("u", [P, NT, 6], scope=s1)
                    rest = sb("rest", [P, NT, 6], scope=s1)
                    part = sb("part", [P, 3, NT, 6], BF16, s1)
                    wl, wa_done, wa_copied, h_turned, h_copied, hw_done, hw_copied, split = (
                        sem(k, s1) for k in ("l0_wl", "wa_done", "wa_copied", "h_turned", "h_copied", "hw_done", "hw_copied", "split"))

                    @block.sync
                    def _(sp):
                        sp.dma_start(gat_wT[:, :, :], io["gat_wT"]).then_inc(wl, 16)
                        sp.dma_start(gat_a[:, :, :], io["gat_a"]).then_inc(wl, 16)
                        sp.dma_start(w_hw[:, 0:HEADS * P].rearrange("p (k o) -> p k o", k=HEADS),
                                     io["gat_W"].rearrange("k p o -> p k o")).then_inc(wl, 16)
                        for kind in ("edge", "node"):
                            for w, b, m in zip(gru_w[kind], gru_b[kind], ("ih", "hh")):
                                sp.dma_start(w[:, :], io[f"{kind}_W{m}T"]).then_inc(wl, 16)
                                sp.dma_start(b[:, :], io[f"{kind}_b{m}"]).then_inc(wl, 16)
                        sp.wait_ge(wl, 16 * 11)

                    @block.tensor
                    def _(pe):
                        for i in range(NT):
                            ins = pe.transpose(bank[i // 4][:, (i % 4) * P:(i % 4 + 1) * P], tile(hT, i), ident[:, :])
                            if i % 4 == 3:
                                ins.then_inc(h_turned, 1)
                        pe.wait_ge(wl, 16 * 11)
                        for k in range(HEADS):
                            ins = pe.matmul(bank[4][:, 2 * k:2 * k + 2], gat_wT[:, k, :], gat_a[:, k, :], start=True, stop=True)
                        ins.then_inc(wa_done, 1)
                        pe.wait_ge(wa_copied, 1)
                        for i in range(NT):
                            if i >= 3:
                                pe.wait_ge(hw_copied, i - 2)
                            pe.matmul(bank[5 + i % 3][:, 0:HEADS * P + 6], tile(hT, i), w_hw[:, :], start=True, stop=True).then_inc(hw_done, 1)

                    @block.vector
                    def _(dve):
                        dve.wait_ge(wa_done, 1)
                        dve.tensor_copy(w_hw[:, HEADS * P:].rearrange("p (s k) -> p k s", s=2),
                                        bank[4][:, 0:6].rearrange("p (k s) -> p k s", k=3)).then_inc(wa_copied, 1)
                        for i in range(NT):
                            dve.wait_ge(hw_done, i + 1)
                            dve.tensor_copy(hW[:, i, :], bank[5 + i % 3][:, 0:HEADS * P])
                            dve.tensor_copy(u[:, i, :], bank[5 + i % 3][:, HEADS * P:HEADS * P + 6]).then_inc(hw_copied, 1)
                        dve.wait_ge(hw_copied, NT)
                        link = Chain(dve, split)
                        link(dve.tensor_copy(part[:, 0, :, :], u[:, :, :]))
                        link(dve.tensor_tensor(rest[:, :, :], u[:, :, :], part[:, 0, :, :], ALU.subtract))
                        link(dve.tensor_copy(part[:, 1, :, :], rest[:, :, :]))
                        link(dve.tensor_tensor(rest[:, :, :], rest[:, :, :], part[:, 1, :, :], ALU.subtract))
                        link(dve.tensor_copy(part[:, 2, :, :], rest[:, :, :]))
                        dve.memset(uP[:, :, 18:19], 0.0)
                        dve.memset(uM[:, :, 18:19], 1.0)
                        for s in range(3):
                            dve.tensor_copy(uP[:, :, 6 * s:6 * s + 6], part[:, s, :, :])
                            dve.tensor_copy(uM[:, :, 6 * s:6 * s + 3], part[:, s, :, 3:6])
                            dve.tensor_copy(uM[:, :, 6 * s + 3:6 * s + 6], part[:, s, :, 0:3])
                        for kind in ("edge", "node"):
                            dve.wait_ge(wl, 16 * 11)
                            bi, bh, bs = gru_b[kind]
                            dve.tensor_tensor(bs[:, :], bi[:, :], bh[:, :], ALU.add)

                    @block.scalar
                    def _(act):
                        for q in range(4):
                            act.wait_ge(h_turned, q + 1)
                            act.copy(h_rows[:, 4 * q:4 * q + 4, :].rearrange("p t d -> p (t d)"), bank[q][:, :])

                with ExitStack() as s2, nc.Block() as block:
                    pos = sb("pos", [P, 2, N], BF16, s2)
                    neg = sb("neg", [P, 2, N], BF16, s2)
                    diag_w = sb("diag_w", [P, P], scope=s2)
                    cleared, masked, a_mm, mask_used, summed, dcol, sup_done = (
                        sem(k, s2) for k in ("cleared", "masked", "a_mm", "mask_used", "summed", "dcol", "sup_done"))

                    @block.sync
                    def _(sp):
                        issue_a(sp, base + NT)

                    @block.vector
                    def _(dve):
                        for j in range(NT):
                            n = base + j
                            blk = ring[:, n % RING, j * P:(j + 1) * P]
                            wait_a(dve, n)
                            dve.tensor_tensor_reduce(out=diag_w[:, :], in0=blk, in1=ident[:, :], scale=1.0, scalar=0.0,
                                                     op0=ALU.mult, op1=ALU.add, accum_out=diag_col[:, j:j + 1]).then_inc(dcol, 1)
                            dve.wait_ge(dcol, j + 1)
                            dve.tensor_tensor(blk, blk, off_diag[:, :], ALU.mult).then_inc(cleared, 1)
                            dve.wait_ge(cleared, j + 1)
                            if j >= 2:
                                dve.wait_ge(mask_used, j - 1)
                            dve.tensor_scalar(pos[:, j % 2, :], ring[:, n % RING, :], 0.0, None, ALU.is_gt)
                            dve.tensor_scalar(neg[:, j % 2, :], ring[:, n % RING, :], 0.0, None, ALU.is_lt).then_inc(masked, 1)
                            if j >= 1:
                                dve.wait_ge(summed, j)
                            dve.tensor_tensor(rowsum[:, :], rowsum[:, :], ring[:, n % RING, :], ALU.add).then_inc(summed, 1)

                    @block.tensor
                    def _(pe):
                        for j in range(NT):
                            n = base + j
                            pe.wait_ge(cleared, j + 1)
                            for c in range(NC):
                                ins = pe.matmul(bank[c][:, :], h_rows[:, j, :], ring[:, n % RING, c * CW:(c + 1) * CW],
                                                start=(j == 0), stop=(j == NT - 1))
                            ins.then_inc(a_mm, 1)
                            pe.wait_ge(masked, j + 1)
                            for c in range(NC):
                                pe.matmul(bank[4 + c][0:19, :], uP[:, j, :], pos[:, j % 2, c * CW:(c + 1) * CW],
                                          start=(j == 0), stop=False)
                                ins = pe.matmul(bank[4 + c][0:19, :], uM[:, j, :], neg[:, j % 2, c * CW:(c + 1) * CW],
                                                start=False, stop=(j == NT - 1))
                            ins.then_inc(mask_used, 1)

                    @block.gpsimd
                    def _(pool):
                        for j in range(NT):
                            pool.wait_ge(a_mm, j + 1)
                            pool.wait_ge(summed, j + 1)
                            pool.sem_inc(a_used, 1)

                with ExitStack() as s3, nc.Block() as block:
                    eT = sb("eT", [19, N], scope=s3)
                    e_sp = sb("e_sp", [P, NT, 18], scope=s3)
                    e6 = sb("e6", [P, NT, 6], scope=s3)
                    top = sb("top", [P, NT, 3], scope=s3)
                    top3 = sb("top3", [P, 4], scope=s3)
                    best = sb("best", [3, 4], scope=s3)
                    best_d = sb("best_d", [3, 3], scope=s3)
                    shift = sb("shift", [P, 3], scope=s3)
                    gpart = sb("gpart", [P, 3, NT, 6], BF16, s3)
                    grest = sb("grest", [P, NT, 6], scope=s3)
                    dblk = sb("dblk", [P, NT, P], scope=s3)
                    e_copied, e_turned, e_step, m_turned, m_best, m_diag, m_spread, g_ready, d_ready, d_done = (
                        sem(k, s3) for k in ("e_copied", "e_turned", "e_step", "m_turned", "m_best", "m_diag", "m_spread", "g_ready", "d_ready", "d_done"))

                    @block.scalar
                    def _(act):
                        for c in range(NC):
                            act.copy(chunk(eT, c), bank[4 + c][0:19, :]).then_inc(e_copied, 1)
                        for c in range(NC):
                            act.copy(chunk(support, c), bank[c][:, :])
                        act.wait_ge(g_ready, 1)
                        act.activation(g[:, :, :], e6[:, :, :], ACT.Exp).then_inc(g_ready, 1)
                        for c in range(NC):
                            act.wait_ge(d_done, c + 1)
                            act.copy(chunk(diag_b, c), bank[4 + c][:, :])

                    @block.tensor
                    def _(pe):
                        pe.wait_ge(e_copied, NC)
                        for i in range(NT):
                            ins = pe.transpose(bank[4][:, 18 * i:18 * i + 18], eT[0:18, i * P:(i + 1) * P], ident[0:18, 0:18])
                        ins.then_inc(e_turned, 1)
                        pe.wait_ge(m_turned, 1)
                        pe.transpose(bank[5][0:3, 0:P], top3[:, 0:3], ident[:, :]).then_inc(m_turned, 1)
                        pe.wait_ge(m_diag, 1)
                        pe.matmul(bank[6][:, 0:3], ones[0:3, :], best_d[:, :], start=True, stop=True).then_inc(m_spread, 1)
                        pe.wait_ge(d_ready, 1)
                        pe.wait_ge(g_ready, 1)
                        for c in range(NC):
                            pe.matmul(bank[4 + c][:, :], ones[:, :], dblk[:, 4 * c:4 * c + 4, :].rearrange("p t d -> p (t d)"),
                                      start=True, stop=True).then_inc(d_done, 1)

                    @block.vector
                    def _(dve):
                        link = Chain(dve, e_step)
                        for j in range(NT):
                            ins = dve.tensor_scalar(dblk[:, j, :], ident[:, :], diag_col[:, j:j + 1], None, ALU.mult)
                        ins.then_inc(d_ready, 1)
                        dve.wait_ge(e_turned, 1)
                        link(dve.tensor_copy(e_sp[:, :, :].rearrange("p t s -> p (t s)"), bank[4][:, 0:NT * 18]))
                        link(dve.tensor_tensor(e6[:, :, :], e_sp[:, :, 12:18], e_sp[:, :, 6:12], ALU.add))
                        link(dve.tensor_tensor(e6[:, :, :], e6[:, :, :], e_sp[:, :, 0:6], ALU.add))
                        link(dve.scalar_tensor_tensor(out=e6[:, :, :], in0=e6[:, :, :], scalar=0.2, in1=e6[:, :, :],
                                                      op0=ALU.mult, op1=ALU.max))
                        link(dve.tensor_tensor(top[:, :, :], e6[:, :, 0:3], e6[:, :, 3:6], ALU.max))
                        dve.tensor_reduce(top3[:, 0:3], top[:, :, :].rearrange("p t k -> p k t"), AX, ALU.max).then_inc(m_turned, 1)
                        dve.wait_ge(m_turned, 2)
                        dve.tensor_reduce(best[:, 0:1], bank[5][0:3, 0:P], AX, ALU.max).then_inc(m_best, 1)
                        dve.wait_ge(m_best, 1)
                        dve.tensor_scalar(best_d[:, :], ident[0:3, 0:3], best[:, 0:1], None, ALU.mult).then_inc(m_diag, 1)
                        dve.wait_ge(m_spread, 1)
                        link(dve.tensor_scalar(shift[:, :], bank[6][:, 0:3], 60.0, None, ALU.subtract))
                        for k in range(6):
                            ins = dve.tensor_scalar(e6[:, :, k], e6[:, :, k], shift[:, k % 3:k % 3 + 1], None, ALU.subtract)
                        ins.then_inc(g_ready, 1)
                        dve.wait_ge(g_ready, 2)
                        link(dve.tensor_copy(gpart[:, 0, :, :], g[:, :, :]))
                        link(dve.tensor_tensor(grest[:, :, :], g[:, :, :], gpart[:, 0, :, :], ALU.subtract))
                        link(dve.tensor_copy(gpart[:, 1, :, :], grest[:, :, :]))
                        link(dve.tensor_tensor(grest[:, :, :], grest[:, :, :], gpart[:, 1, :, :], ALU.subtract))
                        link(dve.tensor_copy(gpart[:, 2, :, :], grest[:, :, :]))
                        for s in range(3):
                            for h in range(2):
                                dve.tensor_copy(g9[h][:, :, 3 * s:3 * s + 3], gpart[:, s, :, 3 * h:3 * h + 3])


            def gru(kind, source):
                with ExitStack() as s4, nc.Block() as block:
                    w_ih, w_hh = gru_w[kind]
                    b_ih, b_hh, b_sum = gru_b[kind]
                    r, z, t, o = (sb(f"{kind}_{k}", [P, 2, CW], scope=s4) for k in "rzto")
                    sig = [sem(f"{kind}_{k}", s4) for k in ("mm", "sg", "tt", "th", "ch", "free")]
                    mm, gates, pre, cand, step, free = sig

                    @block.tensor
                    def _(pe):
                        for c in range(NC):
                            b = 4 * (c % 2)
                            if c >= 2:
                                pe.wait_ge(free, c - 1)
                            for k in range(2):
                                pe.matmul(bank[b + k][:, :], tile(w_ih, k), chunk(source, c), start=True, stop=False)
                                pe.matmul(bank[b + k][:, :], tile(w_hh, k), chunk(hT, c), start=False, stop=True)
                            pe.matmul(bank[b + 2][:, :], tile(w_ih, 2), chunk(source, c), start=True, stop=True)
                            pe.matmul(bank[b + 3][:, :], tile(w_hh, 2), chunk(hT, c), start=True, stop=True).then_inc(mm, 1)

                    @block.scalar
                    def _(act):
                        for c in range(NC):
                            b = 4 * (c % 2)
                            act.wait_ge(mm, c + 1)
                            if c >= 2:
                                act.wait_ge(step, 5 * (c - 1))
                            act.activation(r[:, c % 2, :], bank[b][:, :], ACT.Sigmoid, bias=b_sum[:, 0:1])
                            act.activation(z[:, c % 2, :], bank[b + 1][:, :], ACT.Sigmoid, bias=b_sum[:, 1:2]).then_inc(gates, 1)
                            act.wait_ge(pre, 2 * (c + 1))
                            act.activation(t[:, c % 2, :], t[:, c % 2, :], ACT.Tanh, bias=b_ih[:, 2:3]).then_inc(cand, 1)

                    @block.vector
                    def _(dve):
                        link = Chain(dve, step)
                        for c in range(NC):
                            b = 4 * (c % 2)
                            tc, oc = t[:, c % 2, :], o[:, c % 2, :]
                            dve.wait_ge(gates, c + 1)
                            dve.scalar_tensor_tensor(out=tc, in0=bank[b + 3][:, :], scalar=b_hh[:, 2:3], in1=r[:, c % 2, :],
                                                     op0=ALU.add, op1=ALU.mult).then_inc(pre, 1)
                            dve.wait_ge(pre, 2 * c + 1)
                            ins = dve.tensor_tensor(tc, tc, bank[b + 2][:, :], ALU.add)
                            ins.then_inc(pre, 1)
                            dve.wait_ge(cand, c + 1)
                            link(dve.tensor_tensor(oc, chunk(hT, c), tc, ALU.subtract))
                            link(dve.tensor_tensor(oc, oc, z[:, c % 2, :], ALU.mult))
                            link(dve.tensor_tensor(oc, oc, tc, ALU.add))
                            link(dve.tensor_tensor(oc, oc, chunk(diag_b, c), ALU.mult))
                            link(dve.tensor_tensor(chunk(xT, c), chunk(xT, c), oc, ALU.add))
                            dve.sem_inc(free, 1)

            gru("edge", support)

            base = NT
            with ExitStack() as s5, nc.Block() as block:
                NB = 3
                a_part = [sb(f"a_{k}", [P, NB, CW], scope=s5) for k in ("pos", "neg")]
                a_mask = [sb(f"m_{k}", [P, NB, CW], BF16, s5) for k in ("pos", "neg")]
                G = [sb(f"G_{k}", [P, NB, HEADS * P], scope=s5) for k in ("pos", "neg")]
                pick = sb("pick", [9, HEADS, P], scope=s5)
                pick_col = sb("pick_col", [9, HEADS], scope=s5)
                den9 = sb("den9", [9, CW], scope=s5)
                num = sb("num", [P, HEADS, CW], scope=s5)
                rec = sb("rec", [P, CW], scope=s5)
                picked, parts, G_ready, used, evac, spread, den_used, dstep, finished = (
                    sem(k, s5) for k in ("picked", "parts", "G_ready", "used", "evac", "spread", "den_used", "dstep", "finished"))

                @block.sync
                def _(sp):
                    issue_a(sp, base + NT)

                @block.vector
                def _(dve):
                    link = Chain(dve, dstep)
                    for k in range(HEADS):
                        link(dve.tensor_reduce(pick_col[:, k:k + 1], ident[0:9, k:9:3], AX, ALU.add))
                        dve.tensor_scalar(pick[:, k, :], ones[0:9, :], pick_col[:, k:k + 1], float(HEADS),
                                          ALU.mult, ALU.mult).then_inc(picked, 1)

                    def finish(q):
                        b = 4 * (q % 2)
                        for k in range(HEADS):
                            dve.wait_ge(spread, HEADS * q + k + 1)
                            link(dve.tensor_scalar(rec[:, :], bank[b + k][:, :], 1e-37, None, ALU.max))
                            dve.sem_inc(den_used, 1)
                            link(dve.reciprocal(rec[:, :], rec[:, :]))
                            if k == 0:
                                link(dve.tensor_tensor(chunk(support, q), num[:, k, :], rec[:, :], ALU.mult))
                            else:
                                link(dve.tensor_tensor(rec[:, :], num[:, k, :], rec[:, :], ALU.mult))
                                link(dve.tensor_tensor(chunk(support, q), chunk(support, q), rec[:, :], ALU.add))
                        dve.sem_inc(finished, 1)

                    it = 0
                    for q in range(NC):
                        for j in range(NT):
                            n = base + 4 * q + j // 4
                            a = ring[:, n % RING, (j % 4) * CW:(j % 4 + 1) * CW]
                            if j % 4 == 0:
                                wait_a(dve, n)
                            if j // 4 == q:
                                blk = a[:, (j % 4) * P:(j % 4 + 1) * P]
                                link(dve.tensor_tensor(blk, blk, off_diag[:, :], ALU.mult))
                            if it >= NB:
                                dve.wait_ge(used, it - NB + 1)
                            s = it % NB
                            dve.tensor_scalar(a_part[0][:, s, :], a, 0.0, None, ALU.max)
                            dve.tensor_scalar(a_part[1][:, s, :], a, 0.0, None, ALU.min)
                            dve.tensor_scalar(a_mask[0][:, s, :], a, 0.0, None, ALU.is_gt)
                            ins = dve.tensor_scalar(a_mask[1][:, s, :], a, 0.0, None, ALU.is_lt)
                            ins.then_inc(parts, 1)
                            it += 1
                            if j % 4 == 3:
                                dve.wait_ge(parts, it)
                                dve.sem_inc(a_used, 1)
                            if q >= 1 and j == 5:
                                finish(q - 1)
                    finish(NC - 1)

                @block.scalar
                def _(act):
                    def drain(q):
                        act.wait_ge(used, NT * (q + 1))
                        if q >= 1:
                            act.wait_ge(finished, q)
                        b = 4 * (q % 2)
                        act.copy(den9[:, :], bank[b + 3][0:9, :])
                        for k in range(HEADS):
                            ins = act.copy(num[:, k, :], bank[b + k][:, :])
                        ins.then_inc(evac, 1)
                    it = 0
                    for q in range(NC):
                        for j in range(NT):
                            if it >= NB:
                                act.wait_ge(used, it - NB + 1)
                            for h in range(2):
                                for k in range(HEADS):
                                    ins = act.mul(G[h][:, it % NB, k * P:(k + 1) * P], hW[:, j, k * P:(k + 1) * P],
                                                  g[:, j, 3 * h + k:3 * h + k + 1])
                            ins.then_inc(G_ready, 1)
                            it += 1
                            if q >= 1 and j == 1:
                                drain(q - 1)
                    drain(NC - 1)

                @block.tensor
                def _(pe):
                    def spread_den(q):
                        b = 4 * (q % 2)
                        pe.wait_ge(evac, q + 1)
                        for k in range(HEADS):
                            pe.matmul(bank[b + k][:, :], pick[:, k, :], den9[:, :], start=True, stop=True).then_inc(spread, 1)
                    pe.wait_ge(picked, HEADS)
                    it = 0
                    for q in range(NC):
                        b = 4 * (q % 2)
                        if q >= 2:
                            pe.wait_ge(den_used, HEADS * (q - 1))
                        for j in range(NT):
                            s = it % NB
                            pe.wait_ge(G_ready, it + 1)
                            pe.wait_ge(parts, it + 1)
                            for h in range(2):
                                for k in range(HEADS):
                                    pe.matmul(bank[b + k][:, :], G[h][:, s, k * P:(k + 1) * P], a_part[h][:, s, :],
                                              start=(j == 0 and h == 0), stop=(j == NT - 1 and h == 1))
                                ins = pe.matmul(bank[b + 3][0:9, :], g9[h][:, j, :], a_mask[h][:, s, :],
                                                start=(j == 0 and h == 0), stop=(j == NT - 1 and h == 1))
                            ins.then_inc(used, 1)
                            it += 1
                            if q >= 1 and j == 3:
                                spread_den(q - 1)
                    spread_den(NC - 1)

            gru("node", support)
        clear_retired()
        E, F, C = 8, 512, 320
        FT = F // P
        SLOTS = E * C
        ST = SLOTS // P
        parts_of_c = [(0, P), (P, P), (2 * P, C - 2 * P)]
        h_scat = nc.dram_tensor("h_scat", (SLOTS + N, P), F32, kind="Internal").ap()
        y_slots = nc.dram_tensor("y_slots", (SLOTS, P), F32, kind="Internal").ap()

        with ExitStack() as m0:
            gate_w = sb("gate_w", [P, E], scope=m0)
            gate_b = sb("gate_b", [P, NT, E], scope=m0)
            b2_row = sb("b2_row", [1, E * P], scope=m0)
            zero = sb("zero", [P, ST * P], scope=m0)
            gl, zeroed, zset = sem("gl", m0), sem("zeroed", m0), sem("zset", m0)
            rank_down = sb("rank_down", [P, NT, E], scope=m0)
            token = sb("token", [P, NT], scope=m0)
            keep_w = sb("keep_w", [P, NT], scope=m0)
            slot_s = sb("slot_s", [P, NT], I32, m0)
            slot_g = sb("slot_g", [P, NT], I32, m0)

            def moe_loads(sp):
                sp.dma_start(gate_w[:, :], io["gate_w"]).then_inc(gl, 16)
                sp.dma_start(gate_b[:, :, :], io["gate_b"]).then_inc(gl, 16)
                sp.dma_start(b2_row[:, :], io["moe_b2"]).then_inc(gl, 16)
                sp.wait_ge(gl, 48)

            layer_norm("l0f", moe_loads)

            with ExitStack() as s1, nc.Block() as block:
                h_rows = sb("moe_h_rows", [P, NT, P], scope=s1)
                lg, ex, score, oh, cum, pre_a, pre_b = (sb(f"moe_{k}", [P, NT, E], scope=s1)
                                                        for k in ("lg", "ex", "score", "oh", "cum", "pre_a", "pre_b"))
                mx, best_e, den, pos_t, kept, t1, t2 = (sb(f"moe_{k}", [P, NT], scope=s1)
                                                        for k in ("mx", "best_e", "den", "pos_t", "kept", "t1", "t2"))
                iota_e = sb("iota_e", [P, NT, E], I32, s1)
                iota_t = sb("iota_t", [P, NT], I32, s1)
                cst, h_turned, h_copied, lg_done, ex_in, ex_out, step, oh_ready, cum_done, slots_ready = (
                    sem(f"moe_{k}", s1) for k in ("cst", "h_turned", "h_copied", "lg_done", "ex_in", "ex_out", "step",
                                                  "oh_ready", "cum_done", "slots_ready"))
                sent = sem("moe_sent")

                @block.tensor
                def _(pe):
                    for i in range(NT):
                        ins = pe.matmul(bank[4][:, E * i:E * i + E], tile(hT, i), gate_w[:, :], start=True, stop=True)
                    ins.then_inc(lg_done, 1)
                    for i in range(NT):
                        ins = pe.transpose(bank[i // 4][:, (i % 4) * P:(i % 4 + 1) * P], tile(hT, i), ident[:, :])
                        if i % 4 == 3:
                            ins.then_inc(h_turned, 1)
                    pe.wait_ge(oh_ready, 1)
                    pe.wait_ge(cst, 5)
                    flat = oh[:, :, :].rearrange("p t e -> p (t e)")
                    pe.matmul(bank[5][:, 0:P], tri[:, :], flat, start=True, stop=True)
                    pe.matmul(bank[6][:, 0:P], ones[:, :], flat, start=True, stop=True).then_inc(cum_done, 1)

                @block.scalar
                def _(act):
                    for q in range(4):
                        act.wait_ge(h_turned, q + 1)
                        act.copy(h_rows[:, 4 * q:4 * q + 4, :].rearrange("p t d -> p (t d)"), bank[q][:, :]).then_inc(h_copied, 1)
                    act.wait_ge(ex_in, 1)
                    act.activation(ex[:, :, :], ex[:, :, :], ACT.Exp).then_inc(ex_out, 1)

                @block.vector
                def _(dve):
                    link = Chain(dve, step)

                    def over_e(t):
                        return t[:, :].unsqueeze(2).broadcast_to([P, NT, E])
                    dve.wait_ge(cst, 5)
                    dve.tensor_copy(rank_down[:, :, :], iota_e[:, :, :])
                    link(dve.tensor_copy(token[:, :], iota_t[:, :]))
                    dve.wait_ge(lg_done, 1)
                    link(dve.tensor_tensor(lg[:, :, :], bank[4][:, 0:P].rearrange("p (t e) -> p t e", e=E), gate_b[:, :, :], ALU.add))
                    link(dve.tensor_reduce(mx[:, :], lg[:, :, :], AX, ALU.max))
                    dve.tensor_tensor(ex[:, :, :], lg[:, :, :], over_e(mx), ALU.subtract).then_inc(ex_in, 1)
                    link(dve.tensor_tensor(score[:, :, :], lg[:, :, :], over_e(mx), ALU.is_equal))
                    link(dve.tensor_tensor(score[:, :, :], score[:, :, :], rank_down[:, :, :], ALU.mult))
                    link(dve.tensor_reduce(best_e[:, :], score[:, :, :], AX, ALU.max))
                    dve.tensor_tensor(oh[:, :, :], score[:, :, :], over_e(best_e), ALU.is_equal).then_inc(oh_ready, 1)
                    dve.wait_ge(ex_out, 1)
                    link(dve.tensor_reduce(den[:, :], ex[:, :, :], AX, ALU.add))
                    link(dve.reciprocal(den[:, :], den[:, :]))
                    dve.wait_ge(cum_done, 1)
                    link(dve.tensor_copy(pre_a[:, :, :].rearrange("p t e -> p (t e)"), bank[6][:, 0:P]))
                    src, dst = pre_a, pre_b
                    for sft in (1, 2, 4, 8):
                        dve.tensor_copy(dst[:, 0:sft, :], src[:, 0:sft, :])
                        link(dve.tensor_tensor(dst[:, sft:, :], src[:, sft:, :], src[:, :NT - sft, :], ALU.add))
                        src, dst = dst, src
                    link(dve.tensor_tensor(cum[:, :, :].rearrange("p t e -> p (t e)"), src[:, :, :].rearrange("p t e -> p (t e)"),
                                           bank[6][:, 0:P], ALU.subtract))
                    link(dve.tensor_tensor(cum[:, :, :].rearrange("p t e -> p (t e)"), cum[:, :, :].rearrange("p t e -> p (t e)"),
                                           bank[5][:, 0:P], ALU.add))
                    link(dve.tensor_tensor(cum[:, :, :], cum[:, :, :], oh[:, :, :], ALU.mult))
                    link(dve.tensor_reduce(pos_t[:, :], cum[:, :, :], AX, ALU.add))
                    link(dve.tensor_scalar(pos_t[:, :], pos_t[:, :], 1.0, None, ALU.subtract))
                    link(dve.tensor_scalar(kept[:, :], pos_t[:, :], float(C), None, ALU.is_lt))
                    dve.tensor_tensor(keep_w[:, :], den[:, :], kept[:, :], ALU.mult)
                    link(dve.tensor_scalar(t1[:, :], best_e[:, :], -float(C), float(E * C), ALU.mult, ALU.add))
                    link(dve.scalar_tensor_tensor(out=t2[:, :], in0=pos_t[:, :], scalar=float(C - 1), in1=t1[:, :],
                                                  op0=ALU.min, op1=ALU.add))
                    dve.tensor_copy(slot_g[:, :], t2[:, :])
                    link(dve.tensor_tensor(t1[:, :], t1[:, :], pos_t[:, :], ALU.add))
                    link(dve.tensor_tensor(t1[:, :], t1[:, :], token[:, :], ALU.subtract))
                    link(dve.tensor_tensor(t1[:, :], t1[:, :], kept[:, :], ALU.mult))
                    link(dve.tensor_tensor(t1[:, :], t1[:, :], token[:, :], ALU.add))
                    dve.tensor_copy(slot_s[:, :], t1[:, :]).then_inc(slots_ready, 1)

                @block.gpsimd
                def _(pool):
                    pool.memset(zero[:, :], 0.0).then_inc(zset, 1)
                    pool.memset(tri[:, :], 1.0).then_inc(cst, 1)
                    pool.iota(iota_e[:, :, :], [[0, NT], [-1, E]], base=E, channel_multiplier=0).then_inc(cst, 1)
                    pool.iota(iota_t[:, :], [[P, NT]], base=SLOTS, channel_multiplier=1).then_inc(cst, 1)
                    pool.wait_ge(cst, 3)
                    pool.affine_select(out=tri[:, :], in_=tri[:, :], compare_op=ALU.is_ge, fill=0.0,
                                       base=0, pattern=[[1, P]], channel_multiplier=-1).then_inc(cst, 2)
                    pool.wait_ge(zeroed, 16)
                    pool.wait_ge(h_copied, 4)
                    pool.wait_ge(slots_ready, 1)
                    for i in range(NT):
                        pool.indirect_dma_start(h_scat[:, :], bass.IndirectOffsetOnAxis(ap=slot_s[:, i:i + 1], axis=0),
                                                h_rows[:, i, :], None).then_inc(sent, 16)
                    pool.wait_ge(sent, 16 * NT)

                @block.sync
                def _(sp):
                    sp.wait_ge(zset, 1)
                    sp.dma_start(h_scat[0:SLOTS, :].rearrange("(s p) d -> p s d", p=P),
                                 zero[:, :].rearrange("p (s d) -> p s d", s=ST)).then_inc(zeroed, 16)
                    sp.wait_ge(zeroed, 16)

            with ExitStack() as s2, nc.Block() as block:
                EW = FT * P * 2 + FT
                slot_rows = sb("slot_rows", [P, ST, P], scope=s2)
                slotT = sb("slotT", [P, SLOTS], scope=s2)
                ew = sb("ew", [P, 2, EW], scope=s2)
                mid = sb("mid", [P, 2, FT, C], scope=s2)
                y_sb = sb("y_sb", [P, 2, 3, P], scope=s2)
                rows_in, turned, turned_copied, mid_mm, mid_act, y_mm, y_cp = (
                    sem(f"exp_{k}", s2) for k in ("rows_in", "turned", "turned_copied", "mid_mm", "mid_act", "y_mm", "y_cp"))
                ew_in = [sem(f"ew_in{u}", s2) for u in range(2)]
                y_out = [sem(f"y_out{u}", s2) for u in range(2)]

                def store(sp, e):
                    sp.wait_ge(y_cp, 3 * (e + 1))
                    for s, (at, m) in enumerate(parts_of_c):
                        sp.dma_start(y_slots[e * C + at:e * C + at + m, :], y_sb[0:m, e % 2, s, :]).then_inc(y_out[e % 2], 16)

                @block.sync
                def _(sp):
                    sp.dma_start(slot_rows[:, :, :], h_scat[0:SLOTS, :].rearrange("(s p) d -> p s d", p=P)).then_inc(rows_in, 16)
                    for e in range(E):
                        u = e % 2
                        if e >= 2:
                            sp.wait_ge(y_mm, 3 * (e - 1))
                        sp.dma_start(ew[:, u, :], io["moe_w"][e]).then_inc(ew_in[u], 16)
                        if e >= 1:
                            store(sp, e - 1)
                    store(sp, E - 1)
                    for u in range(2):
                        sp.wait_ge(y_out[u], 16 * 3 * E // 2)

                @block.tensor
                def _(pe):
                    pe.wait_ge(rows_in, 16)
                    for i in range(ST):
                        if i // 4 >= 4 and i % 4 == 0:
                            pe.wait_ge(turned_copied, i // 4 - 3)
                        ins = pe.transpose(bank[i // 4 % 4][:, (i % 4) * P:(i % 4 + 1) * P], slot_rows[:, i, :], ident[:, :])
                        if i % 4 == 3:
                            ins.then_inc(turned, 1)
                    pe.wait_ge(turned_copied, ST // 4)
                    for e in range(E):
                        u = e % 2
                        pe.wait_ge(ew_in[u], 16 * (e // 2 + 1))
                        for f in range(FT):
                            if e >= 1:
                                pe.wait_ge(mid_act, FT * (e - 1) + f + 1)
                            pe.matmul(bank[f][:, 0:C], ew[:, u, f * P:(f + 1) * P], slotT[:, e * C:(e + 1) * C],
                                      start=True, stop=True).then_inc(mid_mm, 1)
                        pe.wait_ge(mid_act, FT * (e + 1))
                        for s, (at, m) in enumerate(parts_of_c):
                            if e >= 1:
                                pe.wait_ge(y_cp, 3 * (e - 1) + s + 1)
                            pe.matmul(bank[4 + s][0:m, 0:P], ones[0:1, 0:m], b2_row[:, e * P:(e + 1) * P], start=True, stop=False)
                            for f in range(FT):
                                ins = pe.matmul(bank[4 + s][0:m, 0:P], mid[:, u, f, at:at + m], ew[:, u, F + f * P:F + (f + 1) * P],
                                                start=False, stop=(f == FT - 1))
                            ins.then_inc(y_mm, 1)

                @block.scalar
                def _(act):
                    for e in range(E):
                        for f in range(FT):
                            act.wait_ge(mid_mm, FT * e + f + 1)
                            if e >= 2:
                                act.wait_ge(y_mm, 3 * (e - 1))
                            act.activation(mid[:, e % 2, f, :], bank[f][:, 0:C], ACT.Relu,
                                           bias=ew[:, e % 2, 2 * F + f:2 * F + f + 1]).then_inc(mid_act, 1)

                @block.vector
                def _(dve):
                    for q in range(ST // 4):
                        dve.wait_ge(turned, q + 1)
                        dve.tensor_copy(chunk(slotT, q), bank[q % 4][:, :]).then_inc(turned_copied, 1)
                    for e in range(E):
                        for s, (at, m) in enumerate(parts_of_c):
                            dve.wait_ge(y_mm, 3 * e + s + 1)
                            if e >= 2:
                                dve.wait_ge(y_out[e % 2], 16 * 3 * (e // 2))
                            dve.tensor_copy(y_sb[0:m, e % 2, s, :], bank[4 + s][0:m, 0:P]).then_inc(y_cp, 1)

            with ExitStack() as s3, nc.Block() as block:
                got = sb("got", [P, NT, P], scope=s3)
                clean = sb("clean", [P, NT, P], scope=s3)
                mask = sb("nan_mask", [P, NT, P], scope=s3)
                big = sb("big", [P, 4 * P], scope=s3)
                small_v = sb("small_v", [P, 4 * P], scope=s3)
                fetched = [sem(f"fetched{q}") for q in range(4)]
                cset, step, cleaned, turned = (sem(f"comb_{k}", s3) for k in ("cset", "step", "cleaned", "turned"))

                @block.gpsimd
                def _(pool):
                    pool.memset(clean[:, :, :], 0.0).then_inc(cset, 1)
                    pool.memset(big[:, :], 10000.0).then_inc(cset, 1)
                    pool.memset(small_v[:, :], -10000.0).then_inc(cset, 1)
                    for i in range(NT):
                        pool.indirect_dma_start(got[:, i, :], None, y_slots[:, :],
                                                bass.IndirectOffsetOnAxis(ap=slot_g[:, i:i + 1], axis=0)).then_inc(fetched[i // 4], 16)

                @block.vector
                def _(dve):
                    link = Chain(dve, step)
                    dve.wait_ge(cset, 3)
                    for q in range(4):
                        def four(t, dt=F32):
                            return t[:, 4 * q:4 * q + 4, :].rearrange("p t d -> p (t d)")
                        dve.wait_ge(fetched[q], 64)
                        for i in range(4 * q, 4 * q + 4):
                            ins = dve.tensor_scalar(got[:, i, :], got[:, i, :], keep_w[:, i:i + 1], None, ALU.mult)
                        link(ins)
                        link(dve.tensor_tensor(four(mask), four(got), four(got), ALU.is_equal))
                        link(dve.copy_predicated(four(clean), four(mask).bitcast(I32), four(got)))
                        link(dve.tensor_scalar(four(mask), four(clean), 3.4028234e38, None, ALU.is_gt))
                        link(dve.copy_predicated(four(clean), four(mask).bitcast(I32), big[:, :]))
                        link(dve.tensor_scalar(four(mask), four(clean), -3.4028234e38, None, ALU.is_lt))
                        dve.copy_predicated(four(clean), four(mask).bitcast(I32), small_v[:, :]).then_inc(cleaned, 1)
                    for q in range(4):
                        dve.wait_ge(turned, q + 1)
                        dve.tensor_tensor(chunk(xT, q), chunk(xT, q), bank[q][:, :], ALU.add)

                @block.tensor
                def _(pe):
                    for q in range(4):
                        pe.wait_ge(cleaned, q + 1)
                        for i in range(4 * q, 4 * q + 4):
                            ins = pe.transpose(bank[q][:, (i % 4) * P:(i % 4 + 1) * P], clean[:, i, :], ident[:, :])
                        ins.then_inc(turned, 1)

        clear_retired()
        dinv = {}

        def gcn(tag, base, w_name, b_name=None, extra=None):
            with ExitStack() as g0:
                w = sb(f"w_{tag}", [P, P], scope=g0)
                bias = sb(f"b_{tag}", [P, 1], scope=g0)
                dcol = sb(f"dcol_{tag}", [P, NT], scope=g0)
                d_blk = sb(f"d_blk_{tag}", [P, NT, P], scope=g0)
                d_b = sb(f"d_b_{tag}", [P, N], scope=g0)
                Z = sb(f"Z_{tag}", [P, NT, P], scope=g0)
                wl = sem(f"wl_{tag}", g0)

                def loads(sp):
                    sp.dma_start(w[:, :], io[w_name]).then_inc(wl, 16)
                    if b_name:
                        sp.dma_start(bias[:, :], io[b_name]).then_inc(wl, 16)
                    sp.wait_ge(wl, 32 if b_name else 16)
                    issue_a(sp, base + RING)
                layer_norm(tag, loads)
                with ExitStack() as s1, nc.Block() as block:
                    deg_done, step, root, placed, spread, d_copied, z_mm, z_cp, a_mm, out_t, scaled = (
                        sem(f"{tag}_{k}", s1) for k in ("deg_done", "step", "root", "placed", "spread", "d_copied",
                                                        "z_mm", "z_cp", "a_mm", "out_t", "scaled"))

                    @block.sync
                    def _(sp):
                        issue_a(sp, base + NT)

                    @block.tensor
                    def _(pe):
                        if extra is not None:
                            for i in range(NT):
                                ins = pe.matmul(bank[7][:, i:i + 1], tile(rowsum, i), ones[:, 0:1], start=True, stop=True)
                            ins.then_inc(deg_done, 1)
                        for i in range(NT):
                            ins = pe.matmul(bank[i // 4][:, (i % 4) * P:(i % 4 + 1) * P], tile(hT, i), w[:, :], start=True, stop=True)
                            if i % 4 == 3:
                                ins.then_inc(z_mm, 1)
                        if extra is not None:
                            for c in range(NC):
                                pe.wait_ge(placed, c + 1)
                                b = 4 + c % 2
                                if c >= 2:
                                    pe.wait_ge(d_copied, c - 1)
                                pe.matmul(bank[b][:, :], ones[:, :], d_blk[:, 4 * c:4 * c + 4, :].rearrange("p t d -> p (t d)"),
                                          start=True, stop=True).then_inc(spread, 1)
                        pe.wait_ge(z_cp, 4)
                        if extra:
                            pe.wait_ge(scaled, NC)
                        for j in range(NT):
                            n = base + j
                            wait_a(pe, n)
                            for c in range(NC):
                                ins = pe.matmul(bank[c][:, :], Z[:, j, :], ring[:, n % RING, c * CW:(c + 1) * CW],
                                                start=(j == 0), stop=(j == NT - 1 and not extra))
                            ins.then_inc(a_used, 1)
                        if extra:
                            for c in range(NC):
                                pe.matmul(bank[c][:, :], w[:, :], chunk(hT, c), start=False, stop=True).then_inc(a_mm, 1)

                    @block.scalar
                    def _(act):
                        if extra is not None:
                            act.wait_ge(step, 2)
                            act.activation(dcol[:, :], dcol[:, :], ACT.Sqrt).then_inc(root, 1)
                            for c in range(NC):
                                act.wait_ge(spread, c + 1)
                                act.copy(chunk(d_b, c), bank[4 + c % 2][:, :]).then_inc(d_copied, 1)
                            if b_name:
                                for c in range(NC):
                                    act.wait_ge(out_t, c + 1)
                                    act.activation(chunk(hT, c), chunk(hT, c), ACT.Relu, bias=bias[:, 0:1]).then_inc(root, 1)
                        else:
                            for c in range(NC):
                                act.wait_ge(a_used, base + NT)
                                act.activation(chunk(hT, c), bank[c][:, :], ACT.Relu, bias=bias[:, 0:1]).then_inc(root, 1)

                    @block.vector
                    def _(dve):
                        link = Chain(dve, step)
                        if extra is not None:
                            dve.wait_ge(deg_done, 1)
                            link(dve.tensor_tensor(dcol[:, :], bank[7][:, 0:NT], diag_col[:, :], ALU.add))
                            link(dve.tensor_scalar(dcol[:, :], dcol[:, :], extra, None, ALU.add))
                            dve.wait_ge(root, 1)
                            link(dve.reciprocal(dcol[:, :], dcol[:, :]))
                            for i in range(NT):
                                ins = dve.tensor_scalar(d_blk[:, i, :], ident[:, :], dcol[:, i:i + 1], None, ALU.mult)
                                if i % 4 == 3:
                                    ins.then_inc(placed, 1)
                        for q in range(4):
                            dve.wait_ge(z_mm, q + 1)
                            for i in range(4 * q, 4 * q + 4):
                                src = bank[q][:, (i % 4) * P:(i % 4 + 1) * P]
                                if extra is None:
                                    ins = dve.tensor_copy(Z[:, i, :], src)
                                else:
                                    ins = dve.tensor_scalar(Z[:, i, :], src, dcol[:, i:i + 1], None, ALU.mult)
                            ins.then_inc(z_cp, 1)
                        if extra:
                            for c in range(NC):
                                dve.wait_ge(d_copied, c + 1)
                                dve.tensor_tensor(chunk(hT, c), chunk(hT, c), chunk(d_b, c), ALU.mult).then_inc(scaled, 1)
                        for c in range(NC):
                            if extra is None:
                                dve.wait_ge(root, c + 1)
                                dve.tensor_tensor(chunk(xT, c), chunk(xT, c), chunk(hT, c), ALU.add)
                                continue
                            if extra:
                                dve.wait_ge(a_mm, c + 1)
                            else:
                                dve.wait_ge(a_used, base + NT)
                            if c == 0:
                                dve.wait_ge(d_copied, NC)
                            ins = dve.tensor_tensor(chunk(hT, c), bank[c][:, :], chunk(d_b, c), ALU.mult)
                            if b_name:
                                ins.then_inc(out_t, 1)
                                dve.wait_ge(root, c + 2)
                                dve.tensor_tensor(chunk(xT, c), chunk(xT, c), chunk(hT, c), ALU.add)
                            else:
                                link(ins)
                                dve.scalar_tensor_tensor(out=chunk(xT, c), in0=chunk(hT, c), scalar=0.0, in1=chunk(xT, c),
                                                         op0=ALU.max, op1=ALU.add)

        gcn("l1g", 2 * NT, "l1_W", None, 0.0)
        clear_retired()
        LEVELS = 8
        NODES = 2 ** LEVELS - 1
        LEAVES = 2 ** (LEVELS - 1)
        RW = 144
        PAIRS = [(NT + 2 ** l - 1 + 3) // 4 * 4 for l in range(LEVELS)]
        OFF = [sum(PAIRS[:l]) for l in range(LEVELS)]
        NP = sum(PAIRS)
        WR = 8
        assert NP % WR == 0
        t_sorted = nc.dram_tensor("t_sorted", (N, RW), F32, kind="Internal").ap()
        o_sorted = nc.dram_tensor("o_sorted", (N, P), F32, kind="Internal").ap()

        def level(t, l):
            return t[:, :, 2 ** l - 1:2 ** (l + 1) - 1]

        with ExitStack() as f0:
            w1T = sb("fff_w1T", [P, NODES], scope=f0)
            b1 = sb("fff_b1", [1, NODES], scope=f0)
            b2 = [sb("fff_b2a", [P, P], scope=f0), sb("fff_b2b", [NODES - P, P], scope=f0)]
            rank = sb("rank", [P, NT], I32, f0)
            wnT = [sb("wnT0", [P, N], scope=f0), sb("wnT1", [P, N], scope=f0)]
            fl = sem("fff_fl", f0)

            def fff_loads(sp):
                sp.dma_start(w1T[:, :], io["fff_w1T"]).then_inc(fl, 16)
                sp.dma_start(b1[:, :], io["fff_b1"]).then_inc(fl, 16)
                sp.dma_start(b2[0][:, :], io["fff_b2"][0:P, :]).then_inc(fl, 16)
                sp.dma_start(b2[1][:, :], io["fff_b2"][P:NODES, :]).then_inc(fl, 16)
                sp.wait_ge(fl, 64)
            layer_norm("l1f", fff_loads)

            with ExitStack() as s1, nc.Block() as block:
                on = sb("on_path", [P, NT, NODES], scope=s1)
                score = sb("fff_score", [P, NT, NODES], scope=s1)
                right = sb("go_right", [P, NT, NODES], scope=s1)
                rows = sb("fff_rows", [P, NT, RW], scope=s1)
                logit, alog, pw = (sb(f"fff_{k}", [P, NT, LEVELS], scope=s1) for k in ("logit", "alog", "pw"))
                leaf_i = sb("leaf_i", [P, LEAVES], I32, s1)
                leaf_f = sb("leaf_f", [P, LEAVES], scope=s1)
                before_a, before_b = (sb(f"before_{k}", [P, NT, LEAVES], scope=s1) for k in "ab")
                leaf_sum = sb("leaf_sum", [P, LEAVES], scope=s1)
                rank_f = sb("rank_f", [P, NT], scope=s1)
                s_mm, s_cp, h_turned, h_copied, step, path_done, g_in, g_out, cnt_done, w_set, wn_turned, wn_cp, iota_set, rank_set, tot_cp = (
                    sem(f"fff_{k}", s1) for k in ("s_mm", "s_cp", "h_turned", "h_copied", "step", "path_done", "g_in", "g_out",
                                                  "cnt_done", "w_set", "wn_turned", "wn_cp", "iota_set", "rank_set", "tot_cp"))
                sent = sem("fff_sent")

                @block.tensor
                def _(pe):
                    for i in range(NT):
                        out = bank[i // 2][:, (i % 2) * 256:(i % 2) * 256 + NODES]
                        pe.matmul(out, ones[0:1, :], b1[:, :], start=True, stop=False)
                        ins = pe.matmul(out, tile(hT, i), w1T[:, :], start=False, stop=True)
                        if i % 2:
                            ins.then_inc(s_mm, 1)
                    for q in range(4):
                        pe.wait_ge(s_cp, q + 1)
                        for i in range(4 * q, 4 * q + 4):
                            ins = pe.transpose(bank[q][:, (i % 4) * P:(i % 4 + 1) * P], tile(hT, i), ident[:, :])
                        ins.then_inc(h_turned, 1)
                    pe.wait_ge(path_done, 1)
                    pe.wait_ge(h_copied, 4)
                    pe.wait_ge(s_cp, NT // 2)
                    for c in range(4):
                        oh = level(on, LEVELS - 1)[:, 4 * c:4 * c + 4, :]
                        pe.matmul(bank[c][:, :].rearrange("p (t n) -> p t n", t=4), tri[:, :], oh, start=True, stop=True)
                        pe.matmul(bank[4 + c][:, :].rearrange("p (t n) -> p t n", t=4), ones[:, :], oh, start=True, stop=True)\
                          .then_inc(cnt_done, 1)
                    pe.wait_ge(w_set, 1)
                    pe.wait_ge(tot_cp, 1)
                    g = 0
                    for c in range(4):
                        for half, m in ((0, P), (1, NODES - P)):
                            if g >= 4:
                                pe.wait_ge(wn_cp, g - 3)
                            for i in range(4 * c, 4 * c + 4):
                                ins = pe.transpose(bank[4 + g % 4][0:m, (i % 4) * P:(i % 4 + 1) * P],
                                                   score[:, i, half * P:half * P + m], ident[:, :])
                            ins.then_inc(wn_turned, 1)
                            g += 1

                @block.scalar
                def _(act):
                    for q in range(4):
                        act.wait_ge(h_turned, q + 1)
                        act.copy(rows[:, 4 * q:4 * q + 4, 0:P], bank[q][:, :].rearrange("p (t d) -> p t d", t=4)).then_inc(h_copied, 1)
                    act.wait_ge(g_in, 1)
                    act.activation(pw[:, :, :], alog[:, :, :], ACT.Gelu).then_inc(g_out, 1)
                    g = 0
                    for c in range(4):
                        for half, m in ((0, P), (1, NODES - P)):
                            act.wait_ge(wn_turned, g + 1)
                            act.copy(wnT[half][0:m, c * CW:(c + 1) * CW], bank[4 + g % 4][0:m, :]).then_inc(wn_cp, 1)
                            g += 1

                @block.vector
                def _(dve):
                    link = Chain(dve, step)
                    for b in range(NT // 2):
                        dve.wait_ge(s_mm, b + 1)
                        dve.tensor_copy(score[:, 2 * b:2 * b + 2, :], bank[b][:, :].rearrange("p (t n) -> p t n", t=2)[:, :, 0:NODES])\
                           .then_inc(s_cp, 1)
                    dve.wait_ge(s_cp, NT // 2)
                    dve.memset(on[:, :, 0:1], 1.0)
                    link(dve.tensor_scalar(right[:, :, :], score[:, :, :], 0.0, None, ALU.is_gt))
                    for l in range(LEVELS - 1):
                        kids = level(on, l + 1).rearrange("p t (n s) -> p t n s", s=2)
                        link(dve.tensor_tensor(kids[:, :, :, 1], level(on, l), level(right, l), ALU.mult))
                        link(dve.tensor_tensor(kids[:, :, :, 0], level(on, l), kids[:, :, :, 1], ALU.subtract))
                    dve.sem_inc(path_done, 1)
                    link(dve.tensor_tensor(score[:, :, :], score[:, :, :], on[:, :, :], ALU.mult))
                    for l in range(LEVELS):
                        ins = dve.tensor_reduce(logit[:, :, l], level(score, l), AX, ALU.add)
                    link(ins)
                    dve.scalar_tensor_tensor(out=alog[:, :, :], in0=logit[:, :, :], scalar=-1.0, in1=logit[:, :, :],
                                             op0=ALU.mult, op1=ALU.max).then_inc(g_in, 1)
                    dve.wait_ge(iota_set, 2)
                    link(dve.tensor_copy(leaf_f[:, :], leaf_i[:, :]))
                    link(dve.tensor_tensor(before_a[:, :, :], level(on, LEVELS - 1),
                                           leaf_f[:, :].unsqueeze(1).broadcast_to([P, NT, LEAVES]), ALU.mult))
                    link(dve.tensor_reduce(rows[:, :, P + LEVELS], before_a[:, :, :], AX, ALU.add))
                    for c in range(4):
                        dve.wait_ge(cnt_done, c + 1)
                        ins = dve.tensor_copy(before_a[:, 4 * c:4 * c + 4, :], bank[4 + c][:, :].rearrange("p (t n) -> p t n", t=4))
                    link(ins)
                    src, dst = before_a, before_b
                    for sft in (1, 2, 4, 8):
                        dve.tensor_copy(dst[:, 0:sft, :], src[:, 0:sft, :])
                        link(dve.tensor_tensor(dst[:, sft:, :], src[:, sft:, :], src[:, :NT - sft, :], ALU.add))
                        src, dst = dst, src
                    link(dve.tensor_tensor_scan(leaf_sum[:, :], ones[:, :], src[:, NT - 1, :], 0.0, ALU.mult, ALU.add))
                    link(dve.tensor_tensor(leaf_sum[:, :], leaf_sum[:, :], src[:, NT - 1, :], ALU.subtract))
                    for c in range(4):
                        v = src[:, 4 * c:4 * c + 4, :]
                        link(dve.tensor_tensor(v, v, bank[4 + c][:, :].rearrange("p (t n) -> p t n", t=4), ALU.subtract))
                        ins = dve.tensor_tensor(v, v, bank[c][:, :].rearrange("p (t n) -> p t n", t=4), ALU.add)
                        link(ins)
                    dve.sem_inc(tot_cp, 1)
                    link(dve.tensor_tensor(src[:, :, :], src[:, :, :], leaf_sum[:, :].unsqueeze(1).broadcast_to([P, NT, LEAVES]), ALU.add))
                    link(dve.tensor_tensor(src[:, :, :], src[:, :, :], level(on, LEVELS - 1), ALU.mult))
                    link(dve.tensor_reduce(rank_f[:, :], src[:, :, :], AX, ALU.add))
                    dve.wait_ge(g_out, 1)
                    dve.tensor_copy(rows[:, :, P:P + LEVELS], pw[:, :, :])
                    dve.memset(rows[:, :, P + LEVELS + 1:RW], 0.0)
                    dve.tensor_scalar(rank[:, :], rank_f[:, :], 1.0, None, ALU.subtract).then_inc(rank_set, 1)
                    for l in range(LEVELS):
                        ins = dve.tensor_tensor(level(score, l), level(on, l),
                                                pw[:, :, l:l + 1].broadcast_to([P, NT, 2 ** l]), ALU.mult)
                    ins.then_inc(w_set, 1)

                @block.gpsimd
                def _(pool):
                    pool.iota(leaf_i[:, :], [[1, LEAVES]], base=0, channel_multiplier=0).then_inc(iota_set, 2)
                    pool.wait_ge(h_copied, 4)
                    pool.wait_ge(rank_set, 1)
                    for i in range(NT):
                        pool.indirect_dma_start(t_sorted[:, :], bass.IndirectOffsetOnAxis(ap=rank[:, i:i + 1], axis=0),
                                                rows[:, i, :], None).then_inc(sent, 16)
                    pool.wait_ge(sent, 16 * NT)

            f1 = f0.enter_context(ExitStack())
            scaled = sb("scaled", [P, LEVELS, N], scope=f1)
            node = sb("node", [P, LEVELS, N], BF16, f1)
            nrel = sb("nrel", [P, NP], scope=f1)
            col_x = sb("col_x", [1, NP], I32, f1)
            col_o = sb("col_o", [1, NP], I32, f1)
            n_abs = sb("n_abs", [1, NP], I32, f1)
            with ExitStack() as s2, nc.Block() as block:
                srt = sb("srt", [P, NT, RW], scope=s2)
                xsT = hT
                leaf_b = ring[:, 0, :].bitcast(I32)
                shifted = ring[:, 1:3, :].bitcast(I32)
                auxT = ring[0:9, 3, :]
                sel = sb("sel", [9, 9, P], scope=s2)
                leaf_t = sb("leaf_t", [NT, LEVELS + 1], scope=s2)
                reach_i = sb("reach_i", [NT, NP], I32, s2)
                reach = sb("reach", [NT, NP], scope=s2)
                skip0 = sb("skip0", [NT, P], scope=s2)
                pair_i = sb("pair_i", [P, NP], I32, s2)
                pair_f = sb("pair_f", [P, NP], scope=s2)
                add_x = sb("add_x", [1, NP], I32, s2)
                add_n = sb("add_n", [1, NP], I32, s2)
                tmp = sb("tab_tmp", [1, NP], scope=s2)
                t128 = sb("t128", [1, NP], scope=s2)
                rows_in, leaf_in, turned, aux_turned, cp, aux_cp, io_set, step, reach_set, tile_mm, spread, used_b, sh_set, sh_used, leaf_set = (
                    sem(f"srt_{k}", s2) for k in ("rows_in", "leaf_in", "turned", "aux_turned", "cp", "aux_cp", "io_set", "step", "reach_set",
                                                  "tile_mm", "spread", "used_b", "sh_set", "sh_used", "leaf_set"))

                @block.sync
                def _(sp):
                    sp.dma_start(leaf_t[:, :], t_sorted.rearrange("(t p) c -> t p c", p=P)[:, 0, P:P + LEVELS + 1]).then_inc(leaf_in, 16)
                    sp.dma_start(srt[:, :, :], t_sorted.rearrange("(t p) c -> p t c", p=P)).then_inc(rows_in, 16)
                    sp.wait_ge(rows_in, 16)

                @block.gpsimd
                def _(pool):
                    for l in range(LEVELS):
                        w = LEAVES >> l
                        at = slice(OFF[l], OFF[l] + PAIRS[l])
                        pool.iota(reach_i[:, at], [[w, PAIRS[l]]], base=w - 1, channel_multiplier=-w).then_inc(io_set, 1)
                        pool.iota(pair_i[:, at], [[1, PAIRS[l]]], base=0, channel_multiplier=0).then_inc(io_set, 1)
                        pool.iota(add_x[:, at], [[0, PAIRS[l]]], base=l * N, channel_multiplier=0).then_inc(io_set, 1)
                        pool.iota(add_n[:, at], [[0, PAIRS[l]]], base=2 ** l - 1, channel_multiplier=0).then_inc(io_set, 1)

                @block.tensor
                def _(pe):
                    pe.wait_ge(rows_in, 16)
                    for i in range(NT):
                        ins = pe.transpose(bank[i // 4][:, (i % 4) * P:(i % 4 + 1) * P], srt[:, i, 0:P], ident[:, :])
                        if i % 4 == 3:
                            ins.then_inc(turned, 1)
                        ins = pe.transpose(bank[4 + i // 4][0:9, (i % 4) * P:(i % 4 + 1) * P], srt[:, i, P:P + 9], ident[:, :])
                        if i % 4 == 3:
                            ins.then_inc(aux_turned, 1)
                    pe.wait_ge(reach_set, 1)
                    pe.wait_ge(cp, 1)
                    pe.matmul(bank[0][:, 0:NP], skip0[:, :], reach[:, :], start=True, stop=True).then_inc(tile_mm, 1)
                    pe.wait_ge(aux_cp, 4)
                    pe.wait_ge(io_set, 4 * LEVELS + 1)
                    for g in range(4 * 9):
                        l = 8 if g < 4 else g // 4 - 1
                        if g >= 4:
                            pe.wait_ge(used_b, g - 3)
                        pe.matmul(bank[4 + g % 4][:, :], sel[:, l, :], auxT[:, (g % 4) * CW:(g % 4 + 1) * CW],
                                  start=True, stop=True).then_inc(spread, 1)

                @block.scalar
                def _(act):
                    for q in range(4):
                        act.wait_ge(turned, q + 1)
                        act.copy(chunk(xsT, q), bank[q][:, :]).then_inc(cp, 1)
                        act.wait_ge(aux_turned, q + 1)
                        act.copy(auxT[:, q * CW:(q + 1) * CW], bank[4 + q][0:9, :]).then_inc(aux_cp, 1)
                    for l in range(LEVELS):
                        act.wait_ge(sh_set, min(l + 1, LEVELS - 1))
                        src = leaf_b[:, :] if l == LEVELS - 1 else shifted[:, l % 2, :]
                        act.copy(node[:, l, :], src).then_inc(sh_used, 1)

                @block.vector
                def _(dve):
                    link = Chain(dve, step)
                    for k in range(9):
                        ins = dve.tensor_scalar(sel[:, k, :], ones[0:9, :], ident[0:9, k:k + 1], None, ALU.mult)
                    ins.then_inc(io_set, 1)
                    link(dve.tensor_scalar(skip0[:, :], ones[0:NT, :], ident[0:NT, 0:1], None, ALU.subtract))
                    dve.wait_ge(leaf_in, 16)
                    dve.wait_ge(io_set, 4 * LEVELS + 1)
                    dve.tensor_scalar(reach[:, :], reach_i[:, :], leaf_t[:, LEVELS:LEVELS + 1], None, ALU.is_ge).then_inc(reach_set, 1)
                    link(dve.tensor_copy(pair_f[:, :], pair_i[:, :]))
                    dve.wait_ge(tile_mm, 1)
                    link(dve.tensor_tensor(nrel[:, :], pair_f[:, :], bank[0][:, 0:NP], ALU.subtract))
                    link(dve.tensor_scalar(t128[:, :], bank[0][0:1, 0:NP], float(P), None, ALU.mult))
                    dve.tensor_copy(col_o[:, :], t128[:, :])
                    dve.tensor_tensor(col_x[:, :], t128[:, :], add_x[:, :], ALU.add)
                    link(dve.tensor_tensor(tmp[:, :], nrel[0:1, :], add_n[:, :], ALU.add))
                    link(dve.tensor_scalar(n_abs[:, :], tmp[:, :], float(NODES - 1), None, ALU.min))
                    for q in range(4):
                        dve.wait_ge(spread, q + 1)
                        dve.tensor_copy(chunk(leaf_b, q), bank[4 + q][:, :]).then_inc(used_b, 1)
                    dve.wait_ge(used_b, 4)
                    dve.wait_ge(cp, 4)
                    for l in range(LEVELS):
                        if l < LEVELS - 1:
                            if l >= 2:
                                dve.wait_ge(sh_used, l - 1)
                            dve.tensor_scalar(shifted[:, l % 2, :], leaf_b[:, :], LEVELS - 1 - l, None, ALU.logical_shift_right).then_inc(sh_set, 1)
                        for q in range(4):
                            dve.wait_ge(spread, 4 * (l + 1) + q + 1)
                            dve.tensor_tensor(scaled[:, l, q * CW:(q + 1) * CW], chunk(xsT, q), bank[4 + q][:, :], ALU.mult).then_inc(used_b, 1)

            with ExitStack() as s3, nc.Block() as block:
                wt = sb("node_w", [P, WR, P], scope=s3)
                picked = sb("picked_tok", [P, WR, P], scope=s3)
                zero_w = sb("zero_w", [P, P], scope=s3)
                w_in = [sem(f"node_w_in{u}", s3) for u in range(WR)]
                pair_used, picked_set, z_set = sem("pair_used", s3), sem("picked_set", s3), sem("z_set", s3)

                @block.sync
                def _(sp):
                    with sp.Fori(0, NP // WR) as i:
                        for u in range(WR):
                            n = sp.value_load(n_abs[0:1, bass.ds(i * WR + u, 1)], min_val=0, max_val=NODES - 1)
                            sp.wait_ge(pair_used, i * WR + u + 1)
                            sp.dma_start(wt[:, u, :], io["fff_w2"][bass.ds(n, 1), :, :].rearrange("a d o -> (a d) o")).then_inc(w_in[u], 16)

                @block.vector
                def _(dve):
                    dve.memset(zero_w[:, :], 0.0).then_inc(z_set, 1)
                    with dve.Fori(0, NP // WR) as i:
                        for u in range(WR):
                            x = dve.value_load(col_x[0:1, bass.ds(i * WR + u, 1)], min_val=0, max_val=LEVELS * N - P)
                            dve.wait_ge(pair_used, i * WR + u + 1)
                            dve.scalar_tensor_tensor(out=picked[:, u, :], in0=node[:, :, :].rearrange("p l t -> p (l t)")[:, bass.ds(x, P)],
                                                     scalar=nrel[:, bass.ds(i * WR + u, 1)],
                                                     in1=scaled[:, :, :].rearrange("p l t -> p (l t)")[:, bass.ds(x, P)],
                                                     op0=ALU.is_equal, op1=ALU.mult).then_inc(picked_set, 1)

                @block.tensor
                def _(pe):
                    pe.wait_ge(z_set, 1)
                    for c in range(4):
                        ins = pe.matmul(bank[c][:, :], zero_w[:, :], scaled[:, 0, c * CW:(c + 1) * CW], start=True, stop=False)
                    ins.then_inc(pair_used, WR)
                    with pe.Fori(0, NP // WR) as i:
                        for u in range(WR):
                            o = pe.value_load(col_o[0:1, bass.ds(i * WR + u, 1)], min_val=0, max_val=N - P)
                            pe.wait_ge(w_in[u], i * 16 + 16)
                            pe.wait_ge(picked_set, i * WR + u + 1)
                            pe.matmul(psum[:, bass.ds(o, P)], wt[:, u, :], picked[:, u, :], start=False, stop=False,
                                      skip_group_check=True).then_inc(pair_used, 1)
                    for c in range(4):
                        pe.matmul(bank[c][:, :], zero_w[:, :], scaled[:, 0, c * CW:(c + 1) * CW], start=False, stop=True)
            f1.close()

            with ExitStack() as s4, nc.Block() as block:
                oT = sb("oT", [P, N], scope=s4)
                o_rows = sb("o_rows", [P, NT, P], scope=s4)
                back = sb("back", [P, NT, P], scope=s4)
                o_cp, o_turned, o_rcp, o_out, x_mm = (sem(f"unsort_{k}", s4) for k in ("o_cp", "o_turned", "o_rcp", "o_out", "x_mm"))
                fetched = [sem(f"unsort_in{q}") for q in range(4)]

                @block.scalar
                def _(act):
                    for c in range(4):
                        act.copy(chunk(oT, c), bank[c][:, :]).then_inc(o_cp, 1)

                @block.tensor
                def _(pe):
                    for c in range(4):
                        pe.wait_ge(o_cp, c + 1)
                        for i in range(4 * c, 4 * c + 4):
                            ins = pe.transpose(bank[4 + c][:, (i % 4) * P:(i % 4 + 1) * P], tile(oT, i), ident[:, :])
                        ins.then_inc(o_turned, 1)
                    for c in range(4):
                        pe.matmul(bank[c][:, :], b2[0][:, :], chunk(wnT[0], c), start=True, stop=False)
                        pe.matmul(bank[c][:, :], b2[1][:, :], wnT[1][0:NODES - P, c * CW:(c + 1) * CW], start=False, stop=False)
                        pe.wait_ge(fetched[c], 64)
                        for i in range(4 * c, 4 * c + 4):
                            ins = pe.matmul(bank[c][:, (i % 4) * P:(i % 4 + 1) * P], back[:, i, :], ident[:, :], start=False, stop=(i % 4 == 3))
                        ins.then_inc(x_mm, 1)

                @block.vector
                def _(dve):
                    for c in range(4):
                        dve.wait_ge(o_turned, c + 1)
                        dve.tensor_copy(o_rows[:, 4 * c:4 * c + 4, :].rearrange("p t d -> p (t d)"), bank[4 + c][:, :]).then_inc(o_rcp, 1)
                    for c in range(4):
                        dve.wait_ge(x_mm, c + 1)
                        dve.tensor_tensor(chunk(xT, c), chunk(xT, c), bank[c][:, :], ALU.add)

                @block.sync
                def _(sp):
                    sp.wait_ge(o_rcp, 4)
                    sp.dma_start(o_sorted.rearrange("(t p) d -> p t d", p=P), o_rows[:, :, :]).then_inc(o_out, 16)
                    sp.wait_ge(o_out, 16)

                @block.gpsimd
                def _(pool):
                    pool.wait_ge(o_out, 16)
                    for i in range(NT):
                        pool.indirect_dma_start(back[:, i, :], None, o_sorted[:, :],
                                                bass.IndirectOffsetOnAxis(ap=rank[:, i:i + 1], axis=0)).then_inc(fetched[i // 4], 16)

        clear_retired()
        gcn("l2g", 3 * NT, "l2_W", "l2_b", None)
        clear_retired()

        with ExitStack() as e0:
            BN_EPS = 0.001
            ew = sb("l2_ew", [P, E, 3 * P], scope=e0)
            bn = sb("l2_bn", [P, 10, E], scope=e0)
            wr = sb("l2_wr", [P, E], scope=e0)
            br = sb("l2_br", [P, NT, E], scope=e0)
            bo = sb("l2_bo", [E, P], scope=e0)
            scale_c = [sb(f"l2_scale{k}", [P, E], scope=e0) for k in range(2)]
            shift_c = [sb(f"l2_shift{k}", [P, E], scope=e0) for k in range(2)]
            bn_eps = sb("bn_eps", [P, 1], scope=e0)
            el = sem("l2_el", e0)

            def l2_loads(sp):
                for t, k in ((wr, "l2_Wr"), (br, "l2_br"), (bo, "l2_bo"), (bn, "l2_bn"), (ew, "l2_ew")):
                    sp.dma_start(t[tuple(slice(None) for _ in t.shape)], io[k]).then_inc(el, 16)
                sp.wait_ge(el, 80)
            layer_norm("l2f", l2_loads)

            with ExitStack() as s1, nc.Block() as block:
                lg, ex, wgt = (sb(f"l2_{k}", [P, NT, E], scope=s1) for k in ("lg", "ex", "wgt"))
                mx, den = (sb(f"l2_{k}", [P, NT], scope=s1) for k in ("mx", "den"))
                wT = sb("l2_wT", [E, N], scope=s1)
                h1 = sb("l2_h1", [P, 2, CW], scope=s1)
                h2 = sb("l2_h2", [P, 2, CW], scope=s1)
                acc = sb("l2_acc", [P, NT, P], scope=s1)
                root = [sb(f"l2_root{k}", [P, E], scope=s1) for k in range(2)]
                eps_set, lg_done, ex_in, ex_out, step, root_set, aff_set, mm1, mm2, mm3, ac1, ac2, acc_used, w_set, w_turned, wT_set, out_mm, acc_done = (
                    sem(f"l2_{k}", s1) for k in ("eps_set", "lg_done", "ex_in", "ex_out", "step", "root_set", "aff_set", "mm1", "mm2", "mm3",
                                                 "ac1", "ac2", "acc_used", "w_set", "w_turned", "wT_set", "out_mm", "acc_done"))
                ITS = E * NC

                @block.gpsimd
                def _(pool):
                    pool.memset(bn_eps[:, :], BN_EPS).then_inc(eps_set, 1)

                @block.tensor
                def _(pe):
                    for i in range(NT):
                        ins = pe.matmul(bank[6][:, E * i:E * i + E], tile(hT, i), wr[:, :], start=True, stop=True)
                    ins.then_inc(lg_done, 1)

                    def first(it):
                        e, c = it // NC, it % NC
                        if it >= 2:
                            pe.wait_ge(ac1, it - 1)
                        pe.matmul(bank[it % 2][:, :], ew[:, e, 0:P], chunk(hT, c), start=True, stop=True).then_inc(mm1, 1)

                    def second(it):
                        pe.wait_ge(ac1, it + 1)
                        if it >= 2:
                            pe.wait_ge(ac2, it - 1)
                        pe.matmul(bank[2 + it % 2][:, :], ew[:, it // NC, P:2 * P], h1[:, it % 2, :], start=True, stop=True).then_inc(mm2, 1)

                    def third(it):
                        pe.wait_ge(ac2, it + 1)
                        if it >= 2:
                            pe.wait_ge(acc_used, it - 1)
                        for i in range(4):
                            ins = pe.matmul(bank[4 + it % 2][:, i * P:(i + 1) * P], h2[:, it % 2, i * P:(i + 1) * P],
                                            ew[:, it // NC, 2 * P:3 * P], start=True, stop=True)
                        ins.then_inc(mm3, 1)
                    for it in range(ITS + 2):
                        if it < ITS:
                            first(it)
                        if 1 <= it <= ITS:
                            second(it - 1)
                        if it >= 2:
                            third(it - 2)
                    pe.wait_ge(w_set, 1)
                    for i in range(NT):
                        if i == 8:
                            pe.wait_ge(wT_set, 1)
                        if i % 4 == 0 and i >= 8:
                            pe.wait_ge(wT_set, i // 4 - 1)
                        ins = pe.transpose(bank[6 + i // 4 % 2][0:E, (i % 4) * P:(i % 4 + 1) * P], wgt[:, i, :], ident[:, :])
                        if i % 4 == 3:
                            ins.then_inc(w_turned, 1)
                    pe.wait_ge(wT_set, 4)
                    pe.wait_ge(acc_done, 1)
                    for c in range(NC):
                        pe.matmul(bank[c][:, :], bo[:, :], wT[:, c * CW:(c + 1) * CW], start=True, stop=False)
                        for i in range(4):
                            ins = pe.matmul(bank[c][:, i * P:(i + 1) * P], acc[:, 4 * c + i, :], ident[:, :], start=False, stop=(i == 3))
                        ins.then_inc(out_mm, 1)

                @block.scalar
                def _(act):
                    act.wait_ge(eps_set, 1)
                    for k in range(2):
                        act.activation(root[k][:, :], bn[:, 5 * k + 4, :], ACT.Sqrt, bias=bn_eps[:, 0:1]).then_inc(root_set, 1)
                    act.wait_ge(ex_in, 1)
                    act.activation(ex[:, :, :], ex[:, :, :], ACT.Exp).then_inc(ex_out, 1)
                    act.wait_ge(aff_set, 2)
                    for it in range(ITS + 1):
                        if it < ITS:
                            e = it // NC
                            act.wait_ge(mm1, it + 1)
                            if it >= 2:
                                act.wait_ge(mm2, it - 1)
                            act.activation(h1[:, it % 2, :], bank[it % 2][:, :], ACT.Relu,
                                           bias=shift_c[0][:, e:e + 1], scale=scale_c[0][:, e:e + 1]).then_inc(ac1, 1)
                        if it >= 1:
                            e = (it - 1) // NC
                            act.wait_ge(mm2, it)
                            if it >= 3:
                                act.wait_ge(mm3, it - 2)
                            act.activation(h2[:, (it - 1) % 2, :], bank[2 + (it - 1) % 2][:, :], ACT.Relu,
                                           bias=shift_c[1][:, e:e + 1], scale=scale_c[1][:, e:e + 1]).then_inc(ac2, 1)
                    for q in range(4):
                        act.wait_ge(w_turned, q + 1)
                        act.copy(wT[:, q * CW:(q + 1) * CW], bank[6 + q % 2][0:E, :]).then_inc(wT_set, 1)

                @block.vector
                def _(dve):
                    link = Chain(dve, step)

                    def over_e(t):
                        return t[:, :].unsqueeze(2).broadcast_to([P, NT, E])
                    dve.wait_ge(lg_done, 1)
                    link(dve.tensor_tensor(lg[:, :, :], bank[6][:, 0:P].rearrange("p (t e) -> p t e", e=E), br[:, :, :], ALU.add))
                    link(dve.tensor_reduce(mx[:, :], lg[:, :, :], AX, ALU.max))
                    dve.tensor_tensor(ex[:, :, :], lg[:, :, :], over_e(mx), ALU.subtract).then_inc(ex_in, 1)
                    dve.wait_ge(root_set, 2)
                    for k in range(2):
                        b, g_, be, m = (bn[:, 5 * k + i, :] for i in range(4))
                        link(dve.reciprocal(root[k][:, :], root[k][:, :]))
                        link(dve.tensor_tensor(scale_c[k][:, :], root[k][:, :], g_, ALU.mult))
                        link(dve.tensor_tensor(shift_c[k][:, :], b, m, ALU.subtract))
                        link(dve.tensor_tensor(shift_c[k][:, :], shift_c[k][:, :], scale_c[k][:, :], ALU.mult))
                        dve.tensor_tensor(shift_c[k][:, :], shift_c[k][:, :], be, ALU.add).then_inc(aff_set, 1)
                    dve.wait_ge(ex_out, 1)
                    link(dve.tensor_reduce(den[:, :], ex[:, :, :], AX, ALU.add))
                    link(dve.reciprocal(den[:, :], den[:, :]))
                    dve.tensor_tensor(wgt[:, :, :], ex[:, :, :], over_e(den), ALU.mult).then_inc(w_set, 1)
                    dve.wait_ge(w_set, 1)
                    for it in range(ITS):
                        e, c = it // NC, it % NC
                        dve.wait_ge(mm3, it + 1)
                        if e >= 1:
                            dve.wait_ge(acc_used, it - NC + 1)
                        for i in range(4):
                            t = 4 * c + i
                            src = bank[4 + it % 2][:, i * P:(i + 1) * P]
                            if e == 0:
                                ins = dve.tensor_scalar(acc[:, t, :], src, wgt[:, t, e:e + 1], None, ALU.mult)
                            else:
                                ins = dve.scalar_tensor_tensor(out=acc[:, t, :], in0=src, scalar=wgt[:, t, e:e + 1], in1=acc[:, t, :],
                                                               op0=ALU.mult, op1=ALU.add)
                        ins.then_inc(acc_used, 1)
                    dve.wait_ge(acc_used, ITS)
                    dve.sem_inc(acc_done, 1)
                    for c in range(NC):
                        dve.wait_ge(out_mm, c + 1)
                        dve.tensor_tensor(chunk(xT, c), chunk(xT, c), bank[c][:, :], ALU.add)
        clear_retired()

        gcn("l3g", 4 * NT, "l3_W", "l3_b", 1.0)
        clear_retired()

        H8, KEYS, TOP = 8, 128, 16
        DK = P // 2
        INV_SQRT = float(P) ** -0.5
        with ExitStack() as p0:
            half_w = sb("half_w", [DK, H8 * 2, P], scope=p0)
            half_k = sb("half_k", [DK, H8 * 2, KEYS], scope=p0)
            key_map = sb("key_map", [P, H8 + 1, 2 * KEYS], scope=p0)
            wq = sb("wq", [P, P], scope=p0)
            wo = sb("wo", [P, H8, P], scope=p0)
            qT = sb("qT", [P, N], scope=p0)
            kT = sb("kT", [P, N], scope=p0)
            kv = sb("kv", [P, NT, 2 * P], scope=p0)
            prob = sb("prob", [P, N], scope=p0)
            probT = sb("probT", [P, NT, P], scope=p0)
            yacc = sb("yacc", [P, NT, P], scope=p0)
            rows = sb("table_rows", [P, 2, TOP, 2 * P], scope=p0)
            causal = sb("causal", [P, P], scope=p0)
            iota16_i = sb("iota16_i", [P, 16], I32, p0)
            iota16 = sb("iota16", [P, 16], BF16, p0)
            pl = sem("pk_loaded", p0)

            def pk_loads(sp):
                sp.dma_start(half_w[:, :, :], io["pk_w"]).then_inc(pl, 16)
                sp.dma_start(half_k[:, :, :], io["pk_k"]).then_inc(pl, 16)
                sp.dma_start(wo[:, :, :], io["pk_wo"]).then_inc(pl, 16)
                sp.wait_ge(pl, 48)
            layer_norm("l3f", pk_loads)

            with ExitStack() as s1, nc.Block() as block:
                map_mm, map_cp, c_set = (sem(f"pk_{k}", s1) for k in ("map_mm", "map_cp", "c_set"))

                @block.tensor
                def _(pe):
                    for k in range(2 * H8):
                        ins = pe.matmul(bank[k // 4][:, (k % 4) * P:(k % 4 + 1) * P], half_w[:, k, :], half_k[:, k, :], start=True, stop=True)
                        if k % 4 == 3:
                            ins.then_inc(map_mm, 1)

                @block.scalar
                def _(act):
                    for q in range(4):
                        act.wait_ge(map_mm, q + 1)
                        act.copy(key_map[:, 2 * q:2 * q + 2, :].rearrange("p h k -> p (h k)"), bank[q][:, :]).then_inc(map_cp, 1)
                    act.copy(key_map[:, H8, :], bank[0][:, 0:2 * KEYS])

                @block.gpsimd
                def _(pool):
                    pool.memset(yacc[:, :, :], 0.0)
                    pool.memset(causal[:, :], 0.0).then_inc(c_set, 1)
                    pool.iota(iota16_i[:, :], [[1, 16]], base=0, channel_multiplier=0).then_inc(c_set, 1)
                    pool.wait_ge(c_set, 2)
                    pool.affine_select(out=causal[:, :], in_=causal[:, :], compare_op=ALU.is_ge, fill=-1e30,
                                       base=0, pattern=[[-1, P]], channel_multiplier=1)

                @block.vector
                def _(dve):
                    dve.wait_ge(c_set, 2)
                    dve.tensor_copy(iota16[:, :], iota16_i[:, :])

            with ExitStack() as s2, nc.Block() as block:
                sims = sb("sims", [P, 2 * KEYS], scope=s2)
                rest = sb("sims_rest", [P, 2 * KEYS], scope=s2)
                top = sb("top16", [P, 2, TOP], scope=s2)
                top_i = sb("top16_i", [P, 2, TOP], mybir.dt.uint32, s2)
                tab = sb("pick_tab", [P, 2, TOP], BF16, s2)
                pair = sb("pair_score", [P, TOP, TOP], scope=s2)
                pair_rest = sb("pair_rest", [P, TOP * TOP], scope=s2)
                best = sb("best16", [P, TOP], scope=s2)
                best_i = sb("best16_i", [P, TOP], mybir.dt.uint32, s2)
                ij_i = sb("ij_i", [P, 2, TOP], mybir.dt.uint32, s2)
                ij = sb("ij", [P, 2, TOP], BF16, s2)
                hot = sb("hot", [P, TOP, 2, TOP], BF16, s2)
                row_f = sb("row_f", [P, TOP], scope=s2)
                head_base = sb("head_base", [P, 1], scope=s2)
                neg_top = sb("neg_top", [P, 1], scope=s2)
                e16 = sb("e16", [P, TOP], scope=s2)
                e_sum = sb("e_sum", [P, 1], scope=s2)
                w16 = sb("w16", [P, 2, TOP], scope=s2)
                row_i = sb("row_i", [P, 2, TOP], I32, s2)
                s_diag = sb("s_diag", [P, P], scope=s2)
                m2 = sb("m2", [P, 2], scope=s2)
                neg_m = sb("neg_m", [P, 1], scope=s2)
                r2 = sb("r2", [P, 2], scope=s2)
                r1 = sb("r1", [P, 1], scope=s2)
                oT = sb("attn_oT", [P, P], scope=s2)
                names = ("sim_mm", "sim_cp", "sim_read", "tk_in", "tk_out", "idx_ready", "ws_done", "wq_in", "q_mm", "q_cp",
                         "kt_mm", "kt_cp", "s_mm", "mx", "exd", "tr_mm", "pt_cp", "pv", "o_cp", "y_mm", "y_acc", "dstep", "act_step")
                S = {k: sem("at_" + k, s2) for k in names}
                rows_in = [sem(f"rows_in{u}") for u in range(2)]

                def banks_of(t):
                    return t // 4 + 1
                BANKS = sum(banks_of(t) for t in range(NT))

                def banks_before(t):
                    return sum(banks_of(k) for k in range(t))

                @block.sync
                def _(sp):
                    with sp.Fori(0, H8) as h:
                        sp.wait_ge(S["q_mm"], h * 4 + 4)
                        sp.dma_start(wq[:, :], io["pk_wq"][bass.ds(h, 1), :, :].rearrange("a d o -> (a d) o")).then_inc(S["wq_in"], 16)

                @block.gpsimd
                def _(pool):
                    with pool.Fori(0, H8) as h:
                        for t in range(NT):
                            pool.wait_ge(S["idx_ready"], h * NT + t + 1)
                            pool.wait_ge(S["ws_done"], h * NT + t + 1)
                            pool.nop(nofuse=True)
                            for k in range(TOP):
                                pool.indirect_dma_start(rows[:, t % 2, k, :], None, io["tables"],
                                                        bass.IndirectOffsetOnAxis(ap=row_i[:, t % 2, k:k + 1], axis=0)).then_inc(rows_in[t % 2], 16)

                @block.tensor
                def _(pe):
                    def sim(t, head, n):
                        pe.wait_ge(S["sim_cp"], n + 1)
                        pe.matmul(bank[4][:, 0:2 * KEYS], tile(hT, t), key_map[:, bass.ds(head, 1), :].rearrange("p a k -> p (a k)"),
                                  start=True, stop=True).then_inc(S["sim_mm"], 1)

                    def attend(h, t, ahead):
                        g = h * NT + t
                        pe.wait_ge(S["ws_done"], g + 3)
                        pe.wait_ge(S["y_acc"], g + 1)
                        pe.transpose(bank[7][:, 0:P], kv[:, t, 0:P], ident[:, :]).then_inc(S["kt_mm"], 1)
                        pe.wait_ge(S["kt_cp"], g + 1)
                        for b in range(banks_of(t)):
                            w = min(CW, (t + 1) * P - b * CW)
                            ins = pe.matmul(bank[b][:, 0:w], tile(qT, t), kT[:, b * CW:b * CW + w], start=True, stop=True)
                        ins.then_inc(S["s_mm"], 1)
                        if ahead:
                            sim(*ahead)
                        pe.wait_ge(S["exd"], g + 1)
                        for b in range(banks_of(t)):
                            k = banks_before(t) + b
                            pe.wait_ge(S["pt_cp"], h * BANKS + k + 1)
                            for j in range(4 * b, min(4 * b + 4, t + 1)):
                                ins = pe.transpose(bank[5 + k % 2][:, (j % 4) * P:(j % 4 + 1) * P], tile(prob, j), ident[:, :])
                            ins.then_inc(S["tr_mm"], 1)
                        pe.wait_ge(S["pt_cp"], h * BANKS + banks_before(t + 1) + 2)
                        for j in range(t + 1):
                            ins = pe.matmul(bank[7][:, P:2 * P], kv[:, j, P:2 * P], probT[:, j, :], start=(j == 0), stop=(j == t))
                        ins.then_inc(S["pv"], 1)
                        pe.wait_ge(S["o_cp"], g + 1)
                        pe.matmul(bank[7][:, 2 * P:3 * P], oT[:, :], wo[:, bass.ds(h, 1), :].rearrange("p a o -> p (a o)"),
                                  start=True, stop=True).then_inc(S["y_mm"], 1)

                    pe.sem_inc(S["q_mm"], 4)
                    sim(0, 0, 0)
                    sim(1, 0, 1)
                    with pe.Fori(0, H8) as h:
                        pe.wait_ge(S["wq_in"], h * 16 + 16)
                        for c in range(NC):
                            ins = pe.matmul(bank[c][:, :], wq[:, :], chunk(hT, c), start=True, stop=True)
                            ins.then_inc(S["q_mm"], 1)
                        sim(2, h, h * NT + 2)
                        pe.wait_ge(S["q_cp"], h * 4 + 4)
                        for t in range(NT):
                            a = t + 3
                            attend(h, t, (a % NT, h + a // NT, h * NT + a) if a < NT + 2 else None)

                @block.scalar
                def _(act):
                    def copy_sims(n):
                        act.wait_ge(S["sim_mm"], n + 1)
                        act.wait_ge(S["sim_read"], n + 1)
                        act.copy(sims[:, :], bank[4][:, 0:2 * KEYS]).then_inc(S["sim_cp"], 1)

                    def softmax16(n):
                        act.wait_ge(S["tk_in"], n + 1)
                        act.activation(e16[:, :], best[:, :], ACT.Exp, bias=neg_top[:, 0:1], accum_out=e_sum[:, 0:1]).then_inc(S["tk_out"], 1)

                    def attend(h, t, n_next):
                        g = h * NT + t
                        act.wait_ge(S["kt_mm"], g + 1)
                        act.copy(tile(kT, t), bank[7][:, 0:P]).then_inc(S["kt_cp"], 1)
                        if n_next is not None:
                            copy_sims(n_next)
                        act.wait_ge(S["mx"], g + 1)
                        if t > 0:
                            act.activation(prob[:, 0:t * P], psum[:, 0:t * P], ACT.Exp, bias=neg_m[:, 0:1], accum_out=r2[:, 0:1])
                        act.activation(tile(prob, t), s_diag[:, :], ACT.Exp, bias=neg_m[:, 0:1], accum_out=r2[:, 1:2]).then_inc(S["exd"], 1)
                        for b in range(banks_of(t)):
                            k = banks_before(t) + b
                            w = min(4, t + 1 - 4 * b)
                            act.wait_ge(S["tr_mm"], h * BANKS + k + 1)
                            act.copy(probT[:, 4 * b:4 * b + w, :].rearrange("p t d -> p (t d)"), bank[5 + k % 2][:, 0:w * P]).then_inc(S["pt_cp"], 1)
                        act.wait_ge(S["pv"], g + 1)
                        act.copy(oT[:, :], bank[7][:, P:2 * P]).then_inc(S["o_cp"], 1)
                        if n_next is not None:
                            softmax16(n_next)

                    act.sem_inc(S["sim_cp"], 1)
                    act.sem_inc(S["pt_cp"], 2)
                    copy_sims(0)
                    softmax16(0)
                    copy_sims(1)
                    softmax16(1)
                    with act.Fori(0, H8) as h:
                        for c in range(NC):
                            act.wait_ge(S["q_mm"], h * 4 + 5 + c)
                            act.mul(chunk(qT, c), bank[c][:, :], INV_SQRT).then_inc(S["q_cp"], 1)
                        copy_sims(h * NT + 2)
                        softmax16(h * NT + 2)
                        for t in range(NT):
                            attend(h, t, h * NT + t + 3 if t + 3 < NT + 2 else None)

                @block.vector
                def _(dve):
                    K = {"n": 0}

                    def link(ins):
                        K["n"] += 1
                        ins.then_inc(S["dstep"], 1)
                        dve.wait_ge(S["dstep"], K["n"])

                    def topk(par, n):
                        dve.wait_ge(S["sim_cp"], n + 2)
                        dve.nop(nofuse=True)
                        for p in range(2):
                            v, r = sims[:, p * KEYS:(p + 1) * KEYS], rest[:, p * KEYS:(p + 1) * KEYS]
                            link(dve.max(top[:, p, 0:8], v))
                            dve.max_index(top_i[:, p, 0:8], top[:, p, 0:8], v)
                            link(dve.match_replace(r, top[:, p, 0:8], v, -3.0e38))
                            link(dve.max(top[:, p, 8:16], r))
                            link(dve.max_index(top_i[:, p, 8:16], top[:, p, 8:16], r))
                        dve.sem_inc(S["sim_read"], 1)
                        dve.tensor_copy(tab[:, 0, :], top_i[:, 0, :])
                        dve.tensor_scalar(tab[:, 1, :], top_i[:, 1, :], float(KEYS), None, ALU.mult)
                        link(dve.tensor_tensor(pair[:, :, :], top[:, 0, :].unsqueeze(2).broadcast_to([P, TOP, TOP]),
                                               top[:, 1, :].unsqueeze(1).broadcast_to([P, TOP, TOP]), ALU.add))
                        flat = pair[:, :, :].rearrange("p a b -> p (a b)")
                        link(dve.max(best[:, 0:8], flat))
                        dve.max_index(best_i[:, 0:8], best[:, 0:8], flat)
                        link(dve.match_replace(pair_rest[:, :], best[:, 0:8], flat, -3.0e38))
                        link(dve.max(best[:, 8:16], pair_rest[:, :]))
                        link(dve.tensor_scalar(neg_top[:, :], best[:, 0:1], -1.0, None, ALU.mult))
                        dve.sem_inc(S["tk_in"], 1)
                        link(dve.max_index(best_i[:, 8:16], best[:, 8:16], pair_rest[:, :]))
                        dve.tensor_scalar(ij_i[:, 0, :], best_i[:, :], 4, None, ALU.logical_shift_right)
                        link(dve.tensor_scalar(ij_i[:, 1, :], best_i[:, :], TOP - 1, None, ALU.bitwise_and))
                        link(dve.tensor_copy(ij[:, :, :], ij_i[:, :, :]))
                        for s_ in range(2):
                            ins = dve.tensor_tensor(hot[:, :, s_, :], iota16[:, :].unsqueeze(1).broadcast_to([P, TOP, TOP]),
                                                    ij[:, s_, :].unsqueeze(2).broadcast_to([P, TOP, TOP]), ALU.is_equal)
                        link(ins)
                        hv = hot[:, :, :, :].rearrange("p k s i -> p k (s i)")
                        link(dve.tensor_tensor(hv, hv, tab[:, :, :].rearrange("p s i -> p (s i)").unsqueeze(1).broadcast_to([P, TOP, 2 * TOP]), ALU.mult))
                        link(dve.tensor_reduce(row_f[:, :], hv, AX, ALU.add))
                        ins = dve.tensor_scalar(row_i[:, par, :], row_f[:, :], head_base[:, 0:1], None, ALU.add)
                        ins.then_inc(S["idx_ready"], 1)

                    def weights(par, n):
                        dve.wait_ge(S["tk_out"], n + 1)
                        link(dve.reciprocal(e_sum[:, :], e_sum[:, :]))
                        link(dve.tensor_scalar(w16[:, par, :], e16[:, :], e_sum[:, 0:1], None, ALU.mult))

                    def weighted_sum(h, t):
                        dve.wait_ge(rows_in[t % 2], h * (NT // 2 * TOP * 16) + (t // 2 + 1) * TOP * 16)
                        for k in range(TOP):
                            if k == 0:
                                ins = dve.tensor_scalar(kv[:, t, :], rows[:, t % 2, k, :], w16[:, t % 2, k:k + 1], None, ALU.mult)
                            else:
                                ins = dve.scalar_tensor_tensor(out=kv[:, t, :], in0=rows[:, t % 2, k, :], scalar=w16[:, t % 2, k:k + 1],
                                                               in1=kv[:, t, :], op0=ALU.mult, op1=ALU.add)
                            if k < TOP - 1:
                                link(ins)
                        ins.then_inc(S["ws_done"], 1)

                    def row_max(h, t):
                        g = h * NT + t
                        dve.wait_ge(S["s_mm"], g + 1)
                        link(dve.tensor_tensor(s_diag[:, :], psum[:, t * P:(t + 1) * P], causal[:, :], ALU.add))
                        if t > 0:
                            dve.tensor_reduce(m2[:, 0:1], psum[:, 0:t * P], AX, ALU.max)
                        link(dve.tensor_reduce(m2[:, 1:2], s_diag[:, :], AX, ALU.max))
                        if t > 0:
                            ins = dve.tensor_scalar(neg_m[:, :], m2[:, 0:1], m2[:, 1:2], -1.0, ALU.max, ALU.mult)
                        else:
                            ins = dve.tensor_scalar(neg_m[:, :], m2[:, 1:2], -1.0, None, ALU.mult)
                        ins.then_inc(S["mx"], 1)

                    def add_out(h, t):
                        dve.wait_ge(S["y_mm"], h * NT + t + 1)
                        if t > 0:
                            link(dve.tensor_tensor(r1[:, :], r2[:, 0:1], r2[:, 1:2], ALU.add))
                            link(dve.reciprocal(r1[:, :], r1[:, :]))
                        else:
                            link(dve.reciprocal(r1[:, :], r2[:, 1:2]))
                        dve.scalar_tensor_tensor(out=yacc[:, t, :], in0=bank[7][:, 2 * P:3 * P], scalar=r1[:, 0:1], in1=yacc[:, t, :],
                                                 op0=ALU.mult, op1=ALU.add).then_inc(S["y_acc"], 1)

                    def body(h):
                        for t in range(NT):
                            if t >= 2:
                                add_out(h, t - 2)
                            weights((t + 1) % 2, h * NT + t + 1)
                            weighted_sum(h, t)
                            if t >= 1:
                                row_max(h, t - 1)
                            if t + 2 == NT:
                                link(dve.tensor_scalar(head_base[:, :], head_base[:, :], float(KEYS * KEYS), None, ALU.add))
                            topk(t % 2, h * NT + t + 2)
                        add_out(h, NT - 2)
                        row_max(h, NT - 1)
                        add_out(h, NT - 1)

                    dve.sem_inc(S["sim_read"], 1)
                    dve.sem_inc(S["ws_done"], 2)
                    dve.sem_inc(S["y_acc"], 1)
                    link(dve.memset(head_base[:, :], 0.0))
                    topk(0, 0)
                    weights(0, 0)
                    topk(1, 1)
                    with dve.Fori(0, H8) as h:
                        dve.sem_clear(S["dstep"])
                        K["n"] = 0
                        body(h)

            with ExitStack() as s3, nc.Block() as block:
                turned = sem("fin_turned", s3)

                @block.tensor
                def _(pe):
                    for i in range(NT):
                        ins = pe.transpose(bank[i // 4][:, (i % 4) * P:(i % 4 + 1) * P], yacc[:, i, :], ident[:, :])
                        if i % 4 == 3:
                            ins.then_inc(turned, 1)

                @block.vector
                def _(dve):
                    for c in range(NC):
                        dve.wait_ge(turned, c + 1)
                        dve.tensor_tensor(chunk(xT, c), chunk(xT, c), bank[c][:, :], ALU.add)

        with nc.Block() as block:
            stored = sem("stored")

            @block.sync
            def _(sp):
                sp.dma_start(io["outT"], xT[:, :]).then_inc(stored, 16)
                sp.wait_ge(stored, 16)


def layouts(np, v):
    out = {"xT": v["x"].T, "adjT": v["adj"].T}
    out["gat_W"] = v["L0_gnn_gat_W"]
    out["gat_wT"] = v["L0_gnn_gat_W"].transpose(2, 0, 1)
    out["gat_a"] = v["L0_gnn_gat_a"].reshape(3, 2, 128).transpose(2, 0, 1)
    for kind in ("edge", "node"):
        for m in ("ih", "hh"):
            out[f"{kind}_W{m}T"] = v[f"L0_gnn_{kind}_W{m}"].T
            out[f"{kind}_b{m}"] = v[f"L0_gnn_{kind}_b{m}"].reshape(3, 128).T
    E = 8
    out["gate_w"] = v["L0_ffn_gate_w"]
    out["gate_b"] = np.broadcast_to(v["L0_ffn_gate_b"], (128, 16, E))
    out["moe_w"] = np.concatenate([
        v["L0_ffn_w1"],
        v["L0_ffn_w2"].reshape(E, 4, 128, 128).transpose(0, 2, 1, 3).reshape(E, 128, 512),
        v["L0_ffn_b1"].reshape(E, 4, 128).transpose(0, 2, 1)], axis=2)
    out["moe_b2"] = v["L0_ffn_b2"].reshape(1, -1)
    out["fff_w1T"] = v["L1_ffn_w1s"].T
    out["fff_b1"] = v["L1_ffn_b1s"].reshape(1, -1)
    out["fff_b2"] = v["L1_ffn_b2s"]
    out["fff_w2"] = v["L1_ffn_w2s"]
    out["l2_W"] = v["L2_gnn_W"]
    out["l2_b"] = v["L2_gnn_b"].reshape(-1, 1)
    out["l2_Wr"] = v["L2_ffn_Wr"]
    out["l2_br"] = np.broadcast_to(v["L2_ffn_br"], (128, 16, E))
    out["l2_bo"] = v["L2_ffn_bo"]
    out["l2_bn"] = np.stack([v[f"L2_ffn_{k}{n}"].T for n in (1, 2) for k in ("b", "g", "be", "m", "v")], axis=1)
    out["l2_ew"] = np.concatenate([v["L2_ffn_W1"], v["L2_ffn_W2"], v["L2_ffn_Wo"]], axis=2).transpose(1, 0, 2)
    out["l3_W"] = v["L3_gnn_W"]
    out["l3_b"] = v["L3_gnn_b"].reshape(-1, 1)
    out["pk_w"] = v["L3_ffn_Wq_pk"].reshape(128, 2, 8, 64).transpose(3, 2, 1, 0).reshape(64, 16, 128)
    out["pk_k"] = v["L3_ffn_pk_keys"].transpose(3, 2, 0, 1).reshape(64, 16, 128)
    out["pk_wq"] = v["L3_ffn_Wq"].reshape(128, 8, 128).transpose(1, 0, 2)
    out["pk_wo"] = v["L3_ffn_Wo"].reshape(8, 128, 128).transpose(1, 0, 2)
    out["tables"] = np.concatenate([v["L3_ffn_keys_table"], v["L3_ffn_values_table"]], axis=1)
    out["l1_W"] = v["L1_gnn_W"]
    return {k: np.ascontiguousarray(a) for k, a in out.items()}


def kernel(**inputs):
    import numpy as np
    import concourse.bacc as bacc
    from concourse import mybir as my
    from concourse.bass_utils import run_bass_kernel_spmd

    nc = bacc.Bacc("TRN2", target_bir_lowering=False, num_devices=1)
    arrays = layouts(np, {k: np.asarray(a) for k, a in inputs.items()})
    io = {k: nc.dram_tensor("in_" + k, a.shape, my.dt.from_np(a.dtype), kind="ExternalInput").ap() for k, a in arrays.items()}
    io["outT"] = nc.dram_tensor("outT", (128, 2048), my.dt.float32, kind="ExternalOutput").ap()
    build(nc, io)
    r = run_bass_kernel_spmd(nc, [{"in_" + k: a for k, a in arrays.items()}], core_ids=[0])
    return np.ascontiguousarray(r.results[0]["outT"].T)
```

```python
from contextlib import ExitStack

import concourse.bass as bass
from concourse import mybir

F32 = mybir.dt.float32
BF16 = mybir.dt.bfloat16
I32 = mybir.dt.int32
ALU = mybir.AluOpType
ACT = mybir.ActivationFunctionType
AX = mybir.AxisListType.X

P = 128
N = 2048
NT = N // P
CW = 512
NC = N // CW
LN_EPS = 1e-5
RING = 4


def build(nc, io, upto=99):
    with ExitStack() as ctx:
        kept = {}

        def sb(name, shape, dt=F32, scope=ctx):
            return scope.enter_context(nc.sbuf_tensor(name, shape, dt))

        retired = []

        def sem(name, scope=ctx):
            s = scope.enter_context(nc.semaphore(name))
            if scope is not ctx:
                assert s.num not in retired
                scope.callback(retired.append, s.num)
            return s

        def clear_retired():
            nums = sorted(retired)
            retired.clear()
            with nc.Block() as block:
                @block.gpsimd
                def _(pool):
                    while nums:
                        first = last = nums.pop(0)
                        while nums and nums[0] == last + 1:
                            last = nums.pop(0)
                        pool.sem_clear(range(first, last + 1))

        psum = ctx.enter_context(nc.psum_tensor("psum", [P, 8 * CW], F32))
        bank = [psum[:, i * CW:(i + 1) * CW] for i in range(8)]
        xT = sb("xT", [P, N])
        hT = sb("hT", [P, N])
        ident = sb("ident", [P, P])
        mean_w = sb("mean_w", [P, P])
        ones = sb("ones", [P, P])
        tri = sb("tri", [P, P])
        eps = sb("eps", [P, 1])
        off_diag = sb("off_diag", [P, P])
        rowsum = sb("rowsum", [P, N])
        diag_col = sb("diag_col", [P, NT])
        ring = sb("ring", [P, RING, N])
        a_ready = [sem(f"a_ready{i}") for i in range(RING)]
        a_used = sem("a_used")

        class Stream:
            issued = 0
            taken = 0

        def a_source(layout, n):
            if layout == "tile":
                return lambda slot: (ring[:, slot, :], io["adjT"][n * P:(n + 1) * P, :])
            q, s = n // 4, n % 4
            return lambda slot: (ring[:, slot, :].rearrange("p (m c) -> p m c", m=4),
                                 io["adjT"][4 * s * P:(4 * s + 4) * P, q * CW:(q + 1) * CW]
                                 .rearrange("(m p) c -> p m c", p=P))

        plan = []
        plan += [a_source("tile", n) for n in range(NT)]
        plan += [a_source("chunk", n) for n in range(NT)]
        for _ in range(3):
            plan += [a_source("tile", n) for n in range(NT)]

        def issue_a(eng, upto_n):
            while Stream.issued < min(upto_n, len(plan)):
                n = Stream.issued
                if n >= RING:
                    eng.wait_ge(a_used, n - RING + 1)
                dst, src = plan[n](n % RING)
                eng.dma_start(dst, src).then_inc(a_ready[n % RING], 16)
                Stream.issued += 1

        def wait_a(eng, n):
            eng.wait_ge(a_ready[n % RING], 16 * (n // RING + 1))

        def chunk(t, c):
            return t[:, c * CW:(c + 1) * CW]

        def tile(t, i):
            return t[:, i * P:(i + 1) * P]

        class Chain:
            def __init__(self, eng, s):
                self.eng, self.s, self.n = eng, s, 0

            def __call__(self, ins):
                self.n += 1
                ins.then_inc(self.s, 1)
                self.eng.wait_ge(self.s, self.n)

        small = {}
        w_loaded = sem("w_loaded")
        n_w = [0]

        def weight(eng, name, shape, src=None, dt=F32, scope=ctx):
            t = sb("w_" + name, shape, dt, scope)
            eng.dma_start(t[tuple(slice(None) for _ in shape)], io[name] if src is None else src).then_inc(w_loaded, 16)
            n_w[0] += 1
            return t

        consts_set = sem("consts_set")
        x_loaded = sem("x_loaded")
        with nc.Block() as block:
            @block.sync
            def _(sp):
                sp.dma_start(xT[:, :], io["xT"]).then_inc(x_loaded, 16)
                issue_a(sp, RING)

            @block.gpsimd
            def _(pool):
                pool.memset(ident[:, :], 0.0).then_inc(consts_set, 1)
                pool.memset(off_diag[:, :], 1.0).then_inc(consts_set, 1)
                pool.memset(mean_w[:, :], 1.0 / P).then_inc(consts_set, 1)
                pool.memset(ones[:, :], 1.0).then_inc(consts_set, 1)
                pool.memset(eps[:, :], LN_EPS).then_inc(consts_set, 1)
                pool.memset(rowsum[:, :], 0.0).then_inc(consts_set, 1)
                pool.wait_ge(consts_set, 2)
                pool.affine_select(out=ident[:, :], in_=ident[:, :], compare_op=ALU.not_equal, fill=1.0,
                                   base=0, pattern=[[-1, P]], channel_multiplier=1).then_inc(consts_set, 1)
                pool.affine_select(out=off_diag[:, :], in_=off_diag[:, :], compare_op=ALU.not_equal, fill=0.0,
                                   base=0, pattern=[[-1, P]], channel_multiplier=1).then_inc(consts_set, 1)
                pool.wait_ge(x_loaded, 16)

        def layer_norm(tag, loads=None):
            with ExitStack() as st, nc.Block() as block:
                squares = sb(f"squares_{tag}", [P, N], scope=st)
                std = sb(f"std_{tag}", [P, NT], scope=st)
                rstd = sb(f"rstd_{tag}", [P, NT], scope=st)
                rstd_d = sb(f"rstd_d_{tag}", [P, NT, P], scope=st)
                mean_done, centred, squared, var_done, std_done, inverted, placed, rstd_spread = (
                    sem(f"{k}_{tag}", st) for k in ("mean_done", "centred", "squared", "var_done", "std_done",
                                                    "inverted", "placed", "rstd_spread"))

                @block.sync
                def _(sp):
                    if loads:
                        loads(sp)

                @block.tensor
                def _(pe):
                    for c in range(NC):
                        pe.matmul(bank[c][:, :], mean_w[:, :], chunk(xT, c), start=True, stop=True).then_inc(mean_done, 1)
                    for i in range(NT):
                        if i % 4 == 0:
                            pe.wait_ge(squared, i // 4 + 1)
                        ins = pe.matmul(bank[4][:, i:i + 1], tile(squares, i), mean_w[:, 0:1], start=True, stop=True)
                    ins.then_inc(var_done, 1)
                    for c in range(NC):
                        pe.wait_ge(placed, c + 1)
                        pe.matmul(bank[c][:, :], ones[:, :], rstd_d[:, 4 * c:4 * c + 4, :].rearrange("p t d -> p (t d)"),
                                  start=True, stop=True).then_inc(rstd_spread, 1)

                @block.scalar
                def _(act):
                    for c in range(NC):
                        act.wait_ge(centred, c + 1)
                        act.activation(chunk(squares, c), chunk(hT, c), ACT.Square).then_inc(squared, 1)
                    act.wait_ge(var_done, 1)
                    act.activation(std[:, :], bank[4][:, 0:NT], ACT.Sqrt, bias=eps[:, 0:1]).then_inc(std_done, 1)

                @block.vector
                def _(dve):
                    for c in range(NC):
                        dve.wait_ge(mean_done, c + 1)
                        dve.tensor_tensor(chunk(hT, c), chunk(xT, c), bank[c][:, :], ALU.subtract).then_inc(centred, 1)
                    dve.wait_ge(std_done, 1)
                    dve.reciprocal(rstd[:, :], std[:, :]).then_inc(inverted, 1)
                    dve.wait_ge(inverted, 1)
                    for i in range(NT):
                        ins = dve.tensor_scalar(rstd_d[:, i, :], ident[:, :], rstd[:, i:i + 1], None, ALU.mult)
                        if i % 4 == 3:
                            ins.then_inc(placed, 1)
                    for c in range(NC):
                        dve.wait_ge(rstd_spread, c + 1)
                        dve.tensor_tensor(chunk(hT, c), chunk(hT, c), bank[c][:, :], ALU.mult)

        HEADS = 3
        base = 0
        layer_norm("l0g")
        with ExitStack() as l0:
            hW = sb("hW", [P, NT, HEADS * P], scope=l0)
            uP = sb("uP", [P, NT, 19], BF16, l0)
            uM = sb("uM", [P, NT, 19], BF16, l0)
            g9 = [sb(f"g9{s}", [P, NT, 9], BF16, l0) for s in "pm"]
            g = sb("g", [P, NT, 6], scope=l0)
            support = sb("support", [P, N], scope=l0)
            diag_b = sb("diag_b", [P, N], scope=l0)
            w_hw = sb("w_hw", [P, HEADS * P + 6], scope=l0)
            gru_w, gru_b = {}, {}
            for kind in ("edge", "node"):
                gru_w[kind] = [sb(f"{kind}_{m}", [P, 3 * P], scope=l0) for m in ("ih", "hh")]
                gru_b[kind] = [sb(f"{kind}_b{m}", [P, 3], scope=l0) for m in ("ih", "hh", "sum")]

            with ExitStack() as st:
                h_rows = sb("h_rows", [P, NT, P], scope=st)
                with ExitStack() as s1, nc.Block() as block:
                    gat_wT = sb("gat_wT", [P, HEADS, P], scope=s1)
                    gat_a = sb("gat_a", [P, HEADS, 2], scope=s1)
                    u = sb("u", [P, NT, 6], scope=s1)
                    rest = sb("rest", [P, NT, 6], scope=s1)
                    part = sb("part", [P, 3, NT, 6], BF16, s1)
                    wl, wa_done, wa_copied, h_turned, h_copied, hw_done, hw_copied, split = (
                        sem(k, s1) for k in ("l0_wl", "wa_done", "wa_copied", "h_turned", "h_copied", "hw_done", "hw_copied", "split"))

                    @block.sync
                    def _(sp):
                        sp.dma_start(gat_wT[:, :, :], io["gat_wT"]).then_inc(wl, 16)
                        sp.dma_start(gat_a[:, :, :], io["gat_a"]).then_inc(wl, 16)
                        sp.dma_start(w_hw[:, 0:HEADS * P].rearrange("p (k o) -> p k o", k=HEADS),
                                     io["gat_W"].rearrange("k p o -> p k o")).then_inc(wl, 16)
                        for kind in ("edge", "node"):
                            for w, b, m in zip(gru_w[kind], gru_b[kind], ("ih", "hh")):
                                sp.dma_start(w[:, :], io[f"{kind}_W{m}T"]).then_inc(wl, 16)
                                sp.dma_start(b[:, :], io[f"{kind}_b{m}"]).then_inc(wl, 16)
                        sp.wait_ge(wl, 16 * 11)

                    @block.tensor
                    def _(pe):
                        for i in range(NT):
                            ins = pe.transpose(bank[i // 4][:, (i % 4) * P:(i % 4 + 1) * P], tile(hT, i), ident[:, :])
                            if i % 4 == 3:
                                ins.then_inc(h_turned, 1)
                        pe.wait_ge(wl, 16 * 11)
                        for k in range(HEADS):
                            ins = pe.matmul(bank[4][:, 2 * k:2 * k + 2], gat_wT[:, k, :], gat_a[:, k, :], start=True, stop=True)
                        ins.then_inc(wa_done, 1)
                        pe.wait_ge(wa_copied, 1)
                        for i in range(NT):
                            if i >= 3:
                                pe.wait_ge(hw_copied, i - 2)
                            pe.matmul(bank[5 + i % 3][:, 0:HEADS * P + 6], tile(hT, i), w_hw[:, :], start=True, stop=True).then_inc(hw_done, 1)

                    @block.vector
                    def _(dve):
                        dve.wait_ge(wa_done, 1)
                        dve.tensor_copy(w_hw[:, HEADS * P:].rearrange("p (s k) -> p k s", s=2),
                                        bank[4][:, 0:6].rearrange("p (k s) -> p k s", k=3)).then_inc(wa_copied, 1)
                        for i in range(NT):
                            dve.wait_ge(hw_done, i + 1)
                            dve.tensor_copy(hW[:, i, :], bank[5 + i % 3][:, 0:HEADS * P])
                            dve.tensor_copy(u[:, i, :], bank[5 + i % 3][:, HEADS * P:HEADS * P + 6]).then_inc(hw_copied, 1)
                        dve.wait_ge(hw_copied, NT)
                        link = Chain(dve, split)
                        link(dve.tensor_copy(part[:, 0, :, :], u[:, :, :]))
                        link(dve.tensor_tensor(rest[:, :, :], u[:, :, :], part[:, 0, :, :], ALU.subtract))
                        link(dve.tensor_copy(part[:, 1, :, :], rest[:, :, :]))
                        link(dve.tensor_tensor(rest[:, :, :], rest[:, :, :], part[:, 1, :, :], ALU.subtract))
                        link(dve.tensor_copy(part[:, 2, :, :], rest[:, :, :]))
                        dve.memset(uP[:, :, 18:19], 0.0)
                        dve.memset(uM[:, :, 18:19], 1.0)
                        for s in range(3):
                            dve.tensor_copy(uP[:, :, 6 * s:6 * s + 6], part[:, s, :, :])
                            dve.tensor_copy(uM[:, :, 6 * s:6 * s + 3], part[:, s, :, 3:6])
                            dve.tensor_copy(uM[:, :, 6 * s + 3:6 * s + 6], part[:, s, :, 0:3])
                        for kind in ("edge", "node"):
                            dve.wait_ge(wl, 16 * 11)
                            bi, bh, bs = gru_b[kind]
                            dve.tensor_tensor(bs[:, :], bi[:, :], bh[:, :], ALU.add)

                    @block.scalar
                    def _(act):
                        for q in range(4):
                            act.wait_ge(h_turned, q + 1)
                            act.copy(h_rows[:, 4 * q:4 * q + 4, :].rearrange("p t d -> p (t d)"), bank[q][:, :])

                with ExitStack() as s2, nc.Block() as block:
                    pos = sb("pos", [P, 2, N], BF16, s2)
                    neg = sb("neg", [P, 2, N], BF16, s2)
                    diag_w = sb("diag_w", [P, P], scope=s2)
                    cleared, masked, a_mm, mask_used, summed, dcol, sup_done = (
                        sem(k, s2) for k in ("cleared", "masked", "a_mm", "mask_used", "summed", "dcol", "sup_done"))

                    @block.sync
                    def _(sp):
                        issue_a(sp, base + NT)

                    @block.vector
                    def _(dve):
                        for j in range(NT):
                            n = base + j
                            blk = ring[:, n % RING, j * P:(j + 1) * P]
                            wait_a(dve, n)
                            dve.tensor_tensor_reduce(out=diag_w[:, :], in0=blk, in1=ident[:, :], scale=1.0, scalar=0.0,
                                                     op0=ALU.mult, op1=ALU.add, accum_out=diag_col[:, j:j + 1]).then_inc(dcol, 1)
                            dve.wait_ge(dcol, j + 1)
                            dve.tensor_tensor(blk, blk, off_diag[:, :], ALU.mult).then_inc(cleared, 1)
                            dve.wait_ge(cleared, j + 1)
                            if j >= 2:
                                dve.wait_ge(mask_used, j - 1)
                            dve.tensor_scalar(pos[:, j % 2, :], ring[:, n % RING, :], 0.0, None, ALU.is_gt)
                            dve.tensor_scalar(neg[:, j % 2, :], ring[:, n % RING, :], 0.0, None, ALU.is_lt).then_inc(masked, 1)
                            if j >= 1:
                                dve.wait_ge(summed, j)
                            dve.tensor_tensor(rowsum[:, :], rowsum[:, :], ring[:, n % RING, :], ALU.add).then_inc(summed, 1)

                    @block.tensor
                    def _(pe):
                        for j in range(NT):
                            n = base + j
                            pe.wait_ge(cleared, j + 1)
                            for c in range(NC):
                                ins = pe.matmul(bank[c][:, :], h_rows[:, j, :], ring[:, n % RING, c * CW:(c + 1) * CW],
                                                start=(j == 0), stop=(j == NT - 1))
                            ins.then_inc(a_mm, 1)
                            pe.wait_ge(masked, j + 1)
                            for c in range(NC):
                                pe.matmul(bank[4 + c][0:19, :], uP[:, j, :], pos[:, j % 2, c * CW:(c + 1) * CW],
                                          start=(j == 0), stop=False)
                                ins = pe.matmul(bank[4 + c][0:19, :], uM[:, j, :], neg[:, j % 2, c * CW:(c + 1) * CW],
                                                start=False, stop=(j == NT - 1))
                            ins.then_inc(mask_used, 1)

                    @block.gpsimd
                    def _(pool):
                        for j in range(NT):
                            pool.wait_ge(a_mm, j + 1)
                            pool.wait_ge(summed, j + 1)
                            pool.sem_inc(a_used, 1)

                with ExitStack() as s3, nc.Block() as block:
                    eT = sb("eT", [19, N], scope=s3)
                    e_sp = sb("e_sp", [P, NT, 18], scope=s3)
                    e6 = sb("e6", [P, NT, 6], scope=s3)
                    top = sb("top", [P, NT, 3], scope=s3)
                    top3 = sb("top3", [P, 4], scope=s3)
                    best = sb("best", [3, 4], scope=s3)
                    best_d = sb("best_d", [3, 3], scope=s3)
                    shift = sb("shift", [P, 3], scope=s3)
                    gpart = sb("gpart", [P, 3, NT, 6], BF16, s3)
                    grest = sb("grest", [P, NT, 6], scope=s3)
                    dblk = sb("dblk", [P, NT, P], scope=s3)
                    e_copied, e_turned, e_step, m_turned, m_best, m_diag, m_spread, g_ready, d_ready, d_done = (
                        sem(k, s3) for k in ("e_copied", "e_turned", "e_step", "m_turned", "m_best", "m_diag", "m_spread", "g_ready", "d_ready", "d_done"))

                    @block.scalar
                    def _(act):
                        for c in range(NC):
                            act.copy(chunk(eT, c), bank[4 + c][0:19, :]).then_inc(e_copied, 1)
                        for c in range(NC):
                            act.copy(chunk(support, c), bank[c][:, :])
                        act.wait_ge(g_ready, 1)
                        act.activation(g[:, :, :], e6[:, :, :], ACT.Exp).then_inc(g_ready, 1)
                        for c in range(NC):
                            act.wait_ge(d_done, c + 1)
                            act.copy(chunk(diag_b, c), bank[4 + c][:, :])

                    @block.tensor
                    def _(pe):
                        pe.wait_ge(e_copied, NC)
                        for i in range(NT):
                            ins = pe.transpose(bank[4][:, 18 * i:18 * i + 18], eT[0:18, i * P:(i + 1) * P], ident[0:18, 0:18])
                        ins.then_inc(e_turned, 1)
                        pe.wait_ge(m_turned, 1)
                        pe.transpose(bank[5][0:3, 0:P], top3[:, 0:3], ident[:, :]).then_inc(m_turned, 1)
                        pe.wait_ge(m_diag, 1)
                        pe.matmul(bank[6][:, 0:3], ones[0:3, :], best_d[:, :], start=True, stop=True).then_inc(m_spread, 1)
                        pe.wait_ge(d_ready, 1)
                        pe.wait_ge(g_ready, 1)
                        for c in range(NC):
                            pe.matmul(bank[4 + c][:, :], ones[:, :], dblk[:, 4 * c:4 * c + 4, :].rearrange("p t d -> p (t d)"),
                                      start=True, stop=True).then_inc(d_done, 1)

                    @block.vector
                    def _(dve):
                        link = Chain(dve, e_step)
                        for j in range(NT):
                            ins = dve.tensor_scalar(dblk[:, j, :], ident[:, :], diag_col[:, j:j + 1], None, ALU.mult)
                        ins.then_inc(d_ready, 1)
                        dve.wait_ge(e_turned, 1)
                        link(dve.tensor_copy(e_sp[:, :, :].rearrange("p t s -> p (t s)"), bank[4][:, 0:NT * 18]))
                        link(dve.tensor_tensor(e6[:, :, :], e_sp[:, :, 12:18], e_sp[:, :, 6:12], ALU.add))
                        link(dve.tensor_tensor(e6[:, :, :], e6[:, :, :], e_sp[:, :, 0:6], ALU.add))
                        link(dve.scalar_tensor_tensor(out=e6[:, :, :], in0=e6[:, :, :], scalar=0.2, in1=e6[:, :, :],
                                                      op0=ALU.mult, op1=ALU.max))
                        link(dve.tensor_tensor(top[:, :, :], e6[:, :, 0:3], e6[:, :, 3:6], ALU.max))
                        dve.tensor_reduce(top3[:, 0:3], top[:, :, :].rearrange("p t k -> p k t"), AX, ALU.max).then_inc(m_turned, 1)
                        dve.wait_ge(m_turned, 2)
                        dve.tensor_reduce(best[:, 0:1], bank[5][0:3, 0:P], AX, ALU.max).then_inc(m_best, 1)
                        dve.wait_ge(m_best, 1)
                        dve.tensor_scalar(best_d[:, :], ident[0:3, 0:3], best[:, 0:1], None, ALU.mult).then_inc(m_diag, 1)
                        dve.wait_ge(m_spread, 1)
                        link(dve.tensor_scalar(shift[:, :], bank[6][:, 0:3], 60.0, None, ALU.subtract))
                        for k in range(6):
                            ins = dve.tensor_scalar(e6[:, :, k], e6[:, :, k], shift[:, k % 3:k % 3 + 1], None, ALU.subtract)
                        ins.then_inc(g_ready, 1)
                        dve.wait_ge(g_ready, 2)
                        link(dve.tensor_copy(gpart[:, 0, :, :], g[:, :, :]))
                        link(dve.tensor_tensor(grest[:, :, :], g[:, :, :], gpart[:, 0, :, :], ALU.subtract))
                        link(dve.tensor_copy(gpart[:, 1, :, :], grest[:, :, :]))
                        link(dve.tensor_tensor(grest[:, :, :], grest[:, :, :], gpart[:, 1, :, :], ALU.subtract))
                        link(dve.tensor_copy(gpart[:, 2, :, :], grest[:, :, :]))
                        for s in range(3):
                            for h in range(2):
                                dve.tensor_copy(g9[h][:, :, 3 * s:3 * s + 3], gpart[:, s, :, 3 * h:3 * h + 3])


            def gru(kind, source):
                with ExitStack() as s4, nc.Block() as block:
                    w_ih, w_hh = gru_w[kind]
                    b_ih, b_hh, b_sum = gru_b[kind]
                    r, z, t, o = (sb(f"{kind}_{k}", [P, 2, CW], scope=s4) for k in "rzto")
                    sig = [sem(f"{kind}_{k}", s4) for k in ("mm", "sg", "tt", "th", "ch", "free")]
                    mm, gates, pre, cand, step, free = sig

                    @block.tensor
                    def _(pe):
                        for c in range(NC):
                            b = 4 * (c % 2)
                            if c >= 2:
                                pe.wait_ge(free, c - 1)
                            for k in range(2):
                                pe.matmul(bank[b + k][:, :], tile(w_ih, k), chunk(source, c), start=True, stop=False)
                                pe.matmul(bank[b + k][:, :], tile(w_hh, k), chunk(hT, c), start=False, stop=True)
                            pe.matmul(bank[b + 2][:, :], tile(w_ih, 2), chunk(source, c), start=True, stop=True)
                            pe.matmul(bank[b + 3][:, :], tile(w_hh, 2), chunk(hT, c), start=True, stop=True).then_inc(mm, 1)

                    @block.scalar
                    def _(act):
                        for c in range(NC):
                            b = 4 * (c % 2)
                            act.wait_ge(mm, c + 1)
                            if c >= 2:
                                act.wait_ge(step, 5 * (c - 1))
                            act.activation(r[:, c % 2, :], bank[b][:, :], ACT.Sigmoid, bias=b_sum[:, 0:1])
                            act.activation(z[:, c % 2, :], bank[b + 1][:, :], ACT.Sigmoid, bias=b_sum[:, 1:2]).then_inc(gates, 1)
                            act.wait_ge(pre, 2 * (c + 1))
                            act.activation(t[:, c % 2, :], t[:, c % 2, :], ACT.Tanh, bias=b_ih[:, 2:3]).then_inc(cand, 1)

                    @block.vector
                    def _(dve):
                        link = Chain(dve, step)
                        for c in range(NC):
                            b = 4 * (c % 2)
                            tc, oc = t[:, c % 2, :], o[:, c % 2, :]
                            dve.wait_ge(gates, c + 1)
                            dve.scalar_tensor_tensor(out=tc, in0=bank[b + 3][:, :], scalar=b_hh[:, 2:3], in1=r[:, c % 2, :],
                                                     op0=ALU.add, op1=ALU.mult).then_inc(pre, 1)
                            dve.wait_ge(pre, 2 * c + 1)
                            ins = dve.tensor_tensor(tc, tc, bank[b + 2][:, :], ALU.add)
                            ins.then_inc(pre, 1)
                            dve.wait_ge(cand, c + 1)
                            link(dve.tensor_tensor(oc, chunk(hT, c), tc, ALU.subtract))
                            link(dve.tensor_tensor(oc, oc, z[:, c % 2, :], ALU.mult))
                            link(dve.tensor_tensor(oc, oc, tc, ALU.add))
                            link(dve.tensor_tensor(oc, oc, chunk(diag_b, c), ALU.mult))
                            link(dve.tensor_tensor(chunk(xT, c), chunk(xT, c), oc, ALU.add))
                            dve.sem_inc(free, 1)

            gru("edge", support)

            base = NT
            with ExitStack() as s5, nc.Block() as block:
                NB = 3
                a_part = [sb(f"a_{k}", [P, NB, CW], scope=s5) for k in ("pos", "neg")]
                a_mask = [sb(f"m_{k}", [P, NB, CW], BF16, s5) for k in ("pos", "neg")]
                G = [sb(f"G_{k}", [P, NB, HEADS * P], scope=s5) for k in ("pos", "neg")]
                pick = sb("pick", [9, HEADS, P], scope=s5)
                pick_col = sb("pick_col", [9, HEADS], scope=s5)
                den9 = sb("den9", [9, CW], scope=s5)
                num = sb("num", [P, HEADS, CW], scope=s5)
                rec = sb("rec", [P, CW], scope=s5)
                picked, parts, G_ready, used, evac, spread, den_used, dstep, finished = (
                    sem(k, s5) for k in ("picked", "parts", "G_ready", "used", "evac", "spread", "den_used", "dstep", "finished"))

                @block.sync
                def _(sp):
                    issue_a(sp, base + NT)

                @block.vector
                def _(dve):
                    link = Chain(dve, dstep)
                    for k in range(HEADS):
                        link(dve.tensor_reduce(pick_col[:, k:k + 1], ident[0:9, k:9:3], AX, ALU.add))
                        dve.tensor_scalar(pick[:, k, :], ones[0:9, :], pick_col[:, k:k + 1], float(HEADS),
                                          ALU.mult, ALU.mult).then_inc(picked, 1)

                    def finish(q):
                        b = 4 * (q % 2)
                        for k in range(HEADS):
                            dve.wait_ge(spread, HEADS * q + k + 1)
                            link(dve.tensor_scalar(rec[:, :], bank[b + k][:, :], 1e-37, None, ALU.max))
                            dve.sem_inc(den_used, 1)
                            link(dve.reciprocal(rec[:, :], rec[:, :]))
                            if k == 0:
                                link(dve.tensor_tensor(chunk(support, q), num[:, k, :], rec[:, :], ALU.mult))
                            else:
                                link(dve.tensor_tensor(rec[:, :], num[:, k, :], rec[:, :], ALU.mult))
                                link(dve.tensor_tensor(chunk(support, q), chunk(support, q), rec[:, :], ALU.add))
                        dve.sem_inc(finished, 1)

                    it = 0
                    for q in range(NC):
                        for j in range(NT):
                            n = base + 4 * q + j // 4
                            a = ring[:, n % RING, (j % 4) * CW:(j % 4 + 1) * CW]
                            if j % 4 == 0:
                                wait_a(dve, n)
                            if j // 4 == q:
                                blk = a[:, (j % 4) * P:(j % 4 + 1) * P]
                                link(dve.tensor_tensor(blk, blk, off_diag[:, :], ALU.mult))
                            if it >= NB:
                                dve.wait_ge(used, it - NB + 1)
                            s = it % NB
                            dve.tensor_scalar(a_part[0][:, s, :], a, 0.0, None, ALU.max)
                            dve.tensor_scalar(a_part[1][:, s, :], a, 0.0, None, ALU.min)
                            dve.tensor_scalar(a_mask[0][:, s, :], a, 0.0, None, ALU.is_gt)
                            ins = dve.tensor_scalar(a_mask[1][:, s, :], a, 0.0, None, ALU.is_lt)
                            ins.then_inc(parts, 1)
                            it += 1
                            if j % 4 == 3:
                                dve.wait_ge(parts, it)
                                dve.sem_inc(a_used, 1)
                            if q >= 1 and j == 5:
                                finish(q - 1)
                    finish(NC - 1)

                @block.scalar
                def _(act):
                    def drain(q):
                        act.wait_ge(used, NT * (q + 1))
                        if q >= 1:
                            act.wait_ge(finished, q)
                        b = 4 * (q % 2)
                        act.copy(den9[:, :], bank[b + 3][0:9, :])
                        for k in range(HEADS):
                            ins = act.copy(num[:, k, :], bank[b + k][:, :])
                        ins.then_inc(evac, 1)
                    it = 0
                    for q in range(NC):
                        for j in range(NT):
                            if it >= NB:
                                act.wait_ge(used, it - NB + 1)
                            for h in range(2):
                                for k in range(HEADS):
                                    ins = act.mul(G[h][:, it % NB, k * P:(k + 1) * P], hW[:, j, k * P:(k + 1) * P],
                                                  g[:, j, 3 * h + k:3 * h + k + 1])
                            ins.then_inc(G_ready, 1)
                            it += 1
                            if q >= 1 and j == 1:
                                drain(q - 1)
                    drain(NC - 1)

                @block.tensor
                def _(pe):
                    def spread_den(q):
                        b = 4 * (q % 2)
                        pe.wait_ge(evac, q + 1)
                        for k in range(HEADS):
                            pe.matmul(bank[b + k][:, :], pick[:, k, :], den9[:, :], start=True, stop=True).then_inc(spread, 1)
                    pe.wait_ge(picked, HEADS)
                    it = 0
                    for q in range(NC):
                        b = 4 * (q % 2)
                        if q >= 2:
                            pe.wait_ge(den_used, HEADS * (q - 1))
                        for j in range(NT):
                            s = it % NB
                            pe.wait_ge(G_ready, it + 1)
                            pe.wait_ge(parts, it + 1)
                            for h in range(2):
                                for k in range(HEADS):
                                    pe.matmul(bank[b + k][:, :], G[h][:, s, k * P:(k + 1) * P], a_part[h][:, s, :],
                                              start=(j == 0 and h == 0), stop=(j == NT - 1 and h == 1))
                                ins = pe.matmul(bank[b + 3][0:9, :], g9[h][:, j, :], a_mask[h][:, s, :],
                                                start=(j == 0 and h == 0), stop=(j == NT - 1 and h == 1))
                            ins.then_inc(used, 1)
                            it += 1
                            if q >= 1 and j == 3:
                                spread_den(q - 1)
                    spread_den(NC - 1)

            gru("node", support)
        clear_retired()
        E, F, C = 8, 512, 320
        FT = F // P
        SLOTS = E * C
        ST = SLOTS // P
        parts_of_c = [(0, P), (P, P), (2 * P, C - 2 * P)]
        h_scat = nc.dram_tensor("h_scat", (SLOTS + N, P), F32, kind="Internal").ap()
        y_slots = nc.dram_tensor("y_slots", (SLOTS, P), F32, kind="Internal").ap()

        with ExitStack() as m0:
            gate_w = sb("gate_w", [P, E], scope=m0)
            gate_b = sb("gate_b", [P, NT, E], scope=m0)
            b2_row = sb("b2_row", [1, E * P], scope=m0)
            zero = sb("zero", [P, ST * P], scope=m0)
            gl, zeroed, zset = sem("gl", m0), sem("zeroed", m0), sem("zset", m0)
            rank_down = sb("rank_down", [P, NT, E], scope=m0)
            token = sb("token", [P, NT], scope=m0)
            keep_w = sb("keep_w", [P, NT], scope=m0)
            slot_s = sb("slot_s", [P, NT], I32, m0)
            slot_g = sb("slot_g", [P, NT], I32, m0)

            def moe_loads(sp):
                sp.dma_start(gate_w[:, :], io["gate_w"]).then_inc(gl, 16)
                sp.dma_start(gate_b[:, :, :], io["gate_b"]).then_inc(gl, 16)
                sp.dma_start(b2_row[:, :], io["moe_b2"]).then_inc(gl, 16)
                sp.wait_ge(gl, 48)

            layer_norm("l0f", moe_loads)

            with ExitStack() as s1, nc.Block() as block:
                h_rows = sb("moe_h_rows", [P, NT, P], scope=s1)
                lg, ex, score, oh, cum, pre_a, pre_b = (sb(f"moe_{k}", [P, NT, E], scope=s1)
                                                        for k in ("lg", "ex", "score", "oh", "cum", "pre_a", "pre_b"))
                mx, best_e, den, pos_t, kept, t1, t2 = (sb(f"moe_{k}", [P, NT], scope=s1)
                                                        for k in ("mx", "best_e", "den", "pos_t", "kept", "t1", "t2"))
                iota_e = sb("iota_e", [P, NT, E], I32, s1)
                iota_t = sb("iota_t", [P, NT], I32, s1)
                cst, h_turned, h_copied, lg_done, ex_in, ex_out, step, oh_ready, cum_done, slots_ready = (
                    sem(f"moe_{k}", s1) for k in ("cst", "h_turned", "h_copied", "lg_done", "ex_in", "ex_out", "step",
                                                  "oh_ready", "cum_done", "slots_ready"))
                sent = sem("moe_sent")

                @block.tensor
                def _(pe):
                    for i in range(NT):
                        ins = pe.matmul(bank[4][:, E * i:E * i + E], tile(hT, i), gate_w[:, :], start=True, stop=True)
                    ins.then_inc(lg_done, 1)
                    for i in range(NT):
                        ins = pe.transpose(bank[i // 4][:, (i % 4) * P:(i % 4 + 1) * P], tile(hT, i), ident[:, :])
                        if i % 4 == 3:
                            ins.then_inc(h_turned, 1)
                    pe.wait_ge(oh_ready, 1)
                    pe.wait_ge(cst, 5)
                    flat = oh[:, :, :].rearrange("p t e -> p (t e)")
                    pe.matmul(bank[5][:, 0:P], tri[:, :], flat, start=True, stop=True)
                    pe.matmul(bank[6][:, 0:P], ones[:, :], flat, start=True, stop=True).then_inc(cum_done, 1)

                @block.scalar
                def _(act):
                    for q in range(4):
                        act.wait_ge(h_turned, q + 1)
                        act.copy(h_rows[:, 4 * q:4 * q + 4, :].rearrange("p t d -> p (t d)"), bank[q][:, :]).then_inc(h_copied, 1)
                    act.wait_ge(ex_in, 1)
                    act.activation(ex[:, :, :], ex[:, :, :], ACT.Exp).then_inc(ex_out, 1)

                @block.vector
                def _(dve):
                    link = Chain(dve, step)

                    def over_e(t):
                        return t[:, :].unsqueeze(2).broadcast_to([P, NT, E])
                    dve.wait_ge(cst, 5)
                    dve.tensor_copy(rank_down[:, :, :], iota_e[:, :, :])
                    link(dve.tensor_copy(token[:, :], iota_t[:, :]))
                    dve.wait_ge(lg_done, 1)
                    link(dve.tensor_tensor(lg[:, :, :], bank[4][:, 0:P].rearrange("p (t e) -> p t e", e=E), gate_b[:, :, :], ALU.add))
                    link(dve.tensor_reduce(mx[:, :], lg[:, :, :], AX, ALU.max))
                    dve.tensor_tensor(ex[:, :, :], lg[:, :, :], over_e(mx), ALU.subtract).then_inc(ex_in, 1)
                    link(dve.tensor_tensor(score[:, :, :], lg[:, :, :], over_e(mx), ALU.is_equal))
                    link(dve.tensor_tensor(score[:, :, :], score[:, :, :], rank_down[:, :, :], ALU.mult))
                    link(dve.tensor_reduce(best_e[:, :], score[:, :, :], AX, ALU.max))
                    dve.tensor_tensor(oh[:, :, :], score[:, :, :], over_e(best_e), ALU.is_equal).then_inc(oh_ready, 1)
                    dve.wait_ge(ex_out, 1)
                    link(dve.tensor_reduce(den[:, :], ex[:, :, :], AX, ALU.add))
                    link(dve.reciprocal(den[:, :], den[:, :]))
                    dve.wait_ge(cum_done, 1)
                    link(dve.tensor_copy(pre_a[:, :, :].rearrange("p t e -> p (t e)"), bank[6][:, 0:P]))
                    src, dst = pre_a, pre_b
                    for sft in (1, 2, 4, 8):
                        dve.tensor_copy(dst[:, 0:sft, :], src[:, 0:sft, :])
                        link(dve.tensor_tensor(dst[:, sft:, :], src[:, sft:, :], src[:, :NT - sft, :], ALU.add))
                        src, dst = dst, src
                    link(dve.tensor_tensor(cum[:, :, :].rearrange("p t e -> p (t e)"), src[:, :, :].rearrange("p t e -> p (t e)"),
                                           bank[6][:, 0:P], ALU.subtract))
                    link(dve.tensor_tensor(cum[:, :, :].rearrange("p t e -> p (t e)"), cum[:, :, :].rearrange("p t e -> p (t e)"),
                                           bank[5][:, 0:P], ALU.add))
                    link(dve.tensor_tensor(cum[:, :, :], cum[:, :, :], oh[:, :, :], ALU.mult))
                    link(dve.tensor_reduce(pos_t[:, :], cum[:, :, :], AX, ALU.add))
                    link(dve.tensor_scalar(pos_t[:, :], pos_t[:, :], 1.0, None, ALU.subtract))
                    link(dve.tensor_scalar(kept[:, :], pos_t[:, :], float(C), None, ALU.is_lt))
                    dve.tensor_tensor(keep_w[:, :], den[:, :], kept[:, :], ALU.mult)
                    link(dve.tensor_scalar(t1[:, :], best_e[:, :], -float(C), float(E * C), ALU.mult, ALU.add))
                    link(dve.scalar_tensor_tensor(out=t2[:, :], in0=pos_t[:, :], scalar=float(C - 1), in1=t1[:, :],
                                                  op0=ALU.min, op1=ALU.add))
                    dve.tensor_copy(slot_g[:, :], t2[:, :])
                    link(dve.tensor_tensor(t1[:, :], t1[:, :], pos_t[:, :], ALU.add))
                    link(dve.tensor_tensor(t1[:, :], t1[:, :], token[:, :], ALU.subtract))
                    link(dve.tensor_tensor(t1[:, :], t1[:, :], kept[:, :], ALU.mult))
                    link(dve.tensor_tensor(t1[:, :], t1[:, :], token[:, :], ALU.add))
                    dve.tensor_copy(slot_s[:, :], t1[:, :]).then_inc(slots_ready, 1)

                @block.gpsimd
                def _(pool):
                    pool.memset(zero[:, :], 0.0).then_inc(zset, 1)
                    pool.memset(tri[:, :], 1.0).then_inc(cst, 1)
                    pool.iota(iota_e[:, :, :], [[0, NT], [-1, E]], base=E, channel_multiplier=0).then_inc(cst, 1)
                    pool.iota(iota_t[:, :], [[P, NT]], base=SLOTS, channel_multiplier=1).then_inc(cst, 1)
                    pool.wait_ge(cst, 3)
                    pool.affine_select(out=tri[:, :], in_=tri[:, :], compare_op=ALU.is_ge, fill=0.0,
                                       base=0, pattern=[[1, P]], channel_multiplier=-1).then_inc(cst, 2)
                    pool.wait_ge(zeroed, 16)
                    pool.wait_ge(h_copied, 4)
                    pool.wait_ge(slots_ready, 1)
                    for i in range(NT):
                        pool.indirect_dma_start(h_scat[:, :], bass.IndirectOffsetOnAxis(ap=slot_s[:, i:i + 1], axis=0),
                                                h_rows[:, i, :], None).then_inc(sent, 16)
                    pool.wait_ge(sent, 16 * NT)

                @block.sync
                def _(sp):
                    sp.wait_ge(zset, 1)
                    sp.dma_start(h_scat[0:SLOTS, :].rearrange("(s p) d -> p s d", p=P),
                                 zero[:, :].rearrange("p (s d) -> p s d", s=ST)).then_inc(zeroed, 16)
                    sp.wait_ge(zeroed, 16)

            with ExitStack() as s2, nc.Block() as block:
                EW = FT * P * 2 + FT
                slot_rows = sb("slot_rows", [P, ST, P], scope=s2)
                slotT = sb("slotT", [P, SLOTS], scope=s2)
                ew = sb("ew", [P, 2, EW], scope=s2)
                mid = sb("mid", [P, 2, FT, C], scope=s2)
                y_sb = sb("y_sb", [P, 2, 3, P], scope=s2)
                rows_in, turned, turned_copied, mid_mm, mid_act, y_mm, y_cp = (
                    sem(f"exp_{k}", s2) for k in ("rows_in", "turned", "turned_copied", "mid_mm", "mid_act", "y_mm", "y_cp"))
                ew_in = [sem(f"ew_in{u}", s2) for u in range(2)]
                y_out = [sem(f"y_out{u}", s2) for u in range(2)]

                def store(sp, e):
                    sp.wait_ge(y_cp, 3 * (e + 1))
                    for s, (at, m) in enumerate(parts_of_c):
                        sp.dma_start(y_slots[e * C + at:e * C + at + m, :], y_sb[0:m, e % 2, s, :]).then_inc(y_out[e % 2], 16)

                @block.sync
                def _(sp):
                    sp.dma_start(slot_rows[:, :, :], h_scat[0:SLOTS, :].rearrange("(s p) d -> p s d", p=P)).then_inc(rows_in, 16)
                    for e in range(E):
                        u = e % 2
                        if e >= 2:
                            sp.wait_ge(y_mm, 3 * (e - 1))
                        sp.dma_start(ew[:, u, :], io["moe_w"][e]).then_inc(ew_in[u], 16)
                        if e >= 1:
                            store(sp, e - 1)
                    store(sp, E - 1)
                    for u in range(2):
                        sp.wait_ge(y_out[u], 16 * 3 * E // 2)

                @block.tensor
                def _(pe):
                    pe.wait_ge(rows_in, 16)
                    for i in range(ST):
                        if i // 4 >= 4 and i % 4 == 0:
                            pe.wait_ge(turned_copied, i // 4 - 3)
                        ins = pe.transpose(bank[i // 4 % 4][:, (i % 4) * P:(i % 4 + 1) * P], slot_rows[:, i, :], ident[:, :])
                        if i % 4 == 3:
                            ins.then_inc(turned, 1)
                    pe.wait_ge(turned_copied, ST // 4)
                    for e in range(E):
                        u = e % 2
                        pe.wait_ge(ew_in[u], 16 * (e // 2 + 1))
                        for f in range(FT):
                            if e >= 1:
                                pe.wait_ge(mid_act, FT * (e - 1) + f + 1)
                            pe.matmul(bank[f][:, 0:C], ew[:, u, f * P:(f + 1) * P], slotT[:, e * C:(e + 1) * C],
                                      start=True, stop=True).then_inc(mid_mm, 1)
                        pe.wait_ge(mid_act, FT * (e + 1))
                        for s, (at, m) in enumerate(parts_of_c):
                            if e >= 1:
                                pe.wait_ge(y_cp, 3 * (e - 1) + s + 1)
                            pe.matmul(bank[4 + s][0:m, 0:P], ones[0:1, 0:m], b2_row[:, e * P:(e + 1) * P], start=True, stop=False)
                            for f in range(FT):
                                ins = pe.matmul(bank[4 + s][0:m, 0:P], mid[:, u, f, at:at + m], ew[:, u, F + f * P:F + (f + 1) * P],
                                                start=False, stop=(f == FT - 1))
                            ins.then_inc(y_mm, 1)

                @block.scalar
                def _(act):
                    for e in range(E):
                        for f in range(FT):
                            act.wait_ge(mid_mm, FT * e + f + 1)
                            if e >= 2:
                                act.wait_ge(y_mm, 3 * (e - 1))
                            act.activation(mid[:, e % 2, f, :], bank[f][:, 0:C], ACT.Relu,
                                           bias=ew[:, e % 2, 2 * F + f:2 * F + f + 1]).then_inc(mid_act, 1)

                @block.vector
                def _(dve):
                    for q in range(ST // 4):
                        dve.wait_ge(turned, q + 1)
                        dve.tensor_copy(chunk(slotT, q), bank[q % 4][:, :]).then_inc(turned_copied, 1)
                    for e in range(E):
                        for s, (at, m) in enumerate(parts_of_c):
                            dve.wait_ge(y_mm, 3 * e + s + 1)
                            if e >= 2:
                                dve.wait_ge(y_out[e % 2], 16 * 3 * (e // 2))
                            dve.tensor_copy(y_sb[0:m, e % 2, s, :], bank[4 + s][0:m, 0:P]).then_inc(y_cp, 1)

            with ExitStack() as s3, nc.Block() as block:
                got = sb("got", [P, NT, P], scope=s3)
                clean = sb("clean", [P, NT, P], scope=s3)
                mask = sb("nan_mask", [P, NT, P], scope=s3)
                big = sb("big", [P, 4 * P], scope=s3)
                small_v = sb("small_v", [P, 4 * P], scope=s3)
                fetched = [sem(f"fetched{q}") for q in range(4)]
                cset, step, cleaned, turned = (sem(f"comb_{k}", s3) for k in ("cset", "step", "cleaned", "turned"))

                @block.gpsimd
                def _(pool):
                    pool.memset(clean[:, :, :], 0.0).then_inc(cset, 1)
                    pool.memset(big[:, :], 10000.0).then_inc(cset, 1)
                    pool.memset(small_v[:, :], -10000.0).then_inc(cset, 1)
                    for i in range(NT):
                        pool.indirect_dma_start(got[:, i, :], None, y_slots[:, :],
                                                bass.IndirectOffsetOnAxis(ap=slot_g[:, i:i + 1], axis=0)).then_inc(fetched[i // 4], 16)

                @block.vector
                def _(dve):
                    link = Chain(dve, step)
                    dve.wait_ge(cset, 3)
                    for q in range(4):
                        def four(t, dt=F32):
                            return t[:, 4 * q:4 * q + 4, :].rearrange("p t d -> p (t d)")
                        dve.wait_ge(fetched[q], 64)
                        for i in range(4 * q, 4 * q + 4):
                            ins = dve.tensor_scalar(got[:, i, :], got[:, i, :], keep_w[:, i:i + 1], None, ALU.mult)
                        link(ins)
                        link(dve.tensor_tensor(four(mask), four(got), four(got), ALU.is_equal))
                        link(dve.copy_predicated(four(clean), four(mask).bitcast(I32), four(got)))
                        link(dve.tensor_scalar(four(mask), four(clean), 3.4028234e38, None, ALU.is_gt))
                        link(dve.copy_predicated(four(clean), four(mask).bitcast(I32), big[:, :]))
                        link(dve.tensor_scalar(four(mask), four(clean), -3.4028234e38, None, ALU.is_lt))
                        dve.copy_predicated(four(clean), four(mask).bitcast(I32), small_v[:, :]).then_inc(cleaned, 1)
                    for q in range(4):
                        dve.wait_ge(turned, q + 1)
                        dve.tensor_tensor(chunk(xT, q), chunk(xT, q), bank[q][:, :], ALU.add)

                @block.tensor
                def _(pe):
                    for q in range(4):
                        pe.wait_ge(cleaned, q + 1)
                        for i in range(4 * q, 4 * q + 4):
                            ins = pe.transpose(bank[q][:, (i % 4) * P:(i % 4 + 1) * P], clean[:, i, :], ident[:, :])
                        ins.then_inc(turned, 1)

        clear_retired()
        dinv = {}

        def gcn(tag, base, w_name, b_name=None, extra=None):
            with ExitStack() as g0:
                w = sb(f"w_{tag}", [P, P], scope=g0)
                bias = sb(f"b_{tag}", [P, 1], scope=g0)
                dcol = sb(f"dcol_{tag}", [P, NT], scope=g0)
                d_blk = sb(f"d_blk_{tag}", [P, NT, P], scope=g0)
                d_b = sb(f"d_b_{tag}", [P, N], scope=g0)
                Z = sb(f"Z_{tag}", [P, NT, P], scope=g0)
                wl = sem(f"wl_{tag}", g0)

                def loads(sp):
                    sp.dma_start(w[:, :], io[w_name]).then_inc(wl, 16)
                    if b_name:
                        sp.dma_start(bias[:, :], io[b_name]).then_inc(wl, 16)
                    sp.wait_ge(wl, 32 if b_name else 16)
                    issue_a(sp, base + RING)
                layer_norm(tag, loads)
                with ExitStack() as s1, nc.Block() as block:
                    deg_done, step, root, placed, spread, d_copied, z_mm, z_cp, a_mm, out_t, scaled = (
                        sem(f"{tag}_{k}", s1) for k in ("deg_done", "step", "root", "placed", "spread", "d_copied",
                                                        "z_mm", "z_cp", "a_mm", "out_t", "scaled"))

                    @block.sync
                    def _(sp):
                        issue_a(sp, base + NT)

                    @block.tensor
                    def _(pe):
                        if extra is not None:
                            for i in range(NT):
                                ins = pe.matmul(bank[7][:, i:i + 1], tile(rowsum, i), ones[:, 0:1], start=True, stop=True)
                            ins.then_inc(deg_done, 1)
                        for i in range(NT):
                            ins = pe.matmul(bank[i // 4][:, (i % 4) * P:(i % 4 + 1) * P], tile(hT, i), w[:, :], start=True, stop=True)
                            if i % 4 == 3:
                                ins.then_inc(z_mm, 1)
                        if extra is not None:
                            for c in range(NC):
                                pe.wait_ge(placed, c + 1)
                                b = 4 + c % 2
                                if c >= 2:
                                    pe.wait_ge(d_copied, c - 1)
                                pe.matmul(bank[b][:, :], ones[:, :], d_blk[:, 4 * c:4 * c + 4, :].rearrange("p t d -> p (t d)"),
                                          start=True, stop=True).then_inc(spread, 1)
                        pe.wait_ge(z_cp, 4)
                        if extra:
                            pe.wait_ge(scaled, NC)
                        for j in range(NT):
                            n = base + j
                            wait_a(pe, n)
                            for c in range(NC):
                                ins = pe.matmul(bank[c][:, :], Z[:, j, :], ring[:, n % RING, c * CW:(c + 1) * CW],
                                                start=(j == 0), stop=(j == NT - 1 and not extra))
                            ins.then_inc(a_used, 1)
                        if extra:
                            for c in range(NC):
                                pe.matmul(bank[c][:, :], w[:, :], chunk(hT, c), start=False, stop=True).then_inc(a_mm, 1)

                    @block.scalar
                    def _(act):
                        if extra is not None:
                            act.wait_ge(step, 2)
                            act.activation(dcol[:, :], dcol[:, :], ACT.Sqrt).then_inc(root, 1)
                            for c in range(NC):
                                act.wait_ge(spread, c + 1)
                                act.copy(chunk(d_b, c), bank[4 + c % 2][:, :]).then_inc(d_copied, 1)
                            if b_name:
                                for c in range(NC):
                                    act.wait_ge(out_t, c + 1)
                                    act.activation(chunk(hT, c), chunk(hT, c), ACT.Relu, bias=bias[:, 0:1]).then_inc(root, 1)
                        else:
                            for c in range(NC):
                                act.wait_ge(a_used, base + NT)
                                act.activation(chunk(hT, c), bank[c][:, :], ACT.Relu, bias=bias[:, 0:1]).then_inc(root, 1)

                    @block.vector
                    def _(dve):
                        link = Chain(dve, step)
                        if extra is not None:
                            dve.wait_ge(deg_done, 1)
                            link(dve.tensor_tensor(dcol[:, :], bank[7][:, 0:NT], diag_col[:, :], ALU.add))
                            link(dve.tensor_scalar(dcol[:, :], dcol[:, :], extra, None, ALU.add))
                            dve.wait_ge(root, 1)
                            link(dve.reciprocal(dcol[:, :], dcol[:, :]))
                            for i in range(NT):
                                ins = dve.tensor_scalar(d_blk[:, i, :], ident[:, :], dcol[:, i:i + 1], None, ALU.mult)
                                if i % 4 == 3:
                                    ins.then_inc(placed, 1)
                        for q in range(4):
                            dve.wait_ge(z_mm, q + 1)
                            for i in range(4 * q, 4 * q + 4):
                                src = bank[q][:, (i % 4) * P:(i % 4 + 1) * P]
                                if extra is None:
                                    ins = dve.tensor_copy(Z[:, i, :], src)
                                else:
                                    ins = dve.tensor_scalar(Z[:, i, :], src, dcol[:, i:i + 1], None, ALU.mult)
                            ins.then_inc(z_cp, 1)
                        if extra:
                            for c in range(NC):
                                dve.wait_ge(d_copied, c + 1)
                                dve.tensor_tensor(chunk(hT, c), chunk(hT, c), chunk(d_b, c), ALU.mult).then_inc(scaled, 1)
                        for c in range(NC):
                            if extra is None:
                                dve.wait_ge(root, c + 1)
                                dve.tensor_tensor(chunk(xT, c), chunk(xT, c), chunk(hT, c), ALU.add)
                                continue
                            if extra:
                                dve.wait_ge(a_mm, c + 1)
                            else:
                                dve.wait_ge(a_used, base + NT)
                            if c == 0:
                                dve.wait_ge(d_copied, NC)
                            ins = dve.tensor_tensor(chunk(hT, c), bank[c][:, :], chunk(d_b, c), ALU.mult)
                            if b_name:
                                ins.then_inc(out_t, 1)
                                dve.wait_ge(root, c + 2)
                                dve.tensor_tensor(chunk(xT, c), chunk(xT, c), chunk(hT, c), ALU.add)
                            else:
                                link(ins)
                                dve.scalar_tensor_tensor(out=chunk(xT, c), in0=chunk(hT, c), scalar=0.0, in1=chunk(xT, c),
                                                         op0=ALU.max, op1=ALU.add)

        gcn("l1g", 2 * NT, "l1_W", None, 0.0)
        clear_retired()
        LEVELS = 8
        NODES = 2 ** LEVELS - 1
        LEAVES = 2 ** (LEVELS - 1)
        RW = 144
        PAIRS = [(NT + 2 ** l - 1 + 3) // 4 * 4 for l in range(LEVELS)]
        OFF = [sum(PAIRS[:l]) for l in range(LEVELS)]
        NP = sum(PAIRS)
        WR = 8
        assert NP % WR == 0
        t_sorted = nc.dram_tensor("t_sorted", (N, RW), F32, kind="Internal").ap()
        o_sorted = nc.dram_tensor("o_sorted", (N, P), F32, kind="Internal").ap()

        def level(t, l):
            return t[:, :, 2 ** l - 1:2 ** (l + 1) - 1]

        with ExitStack() as f0:
            w1T = sb("fff_w1T", [P, NODES], scope=f0)
            b1 = sb("fff_b1", [1, NODES], scope=f0)
            b2 = [sb("fff_b2a", [P, P], scope=f0), sb("fff_b2b", [NODES - P, P], scope=f0)]
            rank = sb("rank", [P, NT], I32, f0)
            wnT = [sb("wnT0", [P, N], scope=f0), sb("wnT1", [P, N], scope=f0)]
            fl = sem("fff_fl", f0)

            def fff_loads(sp):
                sp.dma_start(w1T[:, :], io["fff_w1T"]).then_inc(fl, 16)
                sp.dma_start(b1[:, :], io["fff_b1"]).then_inc(fl, 16)
                sp.dma_start(b2[0][:, :], io["fff_b2"][0:P, :]).then_inc(fl, 16)
                sp.dma_start(b2[1][:, :], io["fff_b2"][P:NODES, :]).then_inc(fl, 16)
                sp.wait_ge(fl, 64)
            layer_norm("l1f", fff_loads)

            with ExitStack() as s1, nc.Block() as block:
                on = sb("on_path", [P, NT, NODES], scope=s1)
                score = sb("fff_score", [P, NT, NODES], scope=s1)
                right = sb("go_right", [P, NT, NODES], scope=s1)
                rows = sb("fff_rows", [P, NT, RW], scope=s1)
                logit, alog, pw = (sb(f"fff_{k}", [P, NT, LEVELS], scope=s1) for k in ("logit", "alog", "pw"))
                leaf_i = sb("leaf_i", [P, LEAVES], I32, s1)
                leaf_f = sb("leaf_f", [P, LEAVES], scope=s1)
                before_a, before_b = (sb(f"before_{k}", [P, NT, LEAVES], scope=s1) for k in "ab")
                leaf_sum = sb("leaf_sum", [P, LEAVES], scope=s1)
                rank_f = sb("rank_f", [P, NT], scope=s1)
                s_mm, s_cp, h_turned, h_copied, step, path_done, g_in, g_out, cnt_done, w_set, wn_turned, wn_cp, iota_set, rank_set, tot_cp = (
                    sem(f"fff_{k}", s1) for k in ("s_mm", "s_cp", "h_turned", "h_copied", "step", "path_done", "g_in", "g_out",
                                                  "cnt_done", "w_set", "wn_turned", "wn_cp", "iota_set", "rank_set", "tot_cp"))
                sent = sem("fff_sent")

                @block.tensor
                def _(pe):
                    for i in range(NT):
                        out = bank[i // 2][:, (i % 2) * 256:(i % 2) * 256 + NODES]
                        pe.matmul(out, ones[0:1, :], b1[:, :], start=True, stop=False)
                        ins = pe.matmul(out, tile(hT, i), w1T[:, :], start=False, stop=True)
                        if i % 2:
                            ins.then_inc(s_mm, 1)
                    for q in range(4):
                        pe.wait_ge(s_cp, q + 1)
                        for i in range(4 * q, 4 * q + 4):
                            ins = pe.transpose(bank[q][:, (i % 4) * P:(i % 4 + 1) * P], tile(hT, i), ident[:, :])
                        ins.then_inc(h_turned, 1)
                    pe.wait_ge(path_done, 1)
                    pe.wait_ge(h_copied, 4)
                    pe.wait_ge(s_cp, NT // 2)
                    for c in range(4):
                        oh = level(on, LEVELS - 1)[:, 4 * c:4 * c + 4, :]
                        pe.matmul(bank[c][:, :].rearrange("p (t n) -> p t n", t=4), tri[:, :], oh, start=True, stop=True)
                        pe.matmul(bank[4 + c][:, :].rearrange("p (t n) -> p t n", t=4), ones[:, :], oh, start=True, stop=True)\
                          .then_inc(cnt_done, 1)
                    pe.wait_ge(w_set, 1)
                    pe.wait_ge(tot_cp, 1)
                    g = 0
                    for c in range(4):
                        for half, m in ((0, P), (1, NODES - P)):
                            if g >= 4:
                                pe.wait_ge(wn_cp, g - 3)
                            for i in range(4 * c, 4 * c + 4):
                                ins = pe.transpose(bank[4 + g % 4][0:m, (i % 4) * P:(i % 4 + 1) * P],
                                                   score[:, i, half * P:half * P + m], ident[:, :])
                            ins.then_inc(wn_turned, 1)
                            g += 1

                @block.scalar
                def _(act):
                    for q in range(4):
                        act.wait_ge(h_turned, q + 1)
                        act.copy(rows[:, 4 * q:4 * q + 4, 0:P], bank[q][:, :].rearrange("p (t d) -> p t d", t=4)).then_inc(h_copied, 1)
                    act.wait_ge(g_in, 1)
                    act.activation(pw[:, :, :], alog[:, :, :], ACT.Gelu).then_inc(g_out, 1)
                    g = 0
                    for c in range(4):
                        for half, m in ((0, P), (1, NODES - P)):
                            act.wait_ge(wn_turned, g + 1)
                            act.copy(wnT[half][0:m, c * CW:(c + 1) * CW], bank[4 + g % 4][0:m, :]).then_inc(wn_cp, 1)
                            g += 1

                @block.vector
                def _(dve):
                    link = Chain(dve, step)
                    for b in range(NT // 2):
                        dve.wait_ge(s_mm, b + 1)
                        dve.tensor_copy(score[:, 2 * b:2 * b + 2, :], bank[b][:, :].rearrange("p (t n) -> p t n", t=2)[:, :, 0:NODES])\
                           .then_inc(s_cp, 1)
                    dve.wait_ge(s_cp, NT // 2)
                    dve.memset(on[:, :, 0:1], 1.0)
                    link(dve.tensor_scalar(right[:, :, :], score[:, :, :], 0.0, None, ALU.is_gt))
                    for l in range(LEVELS - 1):
                        kids = level(on, l + 1).rearrange("p t (n s) -> p t n s", s=2)
                        link(dve.tensor_tensor(kids[:, :, :, 1], level(on, l), level(right, l), ALU.mult))
                        link(dve.tensor_tensor(kids[:, :, :, 0], level(on, l), kids[:, :, :, 1], ALU.subtract))
                    dve.sem_inc(path_done, 1)
                    link(dve.tensor_tensor(score[:, :, :], score[:, :, :], on[:, :, :], ALU.mult))
                    for l in range(LEVELS):
                        ins = dve.tensor_reduce(logit[:, :, l], level(score, l), AX, ALU.add)
                    link(ins)
                    dve.scalar_tensor_tensor(out=alog[:, :, :], in0=logit[:, :, :], scalar=-1.0, in1=logit[:, :, :],
                                             op0=ALU.mult, op1=ALU.max).then_inc(g_in, 1)
                    dve.wait_ge(iota_set, 2)
                    link(dve.tensor_copy(leaf_f[:, :], leaf_i[:, :]))
                    link(dve.tensor_tensor(before_a[:, :, :], level(on, LEVELS - 1),
                                           leaf_f[:, :].unsqueeze(1).broadcast_to([P, NT, LEAVES]), ALU.mult))
                    link(dve.tensor_reduce(rows[:, :, P + LEVELS], before_a[:, :, :], AX, ALU.add))
                    for c in range(4):
                        dve.wait_ge(cnt_done, c + 1)
                        ins = dve.tensor_copy(before_a[:, 4 * c:4 * c + 4, :], bank[4 + c][:, :].rearrange("p (t n) -> p t n", t=4))
                    link(ins)
                    src, dst = before_a, before_b
                    for sft in (1, 2, 4, 8):
                        dve.tensor_copy(dst[:, 0:sft, :], src[:, 0:sft, :])
                        link(dve.tensor_tensor(dst[:, sft:, :], src[:, sft:, :], src[:, :NT - sft, :], ALU.add))
                        src, dst = dst, src
                    link(dve.tensor_tensor_scan(leaf_sum[:, :], ones[:, :], src[:, NT - 1, :], 0.0, ALU.mult, ALU.add))
                    link(dve.tensor_tensor(leaf_sum[:, :], leaf_sum[:, :], src[:, NT - 1, :], ALU.subtract))
                    for c in range(4):
                        v = src[:, 4 * c:4 * c + 4, :]
                        link(dve.tensor_tensor(v, v, bank[4 + c][:, :].rearrange("p (t n) -> p t n", t=4), ALU.subtract))
                        ins = dve.tensor_tensor(v, v, bank[c][:, :].rearrange("p (t n) -> p t n", t=4), ALU.add)
                        link(ins)
                    dve.sem_inc(tot_cp, 1)
                    link(dve.tensor_tensor(src[:, :, :], src[:, :, :], leaf_sum[:, :].unsqueeze(1).broadcast_to([P, NT, LEAVES]), ALU.add))
                    link(dve.tensor_tensor(src[:, :, :], src[:, :, :], level(on, LEVELS - 1), ALU.mult))
                    link(dve.tensor_reduce(rank_f[:, :], src[:, :, :], AX, ALU.add))
                    dve.wait_ge(g_out, 1)
                    dve.tensor_copy(rows[:, :, P:P + LEVELS], pw[:, :, :])
                    dve.memset(rows[:, :, P + LEVELS + 1:RW], 0.0)
                    dve.tensor_scalar(rank[:, :], rank_f[:, :], 1.0, None, ALU.subtract).then_inc(rank_set, 1)
                    for l in range(LEVELS):
                        ins = dve.tensor_tensor(level(score, l), level(on, l),
                                                pw[:, :, l:l + 1].broadcast_to([P, NT, 2 ** l]), ALU.mult)
                    ins.then_inc(w_set, 1)

                @block.gpsimd
                def _(pool):
                    pool.iota(leaf_i[:, :], [[1, LEAVES]], base=0, channel_multiplier=0).then_inc(iota_set, 2)
                    pool.wait_ge(h_copied, 4)
                    pool.wait_ge(rank_set, 1)
                    for i in range(NT):
                        pool.indirect_dma_start(t_sorted[:, :], bass.IndirectOffsetOnAxis(ap=rank[:, i:i + 1], axis=0),
                                                rows[:, i, :], None).then_inc(sent, 16)
                    pool.wait_ge(sent, 16 * NT)

            f1 = f0.enter_context(ExitStack())
            scaled = sb("scaled", [P, LEVELS, N], scope=f1)
            node = sb("node", [P, LEVELS, N], BF16, f1)
            nrel = sb("nrel", [P, NP], scope=f1)
            col_x = sb("col_x", [1, NP], I32, f1)
            col_o = sb("col_o", [1, NP], I32, f1)
            n_abs = sb("n_abs", [1, NP], I32, f1)
            with ExitStack() as s2, nc.Block() as block:
                srt = sb("srt", [P, NT, RW], scope=s2)
                xsT = hT
                leaf_b = ring[:, 0, :].bitcast(I32)
                shifted = ring[:, 1:3, :].bitcast(I32)
                auxT = ring[0:9, 3, :]
                sel = sb("sel", [9, 9, P], scope=s2)
                leaf_t = sb("leaf_t", [NT, LEVELS + 1], scope=s2)
                reach_i = sb("reach_i", [NT, NP], I32, s2)
                reach = sb("reach", [NT, NP], scope=s2)
                skip0 = sb("skip0", [NT, P], scope=s2)
                pair_i = sb("pair_i", [P, NP], I32, s2)
                pair_f = sb("pair_f", [P, NP], scope=s2)
                add_x = sb("add_x", [1, NP], I32, s2)
                add_n = sb("add_n", [1, NP], I32, s2)
                tmp = sb("tab_tmp", [1, NP], scope=s2)
                t128 = sb("t128", [1, NP], scope=s2)
                rows_in, leaf_in, turned, aux_turned, cp, aux_cp, io_set, step, reach_set, tile_mm, spread, used_b, sh_set, sh_used, leaf_set = (
                    sem(f"srt_{k}", s2) for k in ("rows_in", "leaf_in", "turned", "aux_turned", "cp", "aux_cp", "io_set", "step", "reach_set",
                                                  "tile_mm", "spread", "used_b", "sh_set", "sh_used", "leaf_set"))

                @block.sync
                def _(sp):
                    sp.dma_start(leaf_t[:, :], t_sorted.rearrange("(t p) c -> t p c", p=P)[:, 0, P:P + LEVELS + 1]).then_inc(leaf_in, 16)
                    sp.dma_start(srt[:, :, :], t_sorted.rearrange("(t p) c -> p t c", p=P)).then_inc(rows_in, 16)
                    sp.wait_ge(rows_in, 16)

                @block.gpsimd
                def _(pool):
                    for l in range(LEVELS):
                        w = LEAVES >> l
                        at = slice(OFF[l], OFF[l] + PAIRS[l])
                        pool.iota(reach_i[:, at], [[w, PAIRS[l]]], base=w - 1, channel_multiplier=-w).then_inc(io_set, 1)
                        pool.iota(pair_i[:, at], [[1, PAIRS[l]]], base=0, channel_multiplier=0).then_inc(io_set, 1)
                        pool.iota(add_x[:, at], [[0, PAIRS[l]]], base=l * N, channel_multiplier=0).then_inc(io_set, 1)
                        pool.iota(add_n[:, at], [[0, PAIRS[l]]], base=2 ** l - 1, channel_multiplier=0).then_inc(io_set, 1)

                @block.tensor
                def _(pe):
                    pe.wait_ge(rows_in, 16)
                    for i in range(NT):
                        ins = pe.transpose(bank[i // 4][:, (i % 4) * P:(i % 4 + 1) * P], srt[:, i, 0:P], ident[:, :])
                        if i % 4 == 3:
                            ins.then_inc(turned, 1)
                        ins = pe.transpose(bank[4 + i // 4][0:9, (i % 4) * P:(i % 4 + 1) * P], srt[:, i, P:P + 9], ident[:, :])
                        if i % 4 == 3:
                            ins.then_inc(aux_turned, 1)
                    pe.wait_ge(reach_set, 1)
                    pe.wait_ge(cp, 1)
                    pe.matmul(bank[0][:, 0:NP], skip0[:, :], reach[:, :], start=True, stop=True).then_inc(tile_mm, 1)
                    pe.wait_ge(aux_cp, 4)
                    pe.wait_ge(io_set, 4 * LEVELS + 1)
                    for g in range(4 * 9):
                        l = 8 if g < 4 else g // 4 - 1
                        if g >= 4:
                            pe.wait_ge(used_b, g - 3)
                        pe.matmul(bank[4 + g % 4][:, :], sel[:, l, :], auxT[:, (g % 4) * CW:(g % 4 + 1) * CW],
                                  start=True, stop=True).then_inc(spread, 1)

                @block.scalar
                def _(act):
                    for q in range(4):
                        act.wait_ge(turned, q + 1)
                        act.copy(chunk(xsT, q), bank[q][:, :]).then_inc(cp, 1)
                        act.wait_ge(aux_turned, q + 1)
                        act.copy(auxT[:, q * CW:(q + 1) * CW], bank[4 + q][0:9, :]).then_inc(aux_cp, 1)
                    for l in range(LEVELS):
                        act.wait_ge(sh_set, min(l + 1, LEVELS - 1))
                        src = leaf_b[:, :] if l == LEVELS - 1 else shifted[:, l % 2, :]
                        act.copy(node[:, l, :], src).then_inc(sh_used, 1)

                @block.vector
                def _(dve):
                    link = Chain(dve, step)
                    for k in range(9):
                        ins = dve.tensor_scalar(sel[:, k, :], ones[0:9, :], ident[0:9, k:k + 1], None, ALU.mult)
                    ins.then_inc(io_set, 1)
                    link(dve.tensor_scalar(skip0[:, :], ones[0:NT, :], ident[0:NT, 0:1], None, ALU.subtract))
                    dve.wait_ge(leaf_in, 16)
                    dve.wait_ge(io_set, 4 * LEVELS + 1)
                    dve.tensor_scalar(reach[:, :], reach_i[:, :], leaf_t[:, LEVELS:LEVELS + 1], None, ALU.is_ge).then_inc(reach_set, 1)
                    link(dve.tensor_copy(pair_f[:, :], pair_i[:, :]))
                    dve.wait_ge(tile_mm, 1)
                    link(dve.tensor_tensor(nrel[:, :], pair_f[:, :], bank[0][:, 0:NP], ALU.subtract))
                    link(dve.tensor_scalar(t128[:, :], bank[0][0:1, 0:NP], float(P), None, ALU.mult))
                    dve.tensor_copy(col_o[:, :], t128[:, :])
                    dve.tensor_tensor(col_x[:, :], t128[:, :], add_x[:, :], ALU.add)
                    link(dve.tensor_tensor(tmp[:, :], nrel[0:1, :], add_n[:, :], ALU.add))
                    link(dve.tensor_scalar(n_abs[:, :], tmp[:, :], float(NODES - 1), None, ALU.min))
                    for q in range(4):
                        dve.wait_ge(spread, q + 1)
                        dve.tensor_copy(chunk(leaf_b, q), bank[4 + q][:, :]).then_inc(used_b, 1)
                    dve.wait_ge(used_b, 4)
                    dve.wait_ge(cp, 4)
                    for l in range(LEVELS):
                        if l < LEVELS - 1:
                            if l >= 2:
                                dve.wait_ge(sh_used, l - 1)
                            dve.tensor_scalar(shifted[:, l % 2, :], leaf_b[:, :], LEVELS - 1 - l, None, ALU.logical_shift_right).then_inc(sh_set, 1)
                        for q in range(4):
                            dve.wait_ge(spread, 4 * (l + 1) + q + 1)
                            dve.tensor_tensor(scaled[:, l, q * CW:(q + 1) * CW], chunk(xsT, q), bank[4 + q][:, :], ALU.mult).then_inc(used_b, 1)

            with ExitStack() as s3, nc.Block() as block:
                wt = sb("node_w", [P, WR, P], scope=s3)
                picked = sb("picked_tok", [P, WR, P], scope=s3)
                zero_w = sb("zero_w", [P, P], scope=s3)
                w_in = [sem(f"node_w_in{u}", s3) for u in range(WR)]
                pair_used, picked_set, z_set = sem("pair_used", s3), sem("picked_set", s3), sem("z_set", s3)

                @block.sync
                def _(sp):
                    with sp.Fori(0, NP // WR) as i:
                        for u in range(WR):
                            n = sp.value_load(n_abs[0:1, bass.ds(i * WR + u, 1)], min_val=0, max_val=NODES - 1)
                            sp.wait_ge(pair_used, i * WR + u + 1)
                            sp.dma_start(wt[:, u, :], io["fff_w2"][bass.ds(n, 1), :, :].rearrange("a d o -> (a d) o")).then_inc(w_in[u], 16)

                @block.vector
                def _(dve):
                    dve.memset(zero_w[:, :], 0.0).then_inc(z_set, 1)
                    with dve.Fori(0, NP // WR) as i:
                        for u in range(WR):
                            x = dve.value_load(col_x[0:1, bass.ds(i * WR + u, 1)], min_val=0, max_val=LEVELS * N - P)
                            dve.wait_ge(pair_used, i * WR + u + 1)
                            dve.scalar_tensor_tensor(out=picked[:, u, :], in0=node[:, :, :].rearrange("p l t -> p (l t)")[:, bass.ds(x, P)],
                                                     scalar=nrel[:, bass.ds(i * WR + u, 1)],
                                                     in1=scaled[:, :, :].rearrange("p l t -> p (l t)")[:, bass.ds(x, P)],
                                                     op0=ALU.is_equal, op1=ALU.mult).then_inc(picked_set, 1)

                @block.tensor
                def _(pe):
                    pe.wait_ge(z_set, 1)
                    for c in range(4):
                        ins = pe.matmul(bank[c][:, :], zero_w[:, :], scaled[:, 0, c * CW:(c + 1) * CW], start=True, stop=False)
                    ins.then_inc(pair_used, WR)
                    with pe.Fori(0, NP // WR) as i:
                        for u in range(WR):
                            o = pe.value_load(col_o[0:1, bass.ds(i * WR + u, 1)], min_val=0, max_val=N - P)
                            pe.wait_ge(w_in[u], i * 16 + 16)
                            pe.wait_ge(picked_set, i * WR + u + 1)
                            pe.matmul(psum[:, bass.ds(o, P)], wt[:, u, :], picked[:, u, :], start=False, stop=False,
                                      skip_group_check=True).then_inc(pair_used, 1)
                    for c in range(4):
                        pe.matmul(bank[c][:, :], zero_w[:, :], scaled[:, 0, c * CW:(c + 1) * CW], start=False, stop=True)
            f1.close()

            with ExitStack() as s4, nc.Block() as block:
                oT = sb("oT", [P, N], scope=s4)
                o_rows = sb("o_rows", [P, NT, P], scope=s4)
                back = sb("back", [P, NT, P], scope=s4)
                o_cp, o_turned, o_rcp, o_out, x_mm = (sem(f"unsort_{k}", s4) for k in ("o_cp", "o_turned", "o_rcp", "o_out", "x_mm"))
                fetched = [sem(f"unsort_in{q}") for q in range(4)]

                @block.scalar
                def _(act):
                    for c in range(4):
                        act.copy(chunk(oT, c), bank[c][:, :]).then_inc(o_cp, 1)

                @block.tensor
                def _(pe):
                    for c in range(4):
                        pe.wait_ge(o_cp, c + 1)
                        for i in range(4 * c, 4 * c + 4):
                            ins = pe.transpose(bank[4 + c][:, (i % 4) * P:(i % 4 + 1) * P], tile(oT, i), ident[:, :])
                        ins.then_inc(o_turned, 1)
                    for c in range(4):
                        pe.matmul(bank[c][:, :], b2[0][:, :], chunk(wnT[0], c), start=True, stop=False)
                        pe.matmul(bank[c][:, :], b2[1][:, :], wnT[1][0:NODES - P, c * CW:(c + 1) * CW], start=False, stop=False)
                        pe.wait_ge(fetched[c], 64)
                        for i in range(4 * c, 4 * c + 4):
                            ins = pe.matmul(bank[c][:, (i % 4) * P:(i % 4 + 1) * P], back[:, i, :], ident[:, :], start=False, stop=(i % 4 == 3))
                        ins.then_inc(x_mm, 1)

                @block.vector
                def _(dve):
                    for c in range(4):
                        dve.wait_ge(o_turned, c + 1)
                        dve.tensor_copy(o_rows[:, 4 * c:4 * c + 4, :].rearrange("p t d -> p (t d)"), bank[4 + c][:, :]).then_inc(o_rcp, 1)
                    for c in range(4):
                        dve.wait_ge(x_mm, c + 1)
                        dve.tensor_tensor(chunk(xT, c), chunk(xT, c), bank[c][:, :], ALU.add)

                @block.sync
                def _(sp):
                    sp.wait_ge(o_rcp, 4)
                    sp.dma_start(o_sorted.rearrange("(t p) d -> p t d", p=P), o_rows[:, :, :]).then_inc(o_out, 16)
                    sp.wait_ge(o_out, 16)

                @block.gpsimd
                def _(pool):
                    pool.wait_ge(o_out, 16)
                    for i in range(NT):
                        pool.indirect_dma_start(back[:, i, :], None, o_sorted[:, :],
                                                bass.IndirectOffsetOnAxis(ap=rank[:, i:i + 1], axis=0)).then_inc(fetched[i // 4], 16)

        clear_retired()
        gcn("l2g", 3 * NT, "l2_W", "l2_b", None)
        clear_retired()

        with ExitStack() as e0:
            BN_EPS = 0.001
            ew = sb("l2_ew", [P, E, 3 * P], scope=e0)
            bn = sb("l2_bn", [P, 10, E], scope=e0)
            wr = sb("l2_wr", [P, E], scope=e0)
            br = sb("l2_br", [P, NT, E], scope=e0)
            bo = sb("l2_bo", [E, P], scope=e0)
            scale_c = [sb(f"l2_scale{k}", [P, E], scope=e0) for k in range(2)]
            shift_c = [sb(f"l2_shift{k}", [P, E], scope=e0) for k in range(2)]
            bn_eps = sb("bn_eps", [P, 1], scope=e0)
            el = sem("l2_el", e0)

            def l2_loads(sp):
                for t, k in ((wr, "l2_Wr"), (br, "l2_br"), (bo, "l2_bo"), (bn, "l2_bn"), (ew, "l2_ew")):
                    sp.dma_start(t[tuple(slice(None) for _ in t.shape)], io[k]).then_inc(el, 16)
                sp.wait_ge(el, 80)
            layer_norm("l2f", l2_loads)

            with ExitStack() as s1, nc.Block() as block:
                lg, ex, wgt = (sb(f"l2_{k}", [P, NT, E], scope=s1) for k in ("lg", "ex", "wgt"))
                mx, den = (sb(f"l2_{k}", [P, NT], scope=s1) for k in ("mx", "den"))
                wT = sb("l2_wT", [E, N], scope=s1)
                h1 = sb("l2_h1", [P, 2, CW], scope=s1)
                h2 = sb("l2_h2", [P, 2, CW], scope=s1)
                acc = sb("l2_acc", [P, NT, P], scope=s1)
                root = [sb(f"l2_root{k}", [P, E], scope=s1) for k in range(2)]
                eps_set, lg_done, ex_in, ex_out, step, root_set, aff_set, mm1, mm2, mm3, ac1, ac2, acc_used, w_set, w_turned, wT_set, out_mm, acc_done = (
                    sem(f"l2_{k}", s1) for k in ("eps_set", "lg_done", "ex_in", "ex_out", "step", "root_set", "aff_set", "mm1", "mm2", "mm3",
                                                 "ac1", "ac2", "acc_used", "w_set", "w_turned", "wT_set", "out_mm", "acc_done"))
                ITS = E * NC

                @block.gpsimd
                def _(pool):
                    pool.memset(bn_eps[:, :], BN_EPS).then_inc(eps_set, 1)

                @block.tensor
                def _(pe):
                    for i in range(NT):
                        ins = pe.matmul(bank[6][:, E * i:E * i + E], tile(hT, i), wr[:, :], start=True, stop=True)
                    ins.then_inc(lg_done, 1)

                    def first(it):
                        e, c = it // NC, it % NC
                        if it >= 2:
                            pe.wait_ge(ac1, it - 1)
                        pe.matmul(bank[it % 2][:, :], ew[:, e, 0:P], chunk(hT, c), start=True, stop=True).then_inc(mm1, 1)

                    def second(it):
                        pe.wait_ge(ac1, it + 1)
                        if it >= 2:
                            pe.wait_ge(ac2, it - 1)
                        pe.matmul(bank[2 + it % 2][:, :], ew[:, it // NC, P:2 * P], h1[:, it % 2, :], start=True, stop=True).then_inc(mm2, 1)

                    def third(it):
                        pe.wait_ge(ac2, it + 1)
                        if it >= 2:
                            pe.wait_ge(acc_used, it - 1)
                        for i in range(4):
                            ins = pe.matmul(bank[4 + it % 2][:, i * P:(i + 1) * P], h2[:, it % 2, i * P:(i + 1) * P],
                                            ew[:, it // NC, 2 * P:3 * P], start=True, stop=True)
                        ins.then_inc(mm3, 1)
                    for it in range(ITS + 2):
                        if it < ITS:
                            first(it)
                        if 1 <= it <= ITS:
                            second(it - 1)
                        if it >= 2:
                            third(it - 2)
                    pe.wait_ge(w_set, 1)
                    for i in range(NT):
                        if i == 8:
                            pe.wait_ge(wT_set, 1)
                        if i % 4 == 0 and i >= 8:
                            pe.wait_ge(wT_set, i // 4 - 1)
                        ins = pe.transpose(bank[6 + i // 4 % 2][0:E, (i % 4) * P:(i % 4 + 1) * P], wgt[:, i, :], ident[:, :])
                        if i % 4 == 3:
                            ins.then_inc(w_turned, 1)
                    pe.wait_ge(wT_set, 4)
                    pe.wait_ge(acc_done, 1)
                    for c in range(NC):
                        pe.matmul(bank[c][:, :], bo[:, :], wT[:, c * CW:(c + 1) * CW], start=True, stop=False)
                        for i in range(4):
                            ins = pe.matmul(bank[c][:, i * P:(i + 1) * P], acc[:, 4 * c + i, :], ident[:, :], start=False, stop=(i == 3))
                        ins.then_inc(out_mm, 1)

                @block.scalar
                def _(act):
                    act.wait_ge(eps_set, 1)
                    for k in range(2):
                        act.activation(root[k][:, :], bn[:, 5 * k + 4, :], ACT.Sqrt, bias=bn_eps[:, 0:1]).then_inc(root_set, 1)
                    act.wait_ge(ex_in, 1)
                    act.activation(ex[:, :, :], ex[:, :, :], ACT.Exp).then_inc(ex_out, 1)
                    act.wait_ge(aff_set, 2)
                    for it in range(ITS + 1):
                        if it < ITS:
                            e = it // NC
                            act.wait_ge(mm1, it + 1)
                            if it >= 2:
                                act.wait_ge(mm2, it - 1)
                            act.activation(h1[:, it % 2, :], bank[it % 2][:, :], ACT.Relu,
                                           bias=shift_c[0][:, e:e + 1], scale=scale_c[0][:, e:e + 1]).then_inc(ac1, 1)
                        if it >= 1:
                            e = (it - 1) // NC
                            act.wait_ge(mm2, it)
                            if it >= 3:
                                act.wait_ge(mm3, it - 2)
                            act.activation(h2[:, (it - 1) % 2, :], bank[2 + (it - 1) % 2][:, :], ACT.Relu,
                                           bias=shift_c[1][:, e:e + 1], scale=scale_c[1][:, e:e + 1]).then_inc(ac2, 1)
                    for q in range(4):
                        act.wait_ge(w_turned, q + 1)
                        act.copy(wT[:, q * CW:(q + 1) * CW], bank[6 + q % 2][0:E, :]).then_inc(wT_set, 1)

                @block.vector
                def _(dve):
                    link = Chain(dve, step)

                    def over_e(t):
                        return t[:, :].unsqueeze(2).broadcast_to([P, NT, E])
                    dve.wait_ge(lg_done, 1)
                    link(dve.tensor_tensor(lg[:, :, :], bank[6][:, 0:P].rearrange("p (t e) -> p t e", e=E), br[:, :, :], ALU.add))
                    link(dve.tensor_reduce(mx[:, :], lg[:, :, :], AX, ALU.max))
                    dve.tensor_tensor(ex[:, :, :], lg[:, :, :], over_e(mx), ALU.subtract).then_inc(ex_in, 1)
                    dve.wait_ge(root_set, 2)
                    for k in range(2):
                        b, g_, be, m = (bn[:, 5 * k + i, :] for i in range(4))
                        link(dve.reciprocal(root[k][:, :], root[k][:, :]))
                        link(dve.tensor_tensor(scale_c[k][:, :], root[k][:, :], g_, ALU.mult))
                        link(dve.tensor_tensor(shift_c[k][:, :], b, m, ALU.subtract))
                        link(dve.tensor_tensor(shift_c[k][:, :], shift_c[k][:, :], scale_c[k][:, :], ALU.mult))
                        dve.tensor_tensor(shift_c[k][:, :], shift_c[k][:, :], be, ALU.add).then_inc(aff_set, 1)
                    dve.wait_ge(ex_out, 1)
                    link(dve.tensor_reduce(den[:, :], ex[:, :, :], AX, ALU.add))
                    link(dve.reciprocal(den[:, :], den[:, :]))
                    dve.tensor_tensor(wgt[:, :, :], ex[:, :, :], over_e(den), ALU.mult).then_inc(w_set, 1)
                    dve.wait_ge(w_set, 1)
                    for it in range(ITS):
                        e, c = it // NC, it % NC
                        dve.wait_ge(mm3, it + 1)
                        if e >= 1:
                            dve.wait_ge(acc_used, it - NC + 1)
                        for i in range(4):
                            t = 4 * c + i
                            src = bank[4 + it % 2][:, i * P:(i + 1) * P]
                            if e == 0:
                                ins = dve.tensor_scalar(acc[:, t, :], src, wgt[:, t, e:e + 1], None, ALU.mult)
                            else:
                                ins = dve.scalar_tensor_tensor(out=acc[:, t, :], in0=src, scalar=wgt[:, t, e:e + 1], in1=acc[:, t, :],
                                                               op0=ALU.mult, op1=ALU.add)
                        ins.then_inc(acc_used, 1)
                    dve.wait_ge(acc_used, ITS)
                    dve.sem_inc(acc_done, 1)
                    for c in range(NC):
                        dve.wait_ge(out_mm, c + 1)
                        dve.tensor_tensor(chunk(xT, c), chunk(xT, c), bank[c][:, :], ALU.add)
        clear_retired()

        gcn("l3g", 4 * NT, "l3_W", "l3_b", 1.0)
        clear_retired()

        H8, KEYS, TOP = 8, 128, 16
        DK = P // 2
        INV_SQRT = float(P) ** -0.5
        with ExitStack() as p0:
            SLOTS = 4
            half_w = sb("half_w", [DK, H8 * 2, P], scope=p0)
            half_k = sb("half_k", [DK, H8 * 2, KEYS], scope=p0)
            key_map = sb("key_map", [P, H8 + 1, 2 * KEYS], scope=p0)
            wq = sb("wq", [P, P], scope=p0)
            wo = sb("wo", [P, H8 + 1, P], scope=p0)
            qT, kT, prob = (ring[:, k, :] for k in range(3))
            probT = ring[:, 3, :].rearrange("p (t d) -> p t d", t=NT)
            yacc = sb("yacc", [P, NT, P], scope=p0)
            rows = sb("table_rows", [P, SLOTS, TOP, 2 * P], scope=p0)
            oT = sb("attn_oT", [P, P], scope=p0)
            r2 = sb("r2", [P, 2, 2], scope=p0)
            causal = sb("causal", [P, P], scope=p0)
            iota16_i = sb("iota16_i", [P, 16], I32, p0)
            iota16 = sb("iota16", [P, 16], BF16, p0)
            pl = sem("pk_loaded", p0)

            def pk_loads(sp):
                sp.dma_start(half_w[:, :, :], io["pk_w"]).then_inc(pl, 16)
                sp.dma_start(half_k[:, :, :], io["pk_k"]).then_inc(pl, 16)
                sp.dma_start(wo[:, 1:H8 + 1, :], io["pk_wo"]).then_inc(pl, 16)
                sp.wait_ge(pl, 48)
            layer_norm("l3f", pk_loads)
            kv = sb("kv", [P, 2, NT, 2 * P], scope=p0)

            with ExitStack() as s1, nc.Block() as block:
                map_mm, map_cp, c_set = (sem(f"pk_{k}", s1) for k in ("map_mm", "map_cp", "c_set"))

                @block.tensor
                def _(pe):
                    for k in range(2 * H8):
                        ins = pe.matmul(bank[k // 4][:, (k % 4) * P:(k % 4 + 1) * P], half_w[:, k, :], half_k[:, k, :], start=True, stop=True)
                        if k % 4 == 3:
                            ins.then_inc(map_mm, 1)

                @block.scalar
                def _(act):
                    for q in range(4):
                        act.wait_ge(map_mm, q + 1)
                        act.copy(key_map[:, 2 * q:2 * q + 2, :].rearrange("p h k -> p (h k)"), bank[q][:, :]).then_inc(map_cp, 1)
                    act.copy(key_map[:, H8, :], bank[0][:, 0:2 * KEYS])

                @block.gpsimd
                def _(pool):
                    pool.memset(yacc[:, :, :], 0.0)
                    pool.memset(kv[:, 1, :, :], 0.0)
                    pool.memset(causal[:, :], 0.0).then_inc(c_set, 1)
                    pool.iota(iota16_i[:, :], [[1, 16]], base=0, channel_multiplier=0).then_inc(c_set, 1)
                    pool.wait_ge(c_set, 2)
                    pool.affine_select(out=causal[:, :], in_=causal[:, :], compare_op=ALU.is_ge, fill=-1e30,
                                       base=0, pattern=[[-1, P]], channel_multiplier=1)

                @block.vector
                def _(dve):
                    dve.memset(qT[:, :], 0.0)
                    dve.memset(kT[:, :], 0.0)
                    dve.memset(oT[:, :], 0.0)
                    dve.memset(wo[:, 0, :], 0.0)
                    dve.memset(r2[:, :, :], 1.0)
                    dve.wait_ge(c_set, 2)
                    dve.tensor_copy(iota16[:, :], iota16_i[:, :])

            with ExitStack() as s2, nc.Block() as block:
                sims = sb("sims", [P, 2, 2 * KEYS], scope=s2)
                rest = sb("sims_rest", [P, 2 * KEYS], scope=s2)
                top = sb("top16", [P, 2, TOP], scope=s2)
                top_i = sb("top16_i", [P, 2, TOP], mybir.dt.uint32, s2)
                tab = sb("pick_tab", [P, 2, TOP], BF16, s2)
                pair = sb("pair_score", [P, TOP, TOP], scope=s2)
                pair_rest = sb("pair_rest", [P, TOP * TOP], scope=s2)
                best = sb("best16", [P, 2, TOP], scope=s2)
                best_i = sb("best16_i", [P, TOP], mybir.dt.uint32, s2)
                ij_i = sb("ij_i", [P, 2, TOP], mybir.dt.uint32, s2)
                ij = sb("ij", [P, 2, TOP], BF16, s2)
                hot = sb("hot", [P, TOP, 2, TOP], BF16, s2)
                row_f = sb("row_f", [P, TOP], scope=s2)
                head_base = sb("head_base", [P, 1], scope=s2)
                neg_top = sb("neg_top", [P, 2], scope=s2)
                e16 = sb("e16", [P, 2, TOP], scope=s2)
                e_sum = sb("e_sum", [P, 2], scope=s2)
                w16 = sb("w16", [P, SLOTS, TOP], scope=s2)
                row_i = sb("row_i", [P, SLOTS, TOP], I32, s2)
                s_diag = sb("s_diag", [P, P], scope=s2)
                m2 = sb("m2", [P, 2], scope=s2)
                neg_m = sb("neg_m", [P, 1], scope=s2)
                r1 = sb("r1", [P, 1], scope=s2)
                names = ("sim_mm", "sim_cp", "sim_read", "tk_in", "tk_out", "idx_ready", "ws_done", "wq_in", "q_mm", "q_cp",
                         "kt_mm", "kt_cp", "s_mm", "mx", "exd", "tr_mm", "pt_cp", "pv", "o_cp", "y_mm", "y_acc", "dstep", "act_step")
                S = {k: sem("at_" + k, s2) for k in names}
                rows_in = [sem(f"rows_in{u}") for u in range(SLOTS)]

                def banks_of(t):
                    return t // 4 + 1
                BANKS = sum(banks_of(t) for t in range(NT))

                def banks_before(t):
                    return sum(banks_of(k) for k in range(t))

                ROUND = 2 * NT

                def place(c):
                    return c // NT, c // NT % 2, c % NT

                def bank_no(r, c):
                    return (2 * r + c // NT) * BANKS + banks_before(c % NT) + 2 * banks_of(NT - 1)

                @block.sync
                def _(sp):
                    with sp.Fori(0, H8) as h:
                        sp.wait_ge(S["q_mm"], h * 4 + 4)
                        sp.dma_start(wq[:, :], io["pk_wq"][bass.ds(h, 1), :, :].rearrange("a d o -> (a d) o")).then_inc(S["wq_in"], 16)

                @block.gpsimd
                def _(pool):
                    with pool.Fori(0, H8) as h:
                        for t in range(NT):
                            pool.wait_ge(S["idx_ready"], h * NT + t + 1)
                            pool.wait_ge(S["ws_done"], h * NT + t + 1)
                            pool.nop(nofuse=True)
                            for k in range(TOP):
                                pool.indirect_dma_start(rows[:, t % SLOTS, k, :], None, io["tables"],
                                                        bass.IndirectOffsetOnAxis(ap=row_i[:, t % SLOTS, k:k + 1], axis=0)).then_inc(rows_in[t % SLOTS], 16)

                @block.tensor
                def _(pe):
                    def sim(r, c):
                        head, _, t = place(c)
                        pe.wait_ge(S["sim_cp"], r * ROUND + c + 1)
                        pe.matmul(bank[4][:, 0:2 * KEYS], tile(hT, t), key_map[:, bass.ds(r * 2 + head, 1), :].rearrange("p a k -> p (a k)"),
                                  start=True, stop=True).then_inc(S["sim_mm"], 1)

                    def scores(c):
                        t = c % NT
                        for b in range(banks_of(t)):
                            w = min(CW, (t + 1) * P - b * CW)
                            ins = pe.matmul(bank[b][:, 0:w], tile(qT, t), kT[:, b * CW:b * CW + w], start=True, stop=True)
                        ins.then_inc(S["s_mm"], 1)

                    def queries(r, head):
                        pe.wait_ge(S["wq_in"], r * 32 + head * 16 + 16)
                        for c in range(NC):
                            pe.matmul(bank[c][:, :], wq[:, :], chunk(hT, c), start=True, stop=True).then_inc(S["q_mm"], 1)

                    def keys_and_scores(r, c):
                        _, half, t = place(c)
                        pe.wait_ge(S["ws_done"], r * ROUND + c + SLOTS + 1)
                        pe.wait_ge(S["sim_cp"], r * ROUND + c + 7)
                        pe.transpose(bank[4][:, 2 * KEYS:2 * KEYS + P], kv[:, half, t, 0:P], ident[:, :]).then_inc(S["kt_mm"], 1)
                        pe.wait_ge(S["kt_cp"], r * ROUND + c + 2)
                        if t == 0:
                            pe.wait_ge(S["q_cp"], r * 8 + c // NT * 4 + 4)
                        scores(c)

                    def output(r, c):
                        head, half, t = place(c)
                        for b in range(banks_of(t)):
                            pe.wait_ge(S["pt_cp"], bank_no(r, c) + b + 1)
                            for j in range(4 * b, min(4 * b + 4, t + 1)):
                                ins = pe.transpose(bank[5 + (banks_before(t) + b) % 2][:, (j % 4) * P:(j % 4 + 1) * P], tile(prob, j), ident[:, :])
                            ins.then_inc(S["tr_mm"], 1)
                        pe.wait_ge(S["pt_cp"], bank_no(r, c) + banks_of(t) + 2)
                        pe.wait_ge(S["y_acc"], r * ROUND + c + 3)
                        for j in range(t + 1):
                            ins = pe.matmul(bank[7][:, P:2 * P], kv[:, half, j, P:2 * P], probT[:, j, :], start=(j == 0), stop=(j == t))
                        ins.then_inc(S["pv"], 1)
                        pe.wait_ge(S["o_cp"], r * ROUND + c + 3)
                        pe.matmul(bank[7][:, 2 * P:3 * P], oT[:, :], wo[:, bass.ds(r * 2 + head + 1, 1), :].rearrange("p a o -> p (a o)"),
                                  start=True, stop=True).then_inc(S["y_mm"], 1)

                    pe.matmul(bank[7][:, 2 * P:3 * P], oT[:, :], wo[:, 0, :], start=True, stop=True).then_inc(S["y_mm"], 1)
                    scores(-2)
                    pe.sem_inc(S["q_mm"], 4)
                    for n in range(5):
                        sim(0, n)
                    with pe.Fori(0, H8 // 2) as r:
                        for c in range(ROUND):
                            pe.wait_ge(S["exd"], r * ROUND + c + 1)
                            if c % NT == 1:
                                queries(r, c // NT)
                            keys_and_scores(r, c - 1)
                            sim(r, c + 5)
                            output(r, c - 2)
                    pe.wait_ge(S["exd"], H8 * NT + 1)
                    keys_and_scores(H8 // 2, -1)
                    output(H8 // 2, -2)
                    pe.wait_ge(S["exd"], H8 * NT + 2)
                    output(H8 // 2, -1)

                @block.scalar
                def _(act):
                    def copy_sims(r, c):
                        act.wait_ge(S["sim_mm"], r * ROUND + c + 1)
                        act.wait_ge(S["sim_read"], r * ROUND + c + 1)
                        act.copy(sims[:, c % 2, :], bank[4][:, 0:2 * KEYS]).then_inc(S["sim_cp"], 1)

                    def softmax16(r, c):
                        act.wait_ge(S["tk_in"], r * ROUND + c + 1)
                        act.activation(e16[:, c % 2, :], best[:, c % 2, :], ACT.Exp, bias=neg_top[:, c % 2:c % 2 + 1],
                                       accum_out=e_sum[:, c % 2:c % 2 + 1]).then_inc(S["tk_out"], 1)

                    def exponentials(r, c):
                        t = c % NT
                        act.wait_ge(S["mx"], r * ROUND + c + 3)
                        if t > 0:
                            act.activation(prob[:, 0:t * P], psum[:, 0:t * P], ACT.Exp, bias=neg_m[:, 0:1], accum_out=r2[:, c % 2, 0:1])
                        act.activation(tile(prob, t), s_diag[:, :], ACT.Exp, bias=neg_m[:, 0:1], accum_out=r2[:, c % 2, 1:2]).then_inc(S["exd"], 1)

                    def copy_keys(r, c):
                        act.wait_ge(S["kt_mm"], r * ROUND + c + 2)
                        act.copy(tile(kT, c % NT), bank[4][:, 2 * KEYS:2 * KEYS + P]).then_inc(S["kt_cp"], 1)

                    def output(r, c):
                        t = c % NT
                        for b in range(banks_of(t)):
                            w = min(4, t + 1 - 4 * b)
                            act.wait_ge(S["tr_mm"], bank_no(r, c) + b + 1)
                            act.copy(probT[:, 4 * b:4 * b + w, :].rearrange("p t d -> p (t d)"),
                                     bank[5 + (banks_before(t) + b) % 2][:, 0:w * P]).then_inc(S["pt_cp"], 1)
                        act.wait_ge(S["pv"], r * ROUND + c + 3)
                        act.copy(oT[:, :], bank[7][:, P:2 * P]).then_inc(S["o_cp"], 1)

                    act.sem_inc(S["sim_cp"], 1)
                    act.sem_inc(S["pt_cp"], 2)
                    for n in range(5):
                        copy_sims(0, n)
                        if n >= 2:
                            softmax16(0, n - 2)
                    with act.Fori(0, H8 // 2) as r:
                        for c in range(ROUND):
                            softmax16(r, c + 3)
                            exponentials(r, c - 2)
                            if c % NT == 1:
                                for q in range(NC):
                                    act.wait_ge(S["q_mm"], r * 8 + c // NT * 4 + 5 + q)
                                    act.mul(chunk(qT, q), bank[q][:, :], INV_SQRT).then_inc(S["q_cp"], 1)
                            copy_keys(r, c - 1)
                            copy_sims(r, c + 5)
                            output(r, c - 2)
                    exponentials(H8 // 2, -2)
                    copy_keys(H8 // 2, -1)
                    output(H8 // 2, -2)
                    exponentials(H8 // 2, -1)
                    output(H8 // 2, -1)

                @block.vector
                def _(dve):
                    K = {"n": 0, "sum": 0}

                    def done(ins):
                        K["n"] += 1
                        ins.then_inc(S["dstep"], 1)
                        return K["n"]

                    def after(step_no):
                        dve.wait_ge(S["dstep"], step_no)

                    def add_pick(r, c, k):
                        _, half, t = place(c)
                        row, w, acc = rows[:, t % SLOTS, k, :], w16[:, t % SLOTS, k:k + 1], kv[:, half, t, :]
                        if k == 0:
                            dve.wait_ge(rows_in[t % SLOTS], r * (ROUND // SLOTS * TOP * 16) + (c // SLOTS + 1) * TOP * 16)
                            K["sum"] = done(dve.tensor_scalar(acc, row, w, None, ALU.mult))
                            return
                        after(K["sum"])
                        ins = dve.scalar_tensor_tensor(out=acc, in0=row, scalar=w, in1=acc, op0=ALU.mult, op1=ALU.add)
                        if k < TOP - 1:
                            K["sum"] = done(ins)
                        else:
                            ins.then_inc(S["ws_done"], 1)

                    def topk(r, c, pick):
                        slot, b = c % SLOTS, best[:, c % 2, :]
                        v = [sims[:, c % 2, p * KEYS:(p + 1) * KEYS] for p in range(2)]
                        u = [rest[:, p * KEYS:(p + 1) * KEYS] for p in range(2)]
                        if c % NT == 0:
                            after(done(dve.tensor_scalar(head_base[:, :], head_base[:, :], float(KEYS * KEYS), None, ALU.add)))
                        dve.wait_ge(S["sim_cp"], r * ROUND + c + 2)
                        dve.nop(nofuse=True)
                        first = [done(dve.max(top[:, p, 0:8], v[p])) for p in range(2)]
                        cut = []
                        for p in range(2):
                            after(first[p])
                            dve.max_index(top_i[:, p, 0:8], top[:, p, 0:8], v[p])
                            cut.append(done(dve.match_replace(u[p], top[:, p, 0:8], v[p], -3.0e38)))
                        second = []
                        for p in range(2):
                            after(cut[p])
                            second.append(done(dve.max(top[:, p, 8:16], u[p])))
                        after(second[0])
                        dve.max_index(top_i[:, 0, 8:16], top[:, 0, 8:16], u[0]).then_inc(S["sim_read"], 1)
                        after(second[1])
                        summed = done(dve.tensor_tensor(pair[:, :, :], top[:, 0, :].unsqueeze(2).broadcast_to([P, TOP, TOP]),
                                                        top[:, 1, :].unsqueeze(1).broadcast_to([P, TOP, TOP]), ALU.add))
                        dve.max_index(top_i[:, 1, 8:16], top[:, 1, 8:16], u[1])
                        flat = pair[:, :, :].rearrange("p a b -> p (a b)")
                        after(summed)
                        first = done(dve.max(b[:, 0:8], flat))
                        dve.tensor_copy(tab[:, 0, :], top_i[:, 0, :])
                        after(first)
                        dve.max_index(best_i[:, 0:8], b[:, 0:8], flat)
                        cut = done(dve.match_replace(pair_rest[:, :], b[:, 0:8], flat, -3.0e38))
                        dve.tensor_scalar(tab[:, 1, :], top_i[:, 1, :], float(KEYS), None, ALU.mult)
                        after(cut)
                        second = done(dve.max(b[:, 8:16], pair_rest[:, :]))
                        pick(0)
                        after(second)
                        dve.tensor_scalar(neg_top[:, c % 2:c % 2 + 1], b[:, 0:1], -1.0, None, ALU.mult).then_inc(S["tk_in"], 1)
                        placed = done(dve.max_index(best_i[:, 8:16], b[:, 8:16], pair_rest[:, :]))
                        pick(1)
                        after(placed)
                        dve.tensor_scalar(ij_i[:, 0, :], best_i[:, :], 4, None, ALU.logical_shift_right)
                        split = done(dve.tensor_scalar(ij_i[:, 1, :], best_i[:, :], TOP - 1, None, ALU.bitwise_and))
                        pick(2)
                        after(split)
                        split = done(dve.tensor_copy(ij[:, :, :], ij_i[:, :, :]))
                        pick(3)
                        after(split)
                        for s_ in range(2):
                            ins = dve.tensor_tensor(hot[:, :, s_, :], iota16[:, :].unsqueeze(1).broadcast_to([P, TOP, TOP]),
                                                    ij[:, s_, :].unsqueeze(2).broadcast_to([P, TOP, TOP]), ALU.is_equal)
                        marked = done(ins)
                        pick(4)
                        hv = hot[:, :, :, :].rearrange("p k s i -> p k (s i)")
                        after(marked)
                        valued = done(dve.tensor_tensor(hv, hv, tab[:, :, :].rearrange("p s i -> p (s i)").unsqueeze(1).broadcast_to([P, TOP, 2 * TOP]), ALU.mult))
                        pick(5)
                        after(valued)
                        found = done(dve.tensor_reduce(row_f[:, :], hv, AX, ALU.add))
                        pick(6)
                        after(found)
                        dve.tensor_scalar(row_i[:, slot, :], row_f[:, :], head_base[:, 0:1], None, ALU.add).then_inc(S["idx_ready"], 1)

                    def weights(r, c, pick):
                        e = e_sum[:, c % 2:c % 2 + 1]
                        dve.wait_ge(S["tk_out"], r * ROUND + c + 1)
                        inverted = done(dve.reciprocal(e, e))
                        pick(8)
                        after(inverted)
                        return done(dve.tensor_scalar(w16[:, c % SLOTS, :], e16[:, c % 2, :], e, None, ALU.mult))

                    def row_max(r, c, pick):
                        t = c % NT
                        dve.wait_ge(S["s_mm"], r * ROUND + c + 3)
                        masked = done(dve.tensor_tensor(s_diag[:, :], psum[:, t * P:(t + 1) * P], causal[:, :], ALU.add))
                        if t > 0:
                            dve.tensor_reduce(m2[:, 0:1], psum[:, 0:t * P], AX, ALU.max)
                        pick(10)
                        after(masked)
                        reduced = done(dve.tensor_reduce(m2[:, 1:2], s_diag[:, :], AX, ALU.max))
                        pick(11)
                        after(reduced)
                        if t > 0:
                            ins = dve.tensor_scalar(neg_m[:, :], m2[:, 0:1], m2[:, 1:2], -1.0, ALU.max, ALU.mult)
                        else:
                            ins = dve.tensor_scalar(neg_m[:, :], m2[:, 1:2], -1.0, None, ALU.mult)
                        ins.then_inc(S["mx"], 1)

                    def add_out(r, c, pick):
                        t, q = c % NT, r2[:, c % 2, :]
                        dve.wait_ge(S["y_mm"], r * ROUND + c + 4)
                        if t > 0:
                            total = done(dve.tensor_tensor(r1[:, :], q[:, 0:1], q[:, 1:2], ALU.add))
                        else:
                            total = done(dve.tensor_copy(r1[:, :], q[:, 1:2]))
                        pick(13)
                        after(total)
                        inverted = done(dve.reciprocal(r1[:, :], r1[:, :]))
                        pick(14)
                        after(inverted)
                        dve.scalar_tensor_tensor(out=yacc[:, t, :], in0=bank[7][:, 2 * P:3 * P], scalar=r1[:, 0:1], in1=yacc[:, t, :],
                                                 op0=ALU.mult, op1=ALU.add).then_inc(S["y_acc"], 1)

                    def no_pick(k):
                        pass

                    dve.sem_inc(S["sim_read"], 2)
                    dve.sem_inc(S["ws_done"], SLOTS)
                    after(done(dve.memset(head_base[:, :], -float(KEYS * KEYS))))
                    for n in range(3):
                        topk(0, n, no_pick)
                        if n < 2:
                            after(weights(0, n, no_pick))
                    with dve.Fori(0, H8 // 2) as r:
                        dve.sem_clear(S["dstep"])
                        K["n"] = 0
                        for c in range(ROUND):
                            def pick(k):
                                add_pick(r, c, k)
                            topk(r, c + 3, pick)
                            pick(7)
                            weights(r, c + 2, pick)
                            pick(9)
                            row_max(r, c - 2, pick)
                            pick(12)
                            add_out(r, c - 3, pick)
                            pick(15)
                    end = H8 // 2
                    row_max(end, -2, no_pick)
                    add_out(end, -3, no_pick)
                    row_max(end, -1, no_pick)
                    add_out(end, -2, no_pick)
                    add_out(end, -1, no_pick)

            with ExitStack() as s3, nc.Block() as block:
                turned = sem("fin_turned", s3)

                @block.tensor
                def _(pe):
                    for i in range(NT):
                        ins = pe.transpose(bank[i // 4][:, (i % 4) * P:(i % 4 + 1) * P], yacc[:, i, :], ident[:, :])
                        if i % 4 == 3:
                            ins.then_inc(turned, 1)

                @block.vector
                def _(dve):
                    for c in range(NC):
                        dve.wait_ge(turned, c + 1)
                        dve.tensor_tensor(chunk(xT, c), chunk(xT, c), bank[c][:, :], ALU.add)

        with nc.Block() as block:
            stored = sem("stored")

            @block.sync
            def _(sp):
                sp.dma_start(io["outT"], xT[:, :]).then_inc(stored, 16)
                sp.wait_ge(stored, 16)


def layouts(np, v):
    out = {"xT": v["x"].T, "adjT": v["adj"].T}
    out["gat_W"] = v["L0_gnn_gat_W"]
    out["gat_wT"] = v["L0_gnn_gat_W"].transpose(2, 0, 1)
    out["gat_a"] = v["L0_gnn_gat_a"].reshape(3, 2, 128).transpose(2, 0, 1)
    for kind in ("edge", "node"):
        for m in ("ih", "hh"):
            out[f"{kind}_W{m}T"] = v[f"L0_gnn_{kind}_W{m}"].T
            out[f"{kind}_b{m}"] = v[f"L0_gnn_{kind}_b{m}"].reshape(3, 128).T
    E = 8
    out["gate_w"] = v["L0_ffn_gate_w"]
    out["gate_b"] = np.broadcast_to(v["L0_ffn_gate_b"], (128, 16, E))
    out["moe_w"] = np.concatenate([
        v["L0_ffn_w1"],
        v["L0_ffn_w2"].reshape(E, 4, 128, 128).transpose(0, 2, 1, 3).reshape(E, 128, 512),
        v["L0_ffn_b1"].reshape(E, 4, 128).transpose(0, 2, 1)], axis=2)
    out["moe_b2"] = v["L0_ffn_b2"].reshape(1, -1)
    out["fff_w1T"] = v["L1_ffn_w1s"].T
    out["fff_b1"] = v["L1_ffn_b1s"].reshape(1, -1)
    out["fff_b2"] = v["L1_ffn_b2s"]
    out["fff_w2"] = v["L1_ffn_w2s"]
    out["l2_W"] = v["L2_gnn_W"]
    out["l2_b"] = v["L2_gnn_b"].reshape(-1, 1)
    out["l2_Wr"] = v["L2_ffn_Wr"]
    out["l2_br"] = np.broadcast_to(v["L2_ffn_br"], (128, 16, E))
    out["l2_bo"] = v["L2_ffn_bo"]
    out["l2_bn"] = np.stack([v[f"L2_ffn_{k}{n}"].T for n in (1, 2) for k in ("b", "g", "be", "m", "v")], axis=1)
    out["l2_ew"] = np.concatenate([v["L2_ffn_W1"], v["L2_ffn_W2"], v["L2_ffn_Wo"]], axis=2).transpose(1, 0, 2)
    out["l3_W"] = v["L3_gnn_W"]
    out["l3_b"] = v["L3_gnn_b"].reshape(-1, 1)
    out["pk_w"] = v["L3_ffn_Wq_pk"].reshape(128, 2, 8, 64).transpose(3, 2, 1, 0).reshape(64, 16, 128)
    out["pk_k"] = v["L3_ffn_pk_keys"].transpose(3, 2, 0, 1).reshape(64, 16, 128)
    out["pk_wq"] = v["L3_ffn_Wq"].reshape(128, 8, 128).transpose(1, 0, 2)
    out["pk_wo"] = v["L3_ffn_Wo"].reshape(8, 128, 128).transpose(1, 0, 2)
    out["tables"] = np.concatenate([v["L3_ffn_keys_table"], v["L3_ffn_values_table"]], axis=1)
    out["l1_W"] = v["L1_gnn_W"]
    return {k: np.ascontiguousarray(a) for k, a in out.items()}


def kernel(**inputs):
    import numpy as np
    import concourse.bacc as bacc
    from concourse import mybir as my
    from concourse.bass_utils import run_bass_kernel_spmd

    nc = bacc.Bacc("TRN2", target_bir_lowering=False, num_devices=1)
    arrays = layouts(np, {k: np.asarray(a) for k, a in inputs.items()})
    io = {k: nc.dram_tensor("in_" + k, a.shape, my.dt.from_np(a.dtype), kind="ExternalInput").ap() for k, a in arrays.items()}
    io["outT"] = nc.dram_tensor("outT", (128, 2048), my.dt.float32, kind="ExternalOutput").ap()
    build(nc, io)
    r = run_bass_kernel_spmd(nc, [{"in_" + k: a for k, a in arrays.items()}], core_ids=[0])
    return np.ascontiguousarray(r.results[0]["outT"].T)
```
